# Optimizing a Trainium2 kernel written in Bass

```python
import numpy as np
import jax
import jax.numpy as jnp

def _softmax(x, axis=-1):
    return jax.nn.softmax(x, axis=axis)

def _gelu(x):
    return jax.nn.gelu(x, approximate=True)

def _silu(x):
    return jax.nn.silu(x)

def _sigmoid(x):
    return jax.nn.sigmoid(x)

def _layernorm(x, axis=-1, eps=1e-05):
    m = jnp.mean(x, axis=axis, keepdims=True)
    v = jnp.var(x, axis=axis, keepdims=True)
    return (x - m) / jnp.sqrt(v + eps)

def _scatter_add(tgt, idx, src, axis=0):
    return tgt.at[idx].add(src)

def _segment_sum(src, seg, n):
    return jax.ops.segment_sum(src, seg, n)
kernel_name = 'mk_decoder_preln_d1_seqx_r4_2f26c4'

def setup_inputs(seed: int=0):
    np.random.seed(seed)
    _w = jnp.asarray

    def _rec_inputs():
        import jax
        import jax.numpy as jnp
        _rk = jax.random.key(seed)
        x = -0.0002928 + 1 * jax.random.normal(jax.random.fold_in(_rk, 1), (1, 2048, 256), jnp.float32)
        _lenS = 2048 - jax.random.randint(jax.random.fold_in(_rk, 7), (1,), 0, max(1, 2048 // 4) + 1, jnp.int32)
        _lenS2 = 1601 - jax.random.randint(jax.random.fold_in(_rk, 8), (1,), 0, max(1, 1601 // 4) + 1, jnp.int32)
        _ctx_1024P = jax.random.normal(jax.random.fold_in(_rk, 11), (1, 16, 256), jnp.float32)
        _ctx_1024c = jax.random.dirichlet(jax.random.fold_in(_rk, 511), 0.3 * jnp.ones((16,), jnp.float32), (1, 1601))
        _ctx_1024t = jnp.einsum('bsk,bkd->bsd', _ctx_1024c, _ctx_1024P)
        _ctx_1024t = _ctx_1024t * jax.lax.rsqrt(jnp.mean(jnp.square(_ctx_1024t)) + 1e-12) * 0.953939
        ctx_1024 = -1.39393e-06 + 0.999914 * (_ctx_1024t + 0.3 * jax.random.normal(jax.random.fold_in(_rk, 611), (1, 1601, 256), jnp.float32))
        return (x, ctx_1024)
    x, ctx_1024 = _rec_inputs()

    def _L0_attn_setup():
        import jax, jax.numpy as jnp
        import numpy as np
        N_EMBD = 256
        BLOCK_SIZE = 512
        ATTN_SPAN = 64
        LN_EPS = 1e-05

        def _band_mask(T, span, dtype):
            ones = jnp.ones((T, T), dtype=dtype)
            return jnp.tril(ones, 0) * (1.0 - jnp.tril(ones, -span))

        def _layer_norm(h, w, b):
            mu = jnp.mean(h, axis=-1, keepdims=True)
            var = jnp.var(h, axis=-1, keepdims=True)
            return (h - mu) * jax.lax.rsqrt(var + LN_EPS) * w + b
        key = jax.random.key(seed)
        k_x, k_w, k_b, k_lw = jax.random.split(key, 4)
        B, T, C = (4, BLOCK_SIZE, N_EMBD)
        x = jax.random.normal(k_x, (B, T, C), dtype=jnp.float32)
        lim = 1.0 / np.sqrt(C)
        W_qkv = jax.random.uniform(k_w, (C, 3 * C), minval=-lim, maxval=lim, dtype=jnp.float32)
        b_qkv = jax.random.uniform(k_b, (3 * C,), minval=-lim, maxval=lim, dtype=jnp.float32)
        ln_w = jnp.ones((C,), dtype=jnp.float32)
        ln_b = jnp.zeros((C,), dtype=jnp.float32)
        return {'x': x, 'W_qkv': W_qkv, 'b_qkv': b_qkv, 'ln_w': ln_w, 'ln_b': ln_b}
    _L0_attn_all = _L0_attn_setup()
    _L0_attn_in = {k: v for k, v in _L0_attn_all.items() if k in ('W_qkv', 'b_qkv', 'ln_w', 'ln_b')}
    del _L0_attn_all

    def _L0_xattn_setup():
        import jax, jax.numpy as jnp
        import numpy as np
        DIM = 256
        NUM_HEADS = 16
        HEAD_DIM = DIM // NUM_HEADS
        key = jax.random.key(seed)
        ks = jax.random.split(key, 11)
        B, N, C = (2, 512, DIM)
        s = 1.0 / np.sqrt(C)
        inp = {'q': jax.random.normal(ks[0], (B, N, C), jnp.float32), 'k': jax.random.normal(ks[1], (B, N, C), jnp.float32), 'v': jax.random.normal(ks[2], (B, N, C), jnp.float32), 'Wq': jax.random.normal(ks[3], (C, C), jnp.float32) * s, 'bq': jnp.zeros((C,), jnp.float32), 'Wk': jax.random.normal(ks[4], (C, C), jnp.float32) * s, 'bk': jnp.zeros((C,), jnp.float32), 'Wv': jax.random.normal(ks[5], (C, C), jnp.float32) * s, 'bv': jnp.zeros((C,), jnp.float32), 'Wo': jax.random.normal(ks[6], (C, C), jnp.float32) * s, 'bo': jnp.zeros((C,), jnp.float32)}
        return inp
    _L0_xattn_all = _L0_xattn_setup()
    _L0_xattn_in = {k: v for k, v in _L0_xattn_all.items() if k in ('Wq', 'bq', 'Wk', 'bk', 'Wv', 'bv', 'Wo', 'bo')}
    del _L0_xattn_all

    def _L0_ffn_setup():
        import jax, jax.numpy as jnp
        import numpy as np
        D_MODEL = 256
        N_HEAD = 16
        HEAD_DIM = D_MODEL // N_HEAD
        D_FF = 1024
        N_EXPERTS = 4
        EPS = 1e-05

        def _layer_norm(x, gamma, beta):
            mu = jnp.mean(x, axis=-1, keepdims=True)
            var = jnp.mean((x - mu) ** 2, axis=-1, keepdims=True)
            return (x - mu) / jnp.sqrt(var + EPS) * gamma + beta
        key = jax.random.key(seed)
        ks = jax.random.split(key, 20)
        f32 = jnp.float32
        sc = 1.0 / np.sqrt(D_MODEL)
        scf = 1.0 / np.sqrt(D_FF)
        return {'src': jax.random.normal(ks[0], (4, 128, D_MODEL), f32), 'Wq': jax.random.normal(ks[1], (D_MODEL, D_MODEL), f32) * sc, 'bq': jnp.zeros((D_MODEL,), f32), 'Wk': jax.random.normal(ks[2], (D_MODEL, D_MODEL), f32) * sc, 'bk': jnp.zeros((D_MODEL,), f32), 'Wv': jax.random.normal(ks[3], (D_MODEL, D_MODEL), f32) * sc, 'bv': jnp.zeros((D_MODEL,), f32), 'Wo': jax.random.normal(ks[4], (D_MODEL, D_MODEL), f32) * sc, 'bo': jnp.zeros((D_MODEL,), f32), 'router_w': jax.random.normal(ks[5], (D_MODEL, 1), f32) * 0.05, 'router_b': jnp.zeros((1,), f32), 'W1': jax.random.normal(ks[6], (N_EXPERTS, D_MODEL, D_FF), f32) * sc, 'b1': jnp.zeros((N_EXPERTS, D_FF), f32), 'W2': jax.random.normal(ks[7], (N_EXPERTS, D_FF, D_MODEL), f32) * scf, 'b2': jnp.zeros((N_EXPERTS, D_MODEL), f32), 'ln1_g': jnp.ones((D_MODEL,), f32), 'ln1_b': jnp.zeros((D_MODEL,), f32), 'ln2_g': jnp.ones((D_MODEL,), f32), 'ln2_b': jnp.zeros((D_MODEL,), f32)}
    _L0_ffn_all = _L0_ffn_setup()
    _L0_ffn_in = {k: v for k, v in _L0_ffn_all.items() if k in ('Wq', 'bq', 'Wk', 'bk', 'Wv', 'bv', 'Wo', 'bo', 'router_w', 'router_b', 'W1', 'b1', 'W2', 'b2', 'ln1_g', 'ln1_b', 'ln2_g', 'ln2_b')}
    del _L0_ffn_all
    return {'x': x, 'ctx_1024': ctx_1024, 'L0_attn_W_qkv': _L0_attn_in['W_qkv'], 'L0_attn_b_qkv': _L0_attn_in['b_qkv'], 'L0_attn_ln_w': _L0_attn_in['ln_w'], 'L0_attn_ln_b': _L0_attn_in['ln_b'], 'L0_xattn_Wq': _L0_xattn_in['Wq'], 'L0_xattn_bq': _L0_xattn_in['bq'], 'L0_xattn_Wk': _L0_xattn_in['Wk'], 'L0_xattn_bk': _L0_xattn_in['bk'], 'L0_xattn_Wv': _L0_xattn_in['Wv'], 'L0_xattn_bv': _L0_xattn_in['bv'], 'L0_xattn_Wo': _L0_xattn_in['Wo'], 'L0_xattn_bo': _L0_xattn_in['bo'], 'L0_ffn_Wq': _L0_ffn_in['Wq'], 'L0_ffn_bq': _L0_ffn_in['bq'], 'L0_ffn_Wk': _L0_ffn_in['Wk'], 'L0_ffn_bk': _L0_ffn_in['bk'], 'L0_ffn_Wv': _L0_ffn_in['Wv'], 'L0_ffn_bv': _L0_ffn_in['bv'], 'L0_ffn_Wo': _L0_ffn_in['Wo'], 'L0_ffn_bo': _L0_ffn_in['bo'], 'L0_ffn_router_w': _L0_ffn_in['router_w'], 'L0_ffn_router_b': _L0_ffn_in['router_b'], 'L0_ffn_W1': _L0_ffn_in['W1'], 'L0_ffn_b1': _L0_ffn_in['b1'], 'L0_ffn_W2': _L0_ffn_in['W2'], 'L0_ffn_b2': _L0_ffn_in['b2'], 'L0_ffn_ln1_g': _L0_ffn_in['ln1_g'], 'L0_ffn_ln1_b': _L0_ffn_in['ln1_b'], 'L0_ffn_ln2_g': _L0_ffn_in['ln2_g'], 'L0_ffn_ln2_b': _L0_ffn_in['ln2_b']}

def reference(x, ctx_1024, L0_attn_W_qkv, L0_attn_b_qkv, L0_attn_ln_w, L0_attn_ln_b, L0_xattn_Wq, L0_xattn_bq, L0_xattn_Wk, L0_xattn_bk, L0_xattn_Wv, L0_xattn_bv, L0_xattn_Wo, L0_xattn_bo, L0_ffn_Wq, L0_ffn_bq, L0_ffn_Wk, L0_ffn_bk, L0_ffn_Wv, L0_ffn_bv, L0_ffn_Wo, L0_ffn_bo, L0_ffn_router_w, L0_ffn_router_b, L0_ffn_W1, L0_ffn_b1, L0_ffn_W2, L0_ffn_b2, L0_ffn_ln1_g, L0_ffn_ln1_b, L0_ffn_ln2_g, L0_ffn_ln2_b):
    import jax
    import jax.numpy as jnp

    def _L0_attn_ref(x, W_qkv, b_qkv, ln_w, ln_b):
        import jax, jax.numpy as jnp
        import numpy as np
        N_EMBD = 256
        BLOCK_SIZE = 512
        ATTN_SPAN = 64
        LN_EPS = 1e-05

        def _band_mask(T, span, dtype):
            ones = jnp.ones((T, T), dtype=dtype)
            return jnp.tril(ones, 0) * (1.0 - jnp.tril(ones, -span))

        def _layer_norm(h, w, b):
            mu = jnp.mean(h, axis=-1, keepdims=True)
            var = jnp.var(h, axis=-1, keepdims=True)
            return (h - mu) * jax.lax.rsqrt(var + LN_EPS) * w + b
        B, T, C = x.shape
        qkv = x @ W_qkv + b_qkv
        q, k, v = jnp.split(qkv, 3, axis=-1)
        scale = np.sqrt(C * ATTN_SPAN).astype(np.float32)
        scores = jnp.einsum('bid,bjd->bij', q, k) / scale
        scores = scores * _band_mask(T, ATTN_SPAN, x.dtype)[None, :, :]
        out = jnp.einsum('bij,bjd->bid', scores, v)
        return _layer_norm(out, ln_w, ln_b)

    def _L0_xattn_ref(q, k, v, Wq, bq, Wk, bk, Wv, bv, Wo, bo):
        import jax, jax.numpy as jnp
        import numpy as np
        DIM = 256
        NUM_HEADS = 16
        HEAD_DIM = DIM // NUM_HEADS
        B, Nq, C = q.shape
        Nkv = k.shape[1]
        H, D = (NUM_HEADS, HEAD_DIM)
        qh = (q @ Wq.T + bq).reshape(B, Nq, H, D).transpose(0, 2, 1, 3)
        kh = (k @ Wk.T + bk).reshape(B, Nkv, H, D).transpose(0, 2, 1, 3)
        vh = (v @ Wv.T + bv).reshape(B, Nkv, H, D).transpose(0, 2, 1, 3)
        scale = D ** (-0.5)
        attn = jax.nn.softmax(jnp.einsum('bhqd,bhkd->bhqk', qh, kh) * scale, axis=-1)
        out = jnp.einsum('bhqk,bhkd->bhqd', attn, vh)
        out = out.transpose(0, 2, 1, 3).reshape(B, Nq, C)
        return out @ Wo.T + bo

    def _L0_ffn_ref(src, Wq, bq, Wk, bk, Wv, bv, Wo, bo, router_w, router_b, W1, b1, W2, b2, ln1_g, ln1_b, ln2_g, ln2_b):
        import jax, jax.numpy as jnp
        import numpy as np
        D_MODEL = 256
        N_HEAD = 16
        HEAD_DIM = D_MODEL // N_HEAD
        D_FF = 1024
        N_EXPERTS = 4
        EPS = 1e-05

        def _layer_norm(x, gamma, beta):
            mu = jnp.mean(x, axis=-1, keepdims=True)
            var = jnp.mean((x - mu) ** 2, axis=-1, keepdims=True)
            return (x - mu) / jnp.sqrt(var + EPS) * gamma + beta
        B, T, _ = src.shape
        q = (src @ Wq + bq).reshape(B, T, N_HEAD, HEAD_DIM)
        k = (src @ Wk + bk).reshape(B, T, N_HEAD, HEAD_DIM)
        v = (src @ Wv + bv).reshape(B, T, N_HEAD, HEAD_DIM)
        scale = HEAD_DIM ** (-0.5)
        scores = jnp.einsum('bqhd,bkhd->bhqk', q, k) * scale
        probs = jax.nn.softmax(scores, axis=-1)
        attn = jnp.einsum('bhqk,bkhd->bqhd', probs, v).reshape(B, T, D_MODEL)
        attn = attn @ Wo + bo
        x = _layer_norm(src + attn, ln1_g, ln1_b)
        keys = (x @ router_w + router_b)[..., 0]
        expert_idx = jnp.remainder(jnp.floor(keys).astype(jnp.int32), N_EXPERTS)
        ff_out = jnp.zeros_like(x)
        for e in range(N_EXPERTS):
            h = jax.nn.relu(x @ W1[e] + b1[e])
            y = h @ W2[e] + b2[e]
            ff_out = ff_out + jnp.where((expert_idx == e)[..., None], y, 0.0)
        return _layer_norm(x + ff_out, ln2_g, ln2_b)
    x = x + _L0_attn_ref(_layernorm(x, axis=-1), L0_attn_W_qkv, L0_attn_b_qkv, L0_attn_ln_w, L0_attn_ln_b)
    x = x + _L0_xattn_ref(_layernorm(x, axis=-1), ctx_1024, ctx_1024, L0_xattn_Wq, L0_xattn_bq, L0_xattn_Wk, L0_xattn_bk, L0_xattn_Wv, L0_xattn_bv, L0_xattn_Wo, L0_xattn_bo)
    x = x + _L0_ffn_ref(_layernorm(x, axis=-1), L0_ffn_Wq, L0_ffn_bq, L0_ffn_Wk, L0_ffn_bk, L0_ffn_Wv, L0_ffn_bv, L0_ffn_Wo, L0_ffn_bo, L0_ffn_router_w, L0_ffn_router_b, L0_ffn_W1, L0_ffn_b1, L0_ffn_W2, L0_ffn_b2, L0_ffn_ln1_g, L0_ffn_ln1_b, L0_ffn_ln2_g, L0_ffn_ln2_b)
    return x

_drawn_inputs = setup_inputs


def setup_inputs(seed=0):
    import zlib

    import numpy as np

    out = dict(_drawn_inputs(seed))
    spreads = {'L0_attn_ln_w': (1.0, 0.2),
     'L0_attn_ln_b': (0.0, 0.1),
     'L0_xattn_bq': (0.0, 0.1),
     'L0_xattn_bk': (0.0, 0.8),
     'L0_xattn_bv': (0.0, 0.1),
     'L0_xattn_bo': (0.0, 0.1),
     'L0_ffn_bq': (0.0, 0.422),
     'L0_ffn_bk': (0.0, 0.8),
     'L0_ffn_bv': (0.0, 0.1),
     'L0_ffn_bo': (0.0, 0.1),
     'L0_ffn_b1': (0.0, 0.356),
     'L0_ffn_b2': (0.0, 0.1),
     'L0_ffn_ln1_g': (1.0, 0.2),
     'L0_ffn_ln1_b': (0.0, 0.1),
     'L0_ffn_ln2_g': (1.0, 0.2),
     'L0_ffn_ln2_b': (0.0, 0.1)}
    factors = {}
    for name, (base, spread) in spreads.items():
        noise = np.random.default_rng([zlib.crc32(name.encode()), seed]).standard_normal(out[name].shape)
        drawn = base * np.exp(spread * noise) if base else spread * noise
        out[name] = jnp.asarray(drawn.astype(out[name].dtype))
    for name, factor in factors.items():
        out[name] = (out[name] * factor).astype(out[name].dtype)
    return out
```

```python
import concourse.bass as bass
from concourse import mybir
from contextlib import ExitStack


def decoder_layer_kernel(nc, io, out):
    fp32, fp16, i32 = mybir.dt.float32, mybir.dt.float16, mybir.dt.int32
    ALU = mybir.AluOpType
    ACT = mybir.ActivationFunctionType
    AX = mybir.AxisListType

    P = 128
    T, C = io["x"].shape[1:]
    S_CTX = io["ctx_1024"].shape[1]
    NT = T // P
    KC = C // P
    GRP = 4
    NG = NT // GRP
    QG = GRP * P
    EPS = 1e-5
    SPAN = 64
    BAND_SCALE = 1.0 / float((C * SPAN) ** 0.5)
    H, D = 16, C // 16
    SLOT = 64
    MROW = 3 * D
    NCT = -(-S_CTX // P)
    CTX_LAST = S_CTX - (NCT - 1) * P

    ctx = ExitStack()
    with ctx:
        def sb(name, shape, dt=fp32):
            return ctx.enter_context(nc.sbuf_tensor(name, shape, dt))

        def sems(*names):
            return {n: ctx.enter_context(nc.semaphore(n)) for n in names}

        x_sb = sb("x_sb", [P, NT, C])
        src_sb = sb("src_sb", [P, NT, C])
        k_op = sb("k_op", [P, H // 2, T], fp16)
        v_aug = sb("v_aug", [P, NT, H, 2 * D])
        q_arena = sb("q_arena", [P, NT * H * SLOT // 2])
        attn_tok = sb("attn_tok", [P, NT, C])
        p_arena = sb("p_arena", [P, 4 * 1024])
        w_xq = sb("w_xq", [P, KC, C])
        w_xkv = sb("w_xkv", [P, KC, 2 * C])
        w_xo = sb("w_xo", [P, KC, C])
        w_fqkv = sb("w_fqkv", [P, KC, 3 * C])
        w_fo = sb("w_fo", [P, KC, C])
        ROWS = ["xattn_bq", "xattn_bk", "xattn_bv", "xattn_bo", "ffn_bq", "ffn_bk", "ffn_bv", "ffn_bo",
                "ffn_ln1_g", "ffn_ln1_b", "ffn_ln2_g", "ffn_ln2_b"]
        rows = sb("rows", [P, len(ROWS), C])

        def row(name, n=1):
            i = ROWS.index(name)
            return rows[:, i:i + n, :].rearrange("p n c -> p (n c)")

        ident = sb("ident", [P, P])
        ident16 = sb("ident16", [P, P], fp16)
        band_mask = sb("band_mask", [P, 2 * P])
        stat6 = sb("stat6", [P, 4, 6])
        mean_var = sb("mean_var", [P, 4, 2])
        rstd = sb("rstd", [P, 4])
        eps_col = sb("eps_col", [P, 1])
        E, F = io["L0_ffn_W1"].shape[0], io["L0_ffn_W1"].shape[2]
        FC = F // P
        b1_col = sb("b1_col", [P, E, FC])
        b2_sb = sb("b2_sb", [E, C])
        router_col = sb("router_col", [P, KC + 1])
        expert_no = sb("expert_no", [E, 1], i32)
        expert_col = sb("expert_col", [E, 1])

        def carve(arena, at, *shape):
            n = 1
            for k in shape:
                n *= k
            v = arena[:, at:at + n]
            if len(shape) == 2:
                v = v.rearrange("p (a b) -> p a b", b=shape[1])
            if len(shape) == 3:
                v = v.rearrange("p (a b c) -> p a b c", b=shape[1], c=shape[2])
            return v

        q_tok = q_arena[:, :].bitcast(fp16).rearrange("p (t h s) -> p t h s", h=H, s=SLOT)
        w_band = carve(q_arena, 0, KC, 3 * C)
        band_qk = carve(q_arena, 1536, 4, 4, P)
        band_v = carve(q_arena, 3584, 4, C)
        band_st = carve(q_arena, 4608, 2, 2 * P)
        w_xraw = carve(q_arena, 5120, 4, KC, C)
        band_rows = carve(q_arena, 7168, 3, C)
        band_tmp = sb("band_tmp", [P, 2, C])
        bqk_col = sb("bqk_col", [P, 4])
        xin = carve(p_arena, 0, 2, C)
        xT = carve(p_arena, 512, 2, KC, P)

        s_pair = [ctx.enter_context(nc.psum_tensor(f"s_pair{i}", [P, 1024], fp32)) for i in range(2)]
        singles = [ctx.enter_context(nc.psum_tensor(f"bank{i}", [P, 512], fp32)) for i in range(4, 8)]

        def bank(i):
            return s_pair[i // 2][:, (i % 2) * 512:(i % 2 + 1) * 512] if i < 4 else singles[i - 4][:, :]

        s = sems("ld_x0", "ld_x", "ld_band", "ld_xw", "ld_rows", "ld_fw", "const_zero", "const", "stored",
                 "band_zero", "band_ln", "band_xT_ps", "band_xT", "band_qkv_ps", "band_qkv", "band_s", "band_st",
                 "band_av", "band_out", "band_root", "band_ln_root", "band_xb", "xw_ps", "xw", "v_const", "k_const", "q_const",
                 "ld_small", "iota")

        x_view = io["x"][0].rearrange("(t p) c -> p t c", p=P)
        out_view = out[0].rearrange("(t p) c -> p t c", p=P)

        def ticks(eng, n, depth, tick, head=GRP, unroll=GRP):
            loops = (n - head) // unroll
            for t in range(head):
                tick(t, t % unroll)
            with eng.Fori(head // unroll, head // unroll + loops) as g:
                for r in range(unroll):
                    tick(g * unroll + r, r)
            for t in range(head + loops * unroll, n + depth):
                tick(t, t % unroll)

        def tile_at(t, stage, n):
            if isinstance(t, int) and not 0 <= t - stage < n:
                return None
            return t - stage

        def some(t, least=1):
            return not isinstance(t, int) or t >= least

        block = ctx.enter_context(nc.Block())

        def norm_aggr(dve, ring, steps):
            dve.bn_aggr(mean_var[:, ring, :], stat6[:, ring, :]).then_inc(steps, 1)

        def norm_root(act, ring, steps, count, roots):
            act.wait_ge(steps, count + 2)
            act.activation(rstd[:, ring:ring + 1], mean_var[:, ring, 1:2], ACT.Sqrt, bias=eps_col[:, :]).then_inc(roots, 1)

        def norm_apply(dve, i, ring, source, dest, steps, count, roots):
            dve.wait_ge(roots, i + 1)
            dve.reciprocal(rstd[:, ring:ring + 1], rstd[:, ring:ring + 1]).then_inc(steps, 1)
            dve.wait_ge(steps, count + 3)
            dve.tensor_scalar(dest, source, mean_var[:, ring, 0:1], rstd[:, ring:ring + 1],
                              ALU.subtract, ALU.mult).then_inc(steps, 1)

        def band_tensor(pe):
            pe.wait_ge(s["const"], 4)
            pe.wait_ge(s["ld_band"], 16 * 5)
            pe.wait_ge(s["band_zero"], 2)

            def tick(t, r):
                if (i := tile_at(t, 3, NT)) is not None:
                    pe.wait_ge(s["band_st"], i + 1)
                    if some(i):
                        pe.wait_ge(s["band_out"], 5 * i)
                    q, prev = (r - 3) % 4, (r - 4) % 4
                    pe.matmul(bank(7)[:, 0:C], band_st[:, q % 2, 0:P], band_v[:, q, :], start=True, stop=False)
                    pe.matmul(bank(7)[:, 0:C], band_st[:, q % 2, P:2 * P], band_v[:, prev, :],
                              start=False, stop=True).then_inc(s["band_av"], 1)
                if (i := tile_at(t, 2, NT)) is not None:
                    pe.wait_ge(s["band_qkv"], 2 * i + 2)
                    if some(i):
                        pe.wait_ge(s["band_st"], i)
                    q, prev = (r - 2) % 4, (r - 3) % 4
                    for part, keys in ((0, q), (1, prev)):
                        for k in range(KC):
                            last = pe.matmul(bank(6)[:, part * P:(part + 1) * P], band_qk[:, keys, KC + k, :],
                                             band_qk[:, q, k, :], start=k == 0, stop=k == KC - 1)
                    last.then_inc(s["band_s"], 1)
                if (i := tile_at(t, 1, NT)) is not None:
                    pe.wait_ge(s["band_xT"], i + 1)
                    if some(i - 1):
                        pe.wait_ge(s["band_qkv"], 2 * (i - 1))
                    q = (r - 1) % 2
                    for f in range(4):
                        for k in range(KC):
                            pe.matmul(bank(2 + q)[:, f * P:(f + 1) * P], w_band[:, k, f * P:(f + 1) * P], xT[:, q, k, :],
                                      start=k == 0, stop=k == KC - 1)
                    for k in range(KC):
                        last = pe.matmul(bank(4 + q)[:, 0:C], xT[:, q, k, :], w_band[:, k, 2 * C:3 * C],
                                         start=k == 0, stop=k == KC - 1)
                    last.then_inc(s["band_qkv_ps"], 1)
                if (i := tile_at(t, 0, NT)) is not None:
                    pe.wait_ge(s["band_ln"], 4 * i + 4)
                    if some(i - 1):
                        pe.wait_ge(s["band_xT"], i - 1)
                    q = r % 2
                    for k in range(KC):
                        last = pe.transpose(bank(q)[:, k * P:(k + 1) * P], xin[:, q, k * P:(k + 1) * P], ident[:, :])
                    last.then_inc(s["band_xT_ps"], 1)

            ticks(pe, NT, 3, tick)

        def band_scalar(act):
            act.wait_ge(s["const"], 1)

            def tick(t, r):
                if (i := tile_at(t, 3, NT)) is not None:
                    norm_root(act, 2 + (r - 3) % 2, s["band_out"], 5 * i, s["band_root"])
                if (i := tile_at(t, 0, NT)) is not None:
                    norm_root(act, r % 2, s["band_ln"], 4 * i, s["band_ln_root"])
                    act.wait_ge(s["band_xT_ps"], i + 1)
                    if some(i - 1):
                        act.wait_ge(s["band_qkv_ps"], i - 1)
                    act.activation(xT[:, r % 2, :, :], bank(r % 2)[:, 0:C].rearrange("p (k t) -> p k t", k=KC),
                                   ACT.Copy).then_inc(s["band_xT"], 1)

            ticks(act, NT, 3, tick)

        def band_vector(dve):
            dve.memset(band_qk[:, 3, :, :], 0.0).then_inc(s["band_zero"], 1)
            dve.memset(band_v[:, 3, :], 0.0).then_inc(s["band_zero"], 1)
            dve.wait_ge(s["ld_x0"], 16)

            def tick(t, r):
                if isinstance(t, int) and t == GRP - 1:
                    dve.wait_ge(s["ld_x"], 16)
                o = bank(7)[:, 0:C]
                q3 = (r - 3) % 2
                if (i := tile_at(t, 3, NT)) is not None:
                    dve.wait_ge(s["band_av"], i + 1)
                    dve.bn_stats(stat6[:, 2 + q3, :], o).then_inc(s["band_out"], 1)
                if (i := tile_at(t, 0, NT)) is not None:
                    dve.bn_stats(stat6[:, r % 2, :], x_sb[:, i, :]).then_inc(s["band_ln"], 1)
                    dve.wait_ge(s["band_ln"], 4 * i + 1)
                if (i := tile_at(t, 3, NT)) is not None:
                    dve.wait_ge(s["band_out"], 5 * i + 1)
                if (i := tile_at(t, 2, NT)) is not None:
                    dve.wait_ge(s["band_s"], i + 1)
                    if some(i - 1):
                        dve.wait_ge(s["band_av"], i - 1)
                    dve.tensor_tensor(band_st[:, (r - 2) % 2, :], bank(6)[:, 0:2 * P], band_mask[:, :],
                                      ALU.mult).then_inc(s["band_st"], 1)
                if tile_at(t, 3, NT) is not None:
                    norm_aggr(dve, 2 + q3, s["band_out"])
                if tile_at(t, 0, NT) is not None:
                    norm_aggr(dve, r % 2, s["band_ln"])
                if (i := tile_at(t, 3, NT)) is not None:
                    dve.wait_ge(s["band_out"], 5 * i + 2)
                    ring, c = 2 + q3, 5 * i
                    dve.scalar_tensor_tensor(band_tmp[:, q3, :], o, mean_var[:, ring, 0:1], band_rows[:, 1, :],
                                             ALU.subtract, ALU.mult).then_inc(s["band_out"], 1)
                    dve.wait_ge(s["band_root"], i + 1)
                    dve.reciprocal(rstd[:, ring:ring + 1], rstd[:, ring:ring + 1]).then_inc(s["band_out"], 1)
                    dve.wait_ge(s["band_out"], c + 4)
                    dve.wait_ge(s["band_xb"], i + 1)
                    dve.scalar_tensor_tensor(x_sb[:, i, :], band_tmp[:, q3, :], rstd[:, ring:ring + 1], x_sb[:, i, :],
                                             ALU.mult, ALU.add).then_inc(s["band_out"], 1)
                if (i := tile_at(t, 0, NT)) is not None:
                    if some(i - 1):
                        dve.wait_ge(s["band_xT_ps"], i - 1)
                    norm_apply(dve, i, r % 2, x_sb[:, i, :], xin[:, r % 2, :], s["band_ln"], 4 * i, s["band_ln_root"])
                if (i := tile_at(t, 1, NT)) is not None:
                    q = (r - 1) % 4
                    dve.wait_ge(s["band_qkv_ps"], i + 1)
                    dve.tensor_tensor(band_qk[:, q, :, :], bank(2 + q % 2).rearrange("p (f t) -> p f t", f=4),
                                      bqk_col[:, :].unsqueeze(2).broadcast_to([P, 4, P]), ALU.add).then_inc(s["band_qkv"], 1)
                    dve.tensor_tensor(band_v[:, q, :], bank(4 + q % 2)[:, 0:C], band_rows[:, 0, :],
                                      ALU.add).then_inc(s["band_qkv"], 1)

            ticks(dve, NT, 3, tick)

        def band_gpsimd(pool):
            pool.wait_ge(s["ld_band"], 16 * 5)

            def tick(t, r):
                if (i := tile_at(t, 1, NT)) is not None:
                    pool.wait_ge(s["band_ln"], 4 * i + 4)
                    pool.tensor_tensor(x_sb[:, i, :], x_sb[:, i, :], band_rows[:, 2, :], ALU.add).then_inc(s["band_xb"], 1)

            ticks(pool, NT, 1, tick)

        def weights_tensor(pe):
            pe.wait_ge(s["ld_xw"], 16 * 4)
            pe.wait_ge(s["band_xT"], NT)
            pe.wait_ge(s["band_qkv"], 2 * NT)
            for w in range(4):
                for k in range(KC):
                    for o in range(KC):
                        last = pe.transpose(bank(w)[:, k * C + o * P:k * C + (o + 1) * P],
                                            w_xraw[:, w, o, k * P:(k + 1) * P], ident[:, :])
                last.then_inc(s["xw_ps"], 1)

        def weights_scalar(act):
            for w, dest in enumerate((w_xq[:, :, :], w_xkv[:, :, 0:C], w_xkv[:, :, C:2 * C], w_xo[:, :, :])):
                act.wait_ge(s["xw_ps"], w + 1)
                act.activation(dest, bank(w).rearrange("p (k n) -> p k n", k=KC), ACT.Copy).then_inc(s["xw"], 1)

        HEAD = 6

        class Stage:
            def __init__(self, name, tiles, weights, width, bias, has_q, has_kv, front=None, loaded=None):
                self.name, self.tiles, self.weights, self.width = name, tiles, weights, width
                self.bias, self.has_q, self.has_kv, self.front, self.loaded = bias, has_q, has_kv, front, loaded
                self.f = 1 if front else 0
                self.s = {n: ctx.enter_context(nc.semaphore(f"{name}_{n}")) for n in (
                    "in0", "in1", "ln", "root", "xT_ps", "xT", "proj", "sum", "hi", "split", "copy", "kT", "kop",
                    "at", "aT_ps", "aT", "o_ps", "kept", "res", "res_bias")}

            def rows(self, t):
                return CTX_LAST if self.loaded and isinstance(t, int) and t == NCT - 1 else P

        qk32 = carve(p_arena, 1024, 2, 2 * C)
        k_tok = carve(p_arena, 2048, 2, H * SLOT // 2)
        k_tok = k_tok.rearrange("p a b -> p (a b)").bitcast(fp16).rearrange("p (a h s) -> p a h s", h=H, s=SLOT)
        at_in = carve(p_arena, 3072, 2, C)
        aT = carve(p_arena, 3584, 2, KC, P)

        def stage_tensor(pe, st):
            z, f, n = st.s, st.f, st.tiles

            def tick(t, r):
                if st.has_kv and (i := tile_at(t, f + 3, n)) is not None:
                    q, m = (r - f - 3) % 2, st.rows(i)
                    pe.wait_ge(z["split"], i + 1)
                    pe.wait_ge(z["copy"], i + 1)
                    if some(i - 1):
                        pe.wait_ge(z["kop"], i - 1)
                    for pair in range(H // 2):
                        last = pe.transpose(bank(6 + q).bitcast(fp16)[:, pair * P:pair * P + m],
                                            k_tok[0:m, q, 2 * pair:2 * pair + 2, :].rearrange("p h s -> p (h s)"),
                                            ident16[0:m, 0:m])
                    last.then_inc(z["kT"], 1)
                if (i := tile_at(t, f + 2, n)) is not None:
                    q, m = (r - f - 2) % 2, st.rows(i)
                    pe.wait_ge(z["xT"], i + 1)
                    if some(i - 1):
                        pe.wait_ge(z["sum"], i - 1)
                    if some(i):
                        pe.wait_ge(z["split"], i)
                    for at in range(0, st.width, 512):
                        w = min(512, st.width - at)
                        dest = bank(3 + q) if at == 0 else bank(5)
                        for k in range(KC):
                            last = pe.matmul(dest[0:m, 0:w], xT[:, q, k, 0:m], st.weights[:, k, at:at + w],
                                             start=k == 0, stop=k == KC - 1)
                    last.then_inc(z["proj"], 1)
                if (i := tile_at(t, f + 1, n)) is not None:
                    q, m = (r - f - 1) % 2, st.rows(i)
                    if st.loaded:
                        pe.wait_ge(z[f"in{q}"], 16 * half(i, r - f - 1) + 16)
                    else:
                        pe.wait_ge(z["ln"], 4 * i + 4)
                    if some(i):
                        pe.wait_ge(z["xT"], i)
                    for k in range(KC):
                        last = pe.transpose(bank(2)[:, k * P:k * P + m], xin[0:m, q, k * P:(k + 1) * P], ident[0:m, 0:m])
                    last.then_inc(z["xT_ps"], 1)
                if st.front and (i := tile_at(t, 1, n)) is not None:
                    pe.wait_ge(z["aT"], i + 1)
                    if some(i):
                        pe.wait_ge(z["res"], i)
                    for k in range(KC):
                        last = pe.matmul(bank(1)[:, 0:C], aT[:, (r - 1) % 2, k, :], st.front[:, k, :],
                                         start=k == 0, stop=k == KC - 1)
                    last.then_inc(z["o_ps"], 1)
                if st.front and (i := tile_at(t, 0, n)) is not None:
                    pe.wait_ge(z["at"], i + 1)
                    if some(i):
                        pe.wait_ge(z["aT"], i)
                    for k in range(KC):
                        last = pe.transpose(bank(0)[:, k * P:(k + 1) * P], at_in[:, r % 2, k * P:(k + 1) * P], ident[:, :])
                    last.then_inc(z["aT_ps"], 1)

            ticks(pe, n, f + 3, tick, HEAD, 2)

        def stage_scalar(act, st):
            z, f, n = st.s, st.f, st.tiles

            def tick(t, r):
                if st.has_kv and (i := tile_at(t, f + 3, n)) is not None:
                    m = st.rows(i)
                    act.wait_ge(z["kT"], i + 1)
                    act.activation(k_op[:, :, bass.ds(i * P, m)],
                                   bank(6 + (r - f - 3) % 2).bitcast(fp16).rearrange("p (h t) -> p h t", t=P)[:, :, 0:m],
                                   ACT.Copy).then_inc(z["kop"], 1)
                if (i := tile_at(t, f + 1, n)) is not None:
                    q, m = (r - f - 1) % 2, st.rows(i)
                    act.wait_ge(z["xT_ps"], i + 1)
                    if some(i - 1):
                        act.wait_ge(z["proj"], i - 1)
                    act.activation(xT[:, q, :, 0:m], bank(2)[:, 0:C].rearrange("p (k t) -> p k t", k=KC)[:, :, 0:m],
                                   ACT.Copy).then_inc(z["xT"], 1)
                if (i := tile_at(t, f + 2, n)) is not None:
                    q, m = (r - f - 2) % 2, st.rows(i)
                    act.wait_ge(z["hi"], i + 1)
                    if st.has_q:
                        last = act.activation(q_tok[0:m, i, :, D:2 * D], q_tok[0:m, i, :, 0:D], ACT.Copy)
                    if st.has_kv:
                        last = act.activation(k_tok[0:m, q, :, 2 * D:3 * D], k_tok[0:m, q, :, 0:D], ACT.Copy)
                    last.then_inc(z["copy"], 1)
                if st.front and (i := tile_at(t, f + 1, n)) is not None:
                    act.activation(src_sb[:, i, :], xin[:, (r - f - 1) % 2, :], ACT.Copy).then_inc(z["kept"], 1)
                if not st.loaded and (i := tile_at(t, f, n)) is not None:
                    norm_root(act, (r - f) % 2, z["ln"], 4 * i, z["root"])
                if st.front and (i := tile_at(t, 0, n)) is not None:
                    act.wait_ge(z["aT_ps"], i + 1)
                    if some(i - 1):
                        act.wait_ge(z["o_ps"], i - 1)
                    act.activation(aT[:, r % 2, :, :], bank(0)[:, 0:C].rearrange("p (k t) -> p k t", k=KC),
                                   ACT.Copy).then_inc(z["aT"], 1)

            ticks(act, n, f + 3, tick, HEAD, 2)

        def stage_vector(dve, st):
            z, f, n = st.s, st.f, st.tiles
            ck = C if st.has_q else 0
            first = C * (st.has_q + st.has_kv)

            def tick(t, r):
                if st.front and (i := tile_at(t, f, n)) is not None:
                    dve.wait_ge(z["o_ps"], i + 1)
                    dve.wait_ge(z["res_bias"], i + 1)
                    dve.tensor_tensor(x_sb[:, i, :], bank(1)[:, 0:C], x_sb[:, i, :], ALU.add).then_inc(z["res"], 1)
                    dve.wait_ge(z["res"], i + 1)
                if (i := tile_at(t, f + 2, n)) is not None:
                    q, m = (r - f - 2) % 2, st.rows(i)
                    dve.wait_ge(z["proj"], i + 1)
                    dve.tensor_tensor(qk32[0:m, q, 0:first], bank(3 + q)[0:m, 0:first], row(st.bias, first // C)[0:m, :],
                                      ALU.add).then_inc(z["sum"], 1)
                if not st.loaded and (b := tile_at(t, f, n)) is not None:
                    dve.bn_stats(stat6[:, (r - f) % 2, :], x_sb[:, b, :]).then_inc(z["ln"], 1)
                    dve.wait_ge(z["ln"], 4 * b + 1)
                if i is not None:
                    if st.has_kv:
                        v_ps = bank(5)[0:m, 0:C] if first == 2 * C else bank(3 + q)[0:m, C:2 * C]
                        dve.tensor_tensor(v_aug[0:m, i, :, 0:D], v_ps.rearrange("p (h d) -> p h d", h=H),
                                          row(st.bias, 3)[0:m, first:first + C].rearrange("p (h d) -> p h d", h=H)
                                          if st.has_q else row(st.bias, 2)[0:m, C:2 * C].rearrange("p (h d) -> p h d", h=H),
                                          ALU.add)
                    dve.wait_ge(z["sum"], i + 1)
                    parts = []
                    if st.has_q:
                        parts.append((q_tok[0:m, i, :, :], 2 * D, qk32[0:m, q, 0:C].rearrange("p (h d) -> p h d", h=H)))
                    if st.has_kv:
                        if some(i - 1):
                            dve.wait_ge(z["kT"], i - 1)
                        parts.append((k_tok[0:m, q, :, :], D, qk32[0:m, q, ck:ck + C].rearrange("p (h d) -> p h d", h=H)))
                    for op, _, full in parts:
                        last = dve.tensor_copy(op[:, :, 0:D], full)
                    last.then_inc(z["hi"], 1)
                    dve.wait_ge(z["hi"], i + 1)
                    for op, lo, full in parts:
                        last = dve.tensor_tensor(op[:, :, lo:lo + D], full, op[:, :, 0:D], ALU.subtract)
                    last.then_inc(z["split"], 1)
                if not st.loaded and (i := tile_at(t, f, n)) is not None:
                    norm_aggr(dve, (r - f) % 2, z["ln"])
                    if some(i - 1):
                        dve.wait_ge(z["xT_ps"], i - 1)
                        if st.front:
                            dve.wait_ge(z["kept"], i - 1)
                    norm_apply(dve, i, (r - f) % 2, x_sb[:, i, :], xin[:, (r - f) % 2, :], z["ln"], 4 * i, z["root"])

            ticks(dve, n, f + 3, tick, HEAD, 2)

        def stage_gpsimd(pool, st):
            z, f, n = st.s, st.f, st.tiles

            def tick(t, r):
                if st.front and (i := tile_at(t, 0, n)) is not None:
                    if some(i - 1):
                        pool.wait_ge(z["aT_ps"], i - 1)
                    pool.tensor_tensor(x_sb[:, i, :], x_sb[:, i, :], row("xattn_bo"), ALU.add).then_inc(z["res_bias"], 1)
                    pool.tensor_copy(at_in[:, r % 2, :], attn_tok[:, i, :]).then_inc(z["at"], 1)

            ticks(pool, n, f + 3, tick, HEAD, 2)

        def half(i, r):
            return i // 2 if isinstance(i, int) else (i - r % 2) // 2

        def stage_sync(sp, st):
            z, n = st.s, st.tiles

            def tick(t, r):
                m = st.rows(t)
                if some(t - 1):
                    sp.wait_ge(z["xT_ps"], t - 1)
                sp.dma_start(xin[0:m, r % 2, :], st.loaded[bass.ds(t * P, m), :]).then_inc(z[f"in{r % 2}"], 16)

            ticks(sp, n, 0, tick, HEAD, 2)

        ctx_kv = Stage("ctx", NCT, w_xkv, 2 * C, "xattn_bk", has_q=False, has_kv=True, loaded=io["ctx_1024"][0])
        cross_q = Stage("xq", NT, w_xq, C, "xattn_bq", has_q=True, has_kv=False)
        self_qkv = Stage("self", NT, w_fqkv, 3 * C, "ffn_bq", has_q=True, has_kv=True, front=w_xo)

        JOBS = NG * H // 2
        UNITS = 16
        SCALE = float(D) ** -0.5

        q_max = (sb("q_max", [P, 2, QG], fp16)[:, :, :],
                 w_xq[:, :, :].rearrange("p k n -> p (k n)").bitcast(fp16).rearrange("p (a q) -> p a q", a=2))
        q_exp = sb("q_exp", [P, 2, 2, QG], fp16)
        neg_max = sb("neg_max", [P, 2, GRP, 2, 4])
        o_sb = sb("o_sb", [P, QG])
        rden = sb("rden", [P, GRP * 4])
        prob = carve(p_arena, 0, 4, 1024)
        max_bank, o_bank, misc = (bank(4), bank(5)), bank(6), bank(7)
        q_op = q_tok.rearrange("p t h s -> p t (h s)")

        class Attention:
            def __init__(self, name, keys):
                self.tiles = [(i, min(P, keys - i * P)) for i in range(-(-keys // P))]
                self.n = len(self.tiles)
                width = -(-keys // 4)
                self.chunks = [(a, min(width, keys - a)) for a in range(0, keys, width)]
                self.s = {n: ctx.enter_context(nc.semaphore(f"{name}_{n}")) for n in (
                    "q_ps", "q_op", "max_ps", "max", "job", "score", "exp", "pv", "o_sb", "oT", "recip", "out")}
                self.until = [2 * UNITS * (i + 1) // self.n for i in range(self.n)]
                self.turn = next(i for i, u in enumerate(self.until) if u >= UNITS)

            def builds_at(self, h):
                return {1: ("qb", 2 * h + 2), 4: ("qa", 2 * h + 4),
                        self.turn + 1: ("qb", 2 * h + 3), self.turn + 3: ("qa", 2 * h + 5)}

            def maxima_at(self, h, kt, quarter=None):
                first, last = (4 * kt, 4 * kt + 4) if quarter is None else (4 * kt + quarter, 4 * kt + quarter + 1)
                total = 2 * 2 * UNITS
                return [(2 * h + 3 + i // (2 * UNITS), i // 2 % UNITS, i % 2)
                        for i in range(total * first // (4 * self.n), total * last // (4 * self.n))]

            def prob_at(self, h, kt, p):
                return (2 * self.n * h + 2 * kt + p) % 4

        def build_count(kind, n):
            if isinstance(n, int) and (kind, n) in (("qa", 0), ("qb", JOBS - 1)):
                return 1 if n == 0 else 2 * JOBS
            return 2 * n if kind == "qa" else 2 * n + 3

        def exists(n):
            return not isinstance(n, int) or n < JOBS

        def groups(eng, group):
            with eng.Fori(0, NG - 1) as g:
                group(g)
            group(NG - 1)

        FIRST_BUILDS = [("qa", 0), ("qa", 1), ("qb", 0), ("qa", 2), ("qb", 1), ("qa", 3)]

        def attention_tensor(pe, at):
            z = at.s

            def build(kind, g, r):
                n, pair, tile0 = 8 * g + r, r % 8, 4 * g + 4 * (r // 8)
                if kind == "qb":
                    pe.wait_ge(z["job"], n + 1)
                for q in range(GRP):
                    last = pe.matmul(misc[:, q * P:(q + 1) * P], q_op[:, tile0 + q, pair * P:(pair + 1) * P], ident16[:, :],
                                     start=True, stop=True)
                last.then_inc(z["q_ps"], 1)

            def maxima(g, r, u, j):
                n, pair, (k0, width) = 8 * g + r, r % 8, at.chunks[u % 4]
                if u == 0 and j == 0:
                    pe.wait_ge(z["q_op"], build_count("qa", n))
                before = 2 * (UNITS * n + u) + j - 1
                if some(before):
                    pe.wait_ge(z["max"], before)
                pe.matmul(max_bank[j][:, 0:width], q_max[j][:, r % 2, (u // 4) * P:(u // 4 + 1) * P],
                          k_op[:, pair, k0:k0 + width], start=True, stop=True).then_inc(z["max_ps"], 1)

            def sums(g, h, kt, part):
                m, it, whole = at.tiles[kt][1], 4 * g + h, kt in (0, at.n - 1)
                if whole and part == 0:
                    return
                if part == 0 or whole:
                    pe.wait_ge(z["exp"], 2 * at.n * it + 2 * kt + 2)
                if kt == 0 and h:
                    pe.wait_ge(z["o_sb"], it)
                q0, q1 = (0, QG) if whole else (part * QG // 2, (part + 1) * QG // 2)
                for hh in range(4):
                    last = pe.matmul(o_bank[32 * hh:32 * hh + 32, q0:q1], v_aug[0:m, kt, 4 * h + hh, :],
                                     prob[0:m, at.prob_at(h, kt, hh // 2), (hh % 2) * QG + q0:(hh % 2) * QG + q1],
                                     start=kt == 0, stop=kt == at.n - 1, tile_position=(0, 32 * hh))
                if part == 1:
                    last.then_inc(z["pv"], 1)

            def turn_sums(g, h):
                pe.wait_ge(z["o_sb"], 4 * g + h + 1)
                for q in range(GRP):
                    last = pe.transpose(misc[:, q * P:(q + 1) * P], o_sb[:, q * P:(q + 1) * P], ident[:, :])
                last.then_inc(z["oT"], 1)

            for i, (kind, r) in enumerate(FIRST_BUILDS):
                if i:
                    pe.wait_ge(z["q_op"], i)
                build(kind, 0, r)
                if i in (1, 3, 5):
                    for u in range(0 if i == 1 else 2, UNITS):
                        for j in range(2):
                            maxima(0, i // 2, u, j)
                    for u in range(0, 2 if i < 5 else 0):
                        for j in range(2):
                            maxima(0, i // 2 + 1, u, j)
            pe.wait_ge(z["q_op"], len(FIRST_BUILDS))

            def group(g):
                free = (z["out"], 4 * g + 1)
                for h in range(4):
                    it = 4 * g + h
                    for kt, m in at.tiles:
                        for quarter in range(4):
                            p = quarter // 2
                            if quarter % 2 == 0:
                                if kt == 0:
                                    pe.wait_ge(z["q_op"], build_count("qb", 8 * g + 2 * h + p))
                                if kt or h:
                                    pe.wait_ge(z["exp"], 2 * at.n * it + 2 * kt + p - 1)
                                for j in range(2):
                                    last = pe.matmul(s_pair[p][0:m, j * QG:(j + 1) * QG],
                                                     k_op[SLOT * j:SLOT * (j + 1), 2 * h + p, kt * P:kt * P + m],
                                                     q_exp[SLOT * j:SLOT * (j + 1), h % 2, p, :],
                                                     start=True, stop=True, tile_position=(SLOT * j, 0))
                                last.then_inc(z["score"], 1)
                            elif kt:
                                sums(g, h, kt - 1, p)
                            elif h:
                                sums(g, h - 1, at.n - 1, p)
                            for r, u, j in at.maxima_at(h, kt, quarter):
                                if exists(8 * g + r):
                                    maxima(g, r, u, j)
                        if kt in at.builds_at(h):
                            kind, r = at.builds_at(h)[kt]
                            if exists(8 * g + r):
                                pe.wait_ge(*free)
                                build(kind, g, r)
                                free = (z["q_op"], build_count(kind, 8 * g + r))
                        if kt == 2 and h:
                            pe.wait_ge(*free)
                            turn_sums(g, h - 1)
                            free = (z["out"], it + 1)
                for part in range(2):
                    sums(g, 3, at.n - 1, part)
                pe.wait_ge(*free)
                turn_sums(g, 3)

            groups(pe, group)

        def attention_scalar(act, at):
            z = at.s

            def read_build(kind, g, r):
                act.wait_ge(z["q_ps"], build_count(kind, 8 * g + r))
                if kind == "qa":
                    for j in range(2):
                        rows = slice(SLOT * j, SLOT * (j + 1))
                        last = act.activation(q_max[j][rows, r % 2, :], misc[rows, :], ACT.Copy)
                else:
                    last = act.activation(q_exp[:, (r // 2) % 2, r % 2, :], misc, ACT.Copy)
                last.then_inc(z["q_op"], 1)

            def read_sums(g, h):
                act.wait_ge(z["pv"], at.n * (4 * g + h + 1))
                act.activation(o_sb[:, :], o_bank, ACT.Copy).then_inc(z["o_sb"], 1)

            for kind, r in FIRST_BUILDS:
                read_build(kind, 0, r)

            def group(g):
                for h in range(4):
                    it = 4 * g + h
                    for kt, m in at.tiles:
                        for p in range(2):
                            act.wait_ge(z["score"], 2 * at.n * it + 2 * kt + p + 1)
                            if p == 0 and (kt >= 2 or h):
                                act.wait_ge(z["pv"], at.n * it + kt - 1)
                            act.activation(prob[0:m, at.prob_at(h, kt, p), :], s_pair[p][0:m, :], ACT.Exp,
                                           scale=SCALE).then_inc(z["exp"], 1)
                        if kt in at.builds_at(h):
                            kind, r = at.builds_at(h)[kt]
                            if exists(8 * g + r):
                                read_build(kind, g, r)
                        if kt == 0 and h:
                            read_sums(g, h - 1)
                read_sums(g, 3)

            groups(act, group)

        def attention_vector(dve, at):
            z = at.s
            dve.memset(rden[:, :], 1.0).then_inc(z["out"], 1)

            def maxima(g, r, u, j):
                n, (_, width) = 8 * g + r, at.chunks[u % 4]
                dve.wait_ge(z["max_ps"], 2 * (UNITS * n + u) + j + 1)
                dve.tensor_reduce(neg_max[:, r % 2, u // 4, j, u % 4:u % 4 + 1], max_bank[j][:, 0:width], AX.X, ALU.max,
                                  negate=True).then_inc(z["max"], 1)
                if u == UNITS - 1 and j == 1:
                    dve.wait_ge(z["max"], 2 * UNITS * (n + 1))
                    dve.tensor_reduce(q_tok[:, bass.ds(4 * g + 4 * (r // 8), GRP), 2 * (r % 8):2 * (r % 8) + 2, MROW],
                                      neg_max[:, r % 2, :, :, :], AX.X, ALU.min).then_inc(z["job"], 1)

            def result(g, h):
                it = 4 * g + h
                sums = misc.rearrange("p (q h d) -> p q h d", q=GRP, h=4)
                dve.wait_ge(z["oT"], it + 1)
                dve.reciprocal(rden[:, :].rearrange("p (q h) -> p q h", h=4), sums[:, :, :, D]).then_inc(z["recip"], 1)
                dve.wait_ge(z["recip"], it + 1)
                dve.tensor_tensor(attn_tok[:, bass.ds(4 * g, GRP), h * 4 * D:(h + 1) * 4 * D].rearrange("p q (h d) -> p q h d", h=4),
                                  sums[:, :, :, 0:D],
                                  rden[:, :].rearrange("p (q h) -> p q h", h=4).unsqueeze(3).broadcast_to([P, GRP, 4, D]),
                                  ALU.mult).then_inc(z["out"], 1)

            for r in range(3):
                for u in range(UNITS):
                    for j in range(2):
                        maxima(0, r, u, j)

            def group(g):
                for h in range(4):
                    for kt, _ in at.tiles:
                        for r, u, j in at.maxima_at(h, kt):
                            if exists(8 * g + r):
                                maxima(g, r, u, j)
                        if kt == 2 and h:
                            result(g, h - 1)
                result(g, 3)

            groups(dve, group)

        cross = Attention("cross", S_CTX)
        selfa = Attention("selfa", T)

        post = sems(*("post_" + n for n in ("at", "bias", "aT_ps", "aT", "o_ps", "ln", "root", "norm", "xT_ps", "x3T", "kept", "apply")))
        x3T = carve(q_arena, 0, KC, T)
        post_sum = band_tmp

        def post_gpsimd(pool):
            pool.wait_ge(selfa.s["out"], 4 * NG + 1)

            def tick(t, r):
                if (i := tile_at(t, 0, NT)) is not None:
                    if some(i - 1):
                        pool.wait_ge(post["post_aT_ps"], i - 1)
                    pool.tensor_tensor(src_sb[:, i, :], src_sb[:, i, :], row("ffn_bo"), ALU.add).then_inc(post["post_bias"], 1)
                    pool.tensor_copy(at_in[:, r % 2, :], attn_tok[:, i, :]).then_inc(post["post_at"], 1)

            ticks(pool, NT, 3, tick, HEAD, 2)
            pool.wait_ge(self_qkv.s["ln"], 4 * NT)
            pool.tensor_tensor(x_sb[:, :, :], x_sb[:, :, :], row("ffn_ln2_b").unsqueeze(1).broadcast_to([P, NT, C]),
                               ALU.add).then_inc(moe["moe_xb"], 1)

        def post_tensor(pe):
            z = post

            def tick(t, r):
                if (i := tile_at(t, 3, NT)) is not None:
                    pe.wait_ge(z["post_norm"], i + 1)
                    if some(i):
                        pe.wait_ge(z["post_x3T"], i)
                    for k in range(KC):
                        last = pe.transpose(bank(2)[:, k * P:(k + 1) * P], xin[:, (r - 3) % 2, k * P:(k + 1) * P], ident[:, :])
                    last.then_inc(z["post_xT_ps"], 1)
                if (i := tile_at(t, 1, NT)) is not None:
                    pe.wait_ge(z["post_aT"], i + 1)
                    if some(i):
                        pe.wait_ge(z["post_ln"], 3 * i - 2)
                    for k in range(KC):
                        last = pe.matmul(bank(1)[:, 0:C], aT[:, (r - 1) % 2, k, :], w_fo[:, k, :], start=k == 0, stop=k == KC - 1)
                    last.then_inc(z["post_o_ps"], 1)
                if (i := tile_at(t, 0, NT)) is not None:
                    pe.wait_ge(z["post_at"], i + 1)
                    if some(i):
                        pe.wait_ge(z["post_aT"], i)
                    for k in range(KC):
                        last = pe.transpose(bank(0)[:, k * P:(k + 1) * P], at_in[:, r % 2, k * P:(k + 1) * P], ident[:, :])
                    last.then_inc(z["post_aT_ps"], 1)

            ticks(pe, NT, 3, tick, HEAD, 2)

        def post_scalar(act):
            z = post

            def tick(t, r):
                if (i := tile_at(t, 3, NT)) is not None:
                    act.wait_ge(z["post_xT_ps"], i + 1)
                    act.activation(x3T[:, :, bass.ds(i * P, P)], bank(2)[:, 0:C].rearrange("p (k t) -> p k t", k=KC),
                                   ACT.Copy).then_inc(z["post_x3T"], 1)
                    act.activation(src_sb[:, i, :], xin[:, (r - 3) % 2, :], ACT.Copy).then_inc(z["post_kept"], 1)
                if (i := tile_at(t, 0, NT)) is not None:
                    act.wait_ge(z["post_aT_ps"], i + 1)
                    if some(i - 1):
                        act.wait_ge(z["post_o_ps"], i - 1)
                    act.activation(aT[:, r % 2, :, :], bank(0)[:, 0:C].rearrange("p (k t) -> p k t", k=KC),
                                   ACT.Copy).then_inc(z["post_aT"], 1)
                if (i := tile_at(t, 1, NT)) is not None:
                    q = (r - 1) % 2
                    act.wait_ge(z["post_ln"], 3 * i + 3)
                    act.activation(rstd[:, q:q + 1], mean_var[:, q, 1:2], ACT.Sqrt, bias=eps_col[:, :]).then_inc(z["post_root"], 1)

            ticks(act, NT, 3, tick, HEAD, 2)

        def post_vector(dve):
            z = post
            dve.wait_ge(s["ld_small"], 16 * 4)
            for k in range(KC):
                dve.tensor_copy(router_rep[:, k, :], router_col[:, k:k + 1].broadcast_to([P, P])).then_inc(moe["moe_rep"], 1)
            dve.wait_ge(s["iota"], 1)
            dve.tensor_copy(expert_col[:, :], expert_no[:, :]).then_inc(moe["moe_rep"], 1)

            def tick(t, r):
                if (i := tile_at(t, 1, NT)) is not None:
                    q = (r - 1) % 2
                    dve.wait_ge(z["post_o_ps"], i + 1)
                    dve.wait_ge(z["post_bias"], i + 1)
                    dve.tensor_tensor(post_sum[:, q, :], bank(1)[:, 0:C], src_sb[:, i, :], ALU.add).then_inc(z["post_ln"], 1)
                    dve.wait_ge(z["post_ln"], 3 * i + 1)
                    dve.bn_stats(stat6[:, q, :], post_sum[:, q, :]).then_inc(z["post_ln"], 1)
                    dve.wait_ge(z["post_ln"], 3 * i + 2)
                b = tile_at(t, 2, NT)
                p = (r - 2) % 2
                if b is not None:
                    dve.wait_ge(z["post_root"], b + 1)
                    dve.reciprocal(rstd[:, p:p + 1], rstd[:, p:p + 1]).then_inc(z["post_apply"], 1)
                if i is not None:
                    dve.bn_aggr(mean_var[:, q, :], stat6[:, q, :]).then_inc(z["post_ln"], 1)
                if b is not None:
                    dve.scalar_tensor_tensor(post_sum[:, p, :], post_sum[:, p, :], mean_var[:, p, 0:1], row("ffn_ln1_g"),
                                             ALU.subtract, ALU.mult).then_inc(z["post_apply"], 1)
                    dve.wait_ge(z["post_apply"], 2 * b + 2)
                    if some(b - 1):
                        dve.wait_ge(z["post_xT_ps"], b - 1)
                        dve.wait_ge(z["post_kept"], b - 1)
                    dve.scalar_tensor_tensor(xin[:, p, :], post_sum[:, p, :], rstd[:, p:p + 1], row("ffn_ln1_b"),
                                             ALU.mult, ALU.add).then_inc(z["post_norm"], 1)

            ticks(dve, NT, 3, tick, HEAD, 2)

        moe = sems(*("moe_" + n for n in ("w0", "w1", "w2", "w3", "rep", "key_ps", "key", "idx", "onehot", "h_ps", "relu", "hm", "y",
                                          "y_read", "stats", "aggr", "root", "recip", "diff", "xb", "out", "stored")))
        STEPS = E * FC
        w1_sb = k_op[:, :, :].rearrange("p a b -> p (a b)").bitcast(fp32).rearrange("p (e k f) -> p e k f", e=E, k=KC)
        w2_sb = v_aug[:, :, :, :].rearrange("p t h d -> p (t h d)").rearrange("p (e c n) -> p e c n", e=E, c=FC)
        expert = carve(q_arena, KC * T, T)
        key = carve(q_arena, KC * T + T, T)
        out_sb = attn_tok
        key_int = attn_tok[:, :, :].rearrange("p t c -> p (t c)")[:, 0:T].bitcast(i32)
        hidden = carve(p_arena, 1024, 2, QG)
        masked = carve(p_arena, 2048, 2, QG)
        moe_sum = w_xkv[:, :, :].rearrange("p k n -> p (k n)").rearrange("p (q c) -> p q c", c=C)
        onehot = w_fqkv[0:E, 0, 0:QG]
        router_rep = w_fqkv[:, 1, 0:KC * P].rearrange("p (k n) -> p k n", n=P)
        y_ps = [bank(q)[:, 0:C] for q in range(GRP)]
        h_bank, key_bank = (bank(4), bank(5)), tuple(bank(4 + g) for g in range(NG))

        def moe_sync(sp):
            sp.wait_ge(selfa.s["out"], 4 * NG + 1)
            for e in range(E):
                sp.dma_start(w1_sb[:, e, :, :], io["L0_ffn_W1"][e].rearrange("(k p) f -> p k f", p=P)).then_inc(moe[f"moe_w{e}"], 16)
                sp.dma_start(w2_sb[:, e, :, :], io["L0_ffn_W2"][e].rearrange("(c p) n -> p c n", p=P)).then_inc(moe[f"moe_w{e}"], 16)
            with sp.Fori(0, NG) as g:
                sp.wait_ge(moe["moe_out"], GRP * g + GRP)
                sp.dma_start(out_view[:, bass.ds(GRP * g, GRP), :], out_sb[:, bass.ds(GRP * g, GRP), :]).then_inc(moe["moe_stored"], 16)
            sp.wait_ge(moe["moe_stored"], 16 * NG)

        def moe_tensor(pe):
            z = moe
            pe.wait_ge(z["moe_rep"], KC + 1)
            pe.wait_ge(post["post_x3T"], NT)
            for g in range(NG):
                for k in range(KC):
                    last = pe.matmul(key_bank[g], router_rep[:, k, :], x3T[:, k, g * QG:(g + 1) * QG],
                                     start=k == 0, stop=k == KC - 1)
                last.then_inc(z["moe_key_ps"], 1)
            pe.wait_ge(z["moe_key"], NG)

            with pe.Fori(0, NG) as g:
                def hidden_units(step):
                    e, c = step // FC, step % FC
                    pe.wait_ge(z[f"moe_w{e}"], 32)
                    for k in range(KC):
                        last = pe.matmul(h_bank[step % 2], w1_sb[:, e, k, c * P:(c + 1) * P], x3T[:, k, bass.ds(g * QG, QG)],
                                         start=k == 0, stop=k == KC - 1)
                    last.then_inc(z["moe_h_ps"], 1)

                def outputs(step):
                    e, c = step // FC, step % FC
                    pe.wait_ge(z["moe_hm"], STEPS * g + step + 1)
                    if step == 0:
                        pe.wait_ge(z["moe_y_read"], GRP * g + 1)
                    for q in range(GRP):
                        pe.matmul(y_ps[q], masked[:, step % 2, q * P:(q + 1) * P], w2_sb[:, e, c, :],
                                  start=step == 0, stop=False)

                for step in range(STEPS):
                    hidden_units(step)
                    if step:
                        outputs(step - 1)
                outputs(STEPS - 1)
                pe.wait_ge(z["moe_onehot"], g + 1)
                for q in range(GRP):
                    last = pe.matmul(y_ps[q], onehot[:, q * P:(q + 1) * P], b2_sb[:, :], start=False, stop=True)
                last.then_inc(z["moe_y"], 1)

        def moe_scalar(act):
            z = moe
            act.wait_ge(s["ld_small"], 16 * 4)
            act.wait_ge(post["post_norm"], NT)
            with act.Fori(0, NG) as g:
                for step in range(STEPS):
                    act.wait_ge(z["moe_h_ps"], STEPS * g + step + 1)
                    act.activation(hidden[:, step % 2, :], h_bank[step % 2], ACT.Relu,
                                   bias=b1_col[:, step // FC, step % FC:step % FC + 1]).then_inc(z["moe_relu"], 1)
                for q in range(GRP):
                    act.wait_ge(z["moe_aggr"], GRP * g + q + 1)
                    act.activation(rstd[:, q:q + 1], mean_var[:, q, 1:2], ACT.Sqrt, bias=eps_col[:, :]).then_inc(z["moe_root"], 1)

        def moe_vector(dve):
            z = moe
            for g in range(NG):
                dve.wait_ge(z["moe_key_ps"], g + 1)
                dve.tensor_scalar(key[:, g * QG:(g + 1) * QG], key_bank[g], router_col[:, KC:KC + 1], None, ALU.add).then_inc(z["moe_key"], 1)
            dve.wait_ge(z["moe_key"], NG)
            dve.tensor_copy(key_int, key).then_inc(z["moe_idx"], 1)
            dve.wait_ge(z["moe_idx"], 1)
            dve.tensor_copy(expert, key_int).then_inc(z["moe_idx"], 1)
            dve.wait_ge(z["moe_idx"], 2)
            dve.tensor_tensor(key, expert, key, ALU.is_gt).then_inc(z["moe_idx"], 1)
            dve.wait_ge(z["moe_idx"], 3)
            dve.tensor_tensor(expert, expert, key, ALU.subtract).then_inc(z["moe_idx"], 1)
            dve.wait_ge(z["moe_idx"], 4)
            dve.tensor_copy(key_int, expert).then_inc(z["moe_idx"], 1)
            dve.wait_ge(z["moe_idx"], 5)
            dve.tensor_scalar(key_int, key_int, E - 1, None, ALU.bitwise_and).then_inc(z["moe_idx"], 1)
            dve.wait_ge(z["moe_idx"], 6)
            dve.tensor_copy(expert, key_int).then_inc(z["moe_idx"], 1)
            dve.memset(moe_sum[:, 0, 0:1], 0.0).then_inc(z["moe_y_read"], 1)
            dve.wait_ge(z["moe_idx"], 7)

            with dve.Fori(0, NG) as g:
                dve.tensor_scalar(onehot, expert[0:E, bass.ds(g * QG, QG)], expert_col[:, :], None,
                                  ALU.is_equal).then_inc(z["moe_onehot"], 1)
                for step in range(STEPS):
                    dve.wait_ge(z["moe_relu"], STEPS * g + step + 1)
                    dve.scalar_tensor_tensor(masked[:, step % 2, :], expert[:, bass.ds(g * QG, QG)], float(step // FC),
                                             hidden[:, step % 2, :], ALU.is_equal, ALU.mult).then_inc(z["moe_hm"], 1)
                dve.wait_ge(z["moe_y"], g + 1)
                for q in range(GRP):
                    dve.tensor_tensor(moe_sum[:, q, :], y_ps[q], src_sb[:, bass.ds(GRP * g + q, 1), :],
                                      ALU.add).then_inc(z["moe_y_read"], 1)
                for q in range(GRP):
                    dve.wait_ge(z["moe_y_read"], GRP * g + q + 2)
                    dve.bn_stats(stat6[:, q, :], moe_sum[:, q, :]).then_inc(z["moe_stats"], 1)
                dve.wait_ge(s["ld_rows"], 16 * len(ROWS))
                dve.wait_ge(z["moe_stats"], GRP * g + GRP)
                for q in range(GRP):
                    dve.bn_aggr(mean_var[:, q, :], stat6[:, q, :]).then_inc(z["moe_aggr"], 1)
                for q in range(GRP):
                    dve.wait_ge(z["moe_aggr"], GRP * g + q + 1)
                    dve.scalar_tensor_tensor(moe_sum[:, q, :], moe_sum[:, q, :], mean_var[:, q, 0:1], row("ffn_ln2_g"),
                                             ALU.subtract, ALU.mult).then_inc(z["moe_diff"], 1)
                dve.wait_ge(z["moe_root"], GRP * g + GRP)
                dve.reciprocal(rstd[:, :], rstd[:, :]).then_inc(z["moe_recip"], 1)
                dve.wait_ge(z["moe_xb"], 1)
                for q in range(GRP):
                    dve.wait_ge(z["moe_recip"], g + 1)
                    dve.wait_ge(z["moe_diff"], GRP * g + GRP)
                    dve.scalar_tensor_tensor(out_sb[:, bass.ds(GRP * g + q, 1), :], moe_sum[:, q:q + 1, :], rstd[:, q:q + 1],
                                             x_sb[:, bass.ds(GRP * g + q, 1), :], ALU.mult, ALU.add).then_inc(z["moe_out"], 1)

        @block.sync
        def _(sp):
            sp.dma_start(x_sb[:, 0:GRP, :], x_view[:, 0:GRP, :]).then_inc(s["ld_x0"], 16)
            sp.dma_start(w_band[:, :, :], io["L0_attn_W_qkv"].rearrange("(k p) n -> p k n", p=P)).then_inc(s["ld_band"], 16)
            sp.dma_start(bqk_col[:, :], io["L0_attn_b_qkv"][0:2 * C].rearrange("(f p) -> p f", p=P),
                         allow_slow_non_contiguous=True).then_inc(s["ld_band"], 16)
            sp.dma_start(band_rows[:, 0, :], io["L0_attn_b_qkv"][2 * C:3 * C].partition_broadcast(P)).then_inc(s["ld_band"], 16)
            sp.dma_start(band_rows[:, 1, :], io["L0_attn_ln_w"].partition_broadcast(P)).then_inc(s["ld_band"], 16)
            sp.dma_start(band_rows[:, 2, :], io["L0_attn_ln_b"].partition_broadcast(P)).then_inc(s["ld_band"], 16)
            sp.dma_start(x_sb[:, GRP:NT, :], x_view[:, GRP:NT, :]).then_inc(s["ld_x"], 16)
            for w, n in enumerate(("Wq", "Wk", "Wv", "Wo")):
                sp.dma_start(w_xraw[:, w, :, :], io["L0_xattn_" + n].rearrange("(o p) i -> p o i", p=P)).then_inc(s["ld_xw"], 16)
            for n in ROWS:
                sp.dma_start(row(n), io["L0_" + n].partition_broadcast(P)).then_inc(s["ld_rows"], 16)
            sp.dma_start(b1_col[:, :, :], io["L0_ffn_b1"].rearrange("e (c p) -> p e c", p=P),
                         allow_slow_non_contiguous=True).then_inc(s["ld_small"], 16)
            sp.dma_start(b2_sb[:, :], io["L0_ffn_b2"]).then_inc(s["ld_small"], 16)
            sp.dma_start(router_col[:, 0:KC], io["L0_ffn_router_w"].rearrange("(k p) o -> p (k o)", p=P),
                         allow_slow_non_contiguous=True).then_inc(s["ld_small"], 16)
            sp.dma_start(router_col[:, KC:KC + 1], io["L0_ffn_router_b"].partition_broadcast(P)).then_inc(s["ld_small"], 16)
            for w, n in enumerate(("Wq", "Wk", "Wv")):
                sp.dma_start(w_fqkv[:, :, w * C:(w + 1) * C], io["L0_ffn_" + n].rearrange("(k p) n -> p k n", p=P)).then_inc(s["ld_fw"], 16)
            sp.dma_start(w_fo[:, :, :], io["L0_ffn_Wo"].rearrange("(k p) n -> p k n", p=P)).then_inc(s["ld_fw"], 16)
            sp.wait_ge(s["band_xT_ps"], NT)
            stage_sync(sp, ctx_kv)
            moe_sync(sp)

        @block.gpsimd
        def _(pool):
            pool.memset(eps_col[:, :], EPS).then_inc(s["const"], 1)
            pool.iota(expert_no[:, :], pattern=[[0, 1]], base=0, channel_multiplier=1).then_inc(s["iota"], 1)
            pool.memset(ident[:, :], 0.0).then_inc(s["const_zero"], 1)
            pool.memset(ident16[:, :], 0.0).then_inc(s["const_zero"], 1)
            pool.memset(band_mask[:, :], BAND_SCALE).then_inc(s["const_zero"], 1)
            pool.wait_ge(s["const_zero"], 3)
            for m in (ident, ident16):
                pool.affine_select(out=m[:, :], in_=m[:, :], compare_op=ALU.not_equal, fill=1.0, base=0,
                                   pattern=[[-1, P]], channel_multiplier=1).then_inc(s["const"], 1)
            pool.affine_select(out=band_mask[:, :], in_=band_mask[:, :], compare_op=ALU.is_ge, fill=0.0, base=0,
                               pattern=[[1, 2 * P]], channel_multiplier=-1).then_inc(s["const_zero"], 1)
            pool.wait_ge(s["const_zero"], 4)
            pool.affine_select(out=band_mask[:, :], in_=band_mask[:, :], compare_op=ALU.is_ge, fill=0.0, base=SPAN - 1,
                               pattern=[[-1, 2 * P]], channel_multiplier=1).then_inc(s["const"], 1)
            pool.memset(v_aug[:, :, :, D:2 * D], 0.0).then_inc(s["v_const"], 1)
            pool.wait_ge(s["v_const"], 1)
            pool.memset(v_aug[:, :, :, D:D + 1], 1.0).then_inc(s["v_const"], 1)
            for q in range(2):
                pool.memset(k_tok[:, q, :, MROW:SLOT], 0.0).then_inc(s["k_const"], 1)
            pool.wait_ge(s["k_const"], 2)
            for q in range(2):
                pool.memset(k_tok[:, q, :, MROW:MROW + 1], 1.0).then_inc(s["k_const"], 1)
            band_gpsimd(pool)
            pool.wait_ge(s["xw_ps"], 4)
            pool.wait_ge(s["band_out"], 5 * NT)
            pool.memset(q_tok[:, :, :, MROW:SLOT], 0.0).then_inc(s["q_const"], 1)
            pool.wait_ge(cross_q.s["proj"], NT)
            for j in range(2):
                pool.wait_ge(s["q_const"], j + 1)
                pool.memset(q_max[j][SLOT * (1 - j):SLOT * (2 - j), :, :], 0.0).then_inc(s["q_const"], 1)
            pool.wait_ge(s["q_const"], 3)
            pool.wait_ge(cross.s["out"], 4 * NG + 1)
            pool.memset(q_tok[:, :, :, MROW:MROW + 1], 0.0).then_inc(s["q_const"], 1)
            for q in range(2):
                pool.memset(k_tok[:, q, :, MROW:SLOT], 0.0).then_inc(s["k_const"], 1)
            pool.wait_ge(s["k_const"], 6)
            for q in range(2):
                pool.memset(k_tok[:, q, :, MROW:MROW + 1], 1.0).then_inc(s["k_const"], 1)
            stage_gpsimd(pool, self_qkv)
            post_gpsimd(pool)

        @block.tensor
        def _(pe):
            band_tensor(pe)
            weights_tensor(pe)
            pe.wait_ge(s["band_st"], NT)
            pe.wait_ge(s["band_out"], 5 * NT)
            pe.wait_ge(s["xw"], 4)
            pe.wait_ge(s["k_const"], 4)
            stage_tensor(pe, ctx_kv)
            pe.wait_ge(ctx_kv.s["split"], NCT)
            stage_tensor(pe, cross_q)
            pe.wait_ge(cross_q.s["split"], NT)
            pe.wait_ge(cross_q.s["copy"], NT)
            pe.wait_ge(s["q_const"], 3)
            pe.wait_ge(s["v_const"], 2)
            pe.wait_ge(ctx_kv.s["kop"], NCT)
            attention_tensor(pe, cross)
            pe.wait_ge(cross.s["out"], 4 * NG + 1)
            pe.wait_ge(s["k_const"], 8)
            pe.wait_ge(s["ld_fw"], 16 * 4)
            stage_tensor(pe, self_qkv)
            pe.wait_ge(self_qkv.s["split"], NT)
            pe.wait_ge(self_qkv.s["copy"], NT)
            pe.wait_ge(self_qkv.s["kop"], NT)
            pe.wait_ge(s["q_const"], 4)
            attention_tensor(pe, selfa)
            pe.wait_ge(selfa.s["out"], 4 * NG + 1)
            post_tensor(pe)
            moe_tensor(pe)

        @block.scalar
        def _(act):
            band_scalar(act)
            weights_scalar(act)
            stage_scalar(act, ctx_kv)
            stage_scalar(act, cross_q)
            attention_scalar(act, cross)
            stage_scalar(act, self_qkv)
            attention_scalar(act, selfa)
            post_scalar(act)
            moe_scalar(act)

        @block.vector
        def _(dve):
            band_vector(dve)
            dve.wait_ge(s["ld_rows"], 16 * len(ROWS))
            stage_vector(dve, ctx_kv)
            dve.wait_ge(s["xw_ps"], 4)
            stage_vector(dve, cross_q)
            attention_vector(dve, cross)
            stage_vector(dve, self_qkv)
            attention_vector(dve, selfa)
            post_vector(dve)
            moe_vector(dve)


_NAMES = ["x", "ctx_1024"] + ["L0_attn_" + n for n in ("W_qkv", "b_qkv", "ln_w", "ln_b")] + \
    ["L0_xattn_" + n for n in ("Wq", "bq", "Wk", "bk", "Wv", "bv", "Wo", "bo")] + \
    ["L0_ffn_" + n for n in ("Wq", "bq", "Wk", "bk", "Wv", "bv", "Wo", "bo", "router_w", "router_b",
                             "W1", "b1", "W2", "b2", "ln1_g", "ln1_b", "ln2_g", "ln2_b")]


def kernel(**inputs):
    import numpy as _np
    import concourse.bacc as _bacc
    from concourse import mybir as _mybir
    from concourse.bass_utils import run_bass_kernel_spmd as _run

    nc = _bacc.Bacc("TRN2", target_bir_lowering=False, num_devices=1)
    arrays, io = {}, {}
    for name in _NAMES:
        a = _np.ascontiguousarray(inputs[name])
        arrays[f"in_{name}"] = a
        io[name] = nc.dram_tensor(f"in_{name}", a.shape, _mybir.dt.from_np(a.dtype), kind="ExternalInput").ap()
    x = arrays["in_x"]
    out = nc.dram_tensor("out_x", x.shape, _mybir.dt.from_np(x.dtype), kind="ExternalOutput").ap()
    decoder_layer_kernel(nc, io, out)
    r = _run(nc, [arrays], core_ids=[0])
    return r.results[0]["out_x"]
```

```python
import concourse.bass as bass
from concourse import mybir
from contextlib import ExitStack


def decoder_layer_kernel(nc, io, out):
    fp32, fp16, i32 = mybir.dt.float32, mybir.dt.float16, mybir.dt.int32
    ALU = mybir.AluOpType
    ACT = mybir.ActivationFunctionType
    AX = mybir.AxisListType

    P = 128
    T, C = io["x"].shape[1:]
    S_CTX = io["ctx_1024"].shape[1]
    NT = T // P
    KC = C // P
    GRP = 4
    NG = NT // GRP
    QG = GRP * P
    EPS = 1e-5
    SPAN = 64
    BAND_SCALE = 1.0 / float((C * SPAN) ** 0.5)
    H, D = 16, C // 16
    SLOT = 64
    MROW = 3 * D
    NCT = -(-S_CTX // P)
    CTX_LAST = S_CTX - (NCT - 1) * P

    ctx = ExitStack()
    with ctx:
        def sb(name, shape, dt=fp32):
            return ctx.enter_context(nc.sbuf_tensor(name, shape, dt))

        def sems(*names):
            return {n: ctx.enter_context(nc.semaphore(n)) for n in names}

        x_sb = sb("x_sb", [P, NT, C])
        src_sb = sb("src_sb", [P, NT, C])
        k_op = sb("k_op", [P, H // 2, T], fp16)
        v_aug = sb("v_aug", [P, NT, H, 2 * D])
        q_arena = sb("q_arena", [P, NT * H * SLOT // 2])
        attn_tok = sb("attn_tok", [P, NT, C])
        p_arena = sb("p_arena", [P, 4 * 1024])
        w_xq = sb("w_xq", [P, KC, C])
        w_xkv = sb("w_xkv", [P, KC, 2 * C])
        w_xo = sb("w_xo", [P, KC, C])
        w_fqkv = sb("w_fqkv", [P, KC, 3 * C])
        w_fo = sb("w_fo", [P, KC, C])
        ROWS = ["xattn_bq", "xattn_bk", "xattn_bv", "xattn_bo", "ffn_bq", "ffn_bk", "ffn_bv", "ffn_bo",
                "ffn_ln1_g", "ffn_ln1_b", "ffn_ln2_g", "ffn_ln2_b"]
        rows = sb("rows", [P, len(ROWS), C])

        def row(name, n=1):
            i = ROWS.index(name)
            return rows[:, i:i + n, :].rearrange("p n c -> p (n c)")

        ident = sb("ident", [P, P])
        ident16 = sb("ident16", [P, P], fp16)
        band_mask = sb("band_mask", [P, 2 * P])
        stat6 = sb("stat6", [P, 4, 6])
        mean_var = sb("mean_var", [P, 4, 2])
        rstd = sb("rstd", [P, 4])
        eps_col = sb("eps_col", [P, 1])
        E, F = io["L0_ffn_W1"].shape[0], io["L0_ffn_W1"].shape[2]
        FC = F // P
        b1_col = sb("b1_col", [P, E, FC])
        b1_use = sb("b1_use", [P, FC])
        router_col = sb("router_col", [P, KC + 1])
        dest = sb("dest", [P, NT], i32)

        def carve(arena, at, *shape):
            n = 1
            for k in shape:
                n *= k
            v = arena[:, at:at + n]
            if len(shape) == 2:
                v = v.rearrange("p (a b) -> p a b", b=shape[1])
            if len(shape) == 3:
                v = v.rearrange("p (a b c) -> p a b c", b=shape[1], c=shape[2])
            return v

        q_tok = q_arena[:, :].bitcast(fp16).rearrange("p (t h s) -> p t h s", h=H, s=SLOT)
        w_band = carve(q_arena, 0, KC, 3 * C)
        band_qk = carve(q_arena, 1536, 4, 4, P)
        band_v = carve(q_arena, 3584, 4, C)
        band_st = carve(q_arena, 4608, 2, 2 * P)
        w_xraw = carve(q_arena, 5120, 4, KC, C)
        band_rows = carve(q_arena, 7168, 3, C)
        band_tmp = sb("band_tmp", [P, 2, C])
        bqk_col = sb("bqk_col", [P, 4])
        xin = carve(p_arena, 0, 2, C)
        xT = carve(p_arena, 512, 2, KC, P)

        s_pair = [ctx.enter_context(nc.psum_tensor(f"s_pair{i}", [P, 1024], fp32)) for i in range(2)]
        singles = [ctx.enter_context(nc.psum_tensor(f"bank{i}", [P, 512], fp32)) for i in range(4, 8)]

        def bank(i):
            return s_pair[i // 2][:, (i % 2) * 512:(i % 2 + 1) * 512] if i < 4 else singles[i - 4][:, :]

        s = sems("ld_x0", "ld_x", "ld_band", "ld_xw", "ld_rows", "ld_fw", "const_zero", "const", "stored",
                 "band_zero", "band_ln", "band_xT_ps", "band_xT", "band_qkv_ps", "band_qkv", "band_s", "band_st",
                 "band_av", "band_out", "band_root", "band_ln_root", "band_xb", "xw_ps", "xw", "v_const", "k_const", "q_const",
                 "ld_small")

        x_view = io["x"][0].rearrange("(t p) c -> p t c", p=P)
        out_view = out[0].rearrange("(t p) c -> p t c", p=P)

        def ticks(eng, n, depth, tick, head=GRP, unroll=GRP):
            loops = (n - head) // unroll
            for t in range(head):
                tick(t, t % unroll)
            with eng.Fori(head // unroll, head // unroll + loops) as g:
                for r in range(unroll):
                    tick(g * unroll + r, r)
            for t in range(head + loops * unroll, n + depth):
                tick(t, t % unroll)

        def tile_at(t, stage, n):
            if isinstance(t, int) and not 0 <= t - stage < n:
                return None
            return t - stage

        def some(t, least=1):
            return not isinstance(t, int) or t >= least

        block = ctx.enter_context(nc.Block())

        def norm_aggr(dve, ring, steps):
            dve.bn_aggr(mean_var[:, ring, :], stat6[:, ring, :]).then_inc(steps, 1)

        def norm_root(act, ring, steps, count, roots):
            act.wait_ge(steps, count + 2)
            act.activation(rstd[:, ring:ring + 1], mean_var[:, ring, 1:2], ACT.Sqrt, bias=eps_col[:, :]).then_inc(roots, 1)

        def norm_apply(dve, i, ring, source, dest, steps, count, roots):
            dve.wait_ge(roots, i + 1)
            dve.reciprocal(rstd[:, ring:ring + 1], rstd[:, ring:ring + 1]).then_inc(steps, 1)
            dve.wait_ge(steps, count + 3)
            dve.tensor_scalar(dest, source, mean_var[:, ring, 0:1], rstd[:, ring:ring + 1],
                              ALU.subtract, ALU.mult).then_inc(steps, 1)

        def band_tensor(pe):
            pe.wait_ge(s["const"], 4)
            pe.wait_ge(s["ld_band"], 16 * 5)
            pe.wait_ge(s["band_zero"], 2)

            def tick(t, r):
                if (i := tile_at(t, 3, NT)) is not None:
                    pe.wait_ge(s["band_st"], i + 1)
                    if some(i):
                        pe.wait_ge(s["band_out"], 5 * i)
                    q, prev = (r - 3) % 4, (r - 4) % 4
                    pe.matmul(bank(7)[:, 0:C], band_st[:, q % 2, 0:P], band_v[:, q, :], start=True, stop=False)
                    pe.matmul(bank(7)[:, 0:C], band_st[:, q % 2, P:2 * P], band_v[:, prev, :],
                              start=False, stop=True).then_inc(s["band_av"], 1)
                if (i := tile_at(t, 2, NT)) is not None:
                    pe.wait_ge(s["band_qkv"], 2 * i + 2)
                    if some(i):
                        pe.wait_ge(s["band_st"], i)
                    q, prev = (r - 2) % 4, (r - 3) % 4
                    for part, keys in ((0, q), (1, prev)):
                        for k in range(KC):
                            last = pe.matmul(bank(6)[:, part * P:(part + 1) * P], band_qk[:, keys, KC + k, :],
                                             band_qk[:, q, k, :], start=k == 0, stop=k == KC - 1)
                    last.then_inc(s["band_s"], 1)
                if (i := tile_at(t, 1, NT)) is not None:
                    pe.wait_ge(s["band_xT"], i + 1)
                    if some(i - 1):
                        pe.wait_ge(s["band_qkv"], 2 * (i - 1))
                    q = (r - 1) % 2
                    for f in range(4):
                        for k in range(KC):
                            pe.matmul(bank(2 + q)[:, f * P:(f + 1) * P], w_band[:, k, f * P:(f + 1) * P], xT[:, q, k, :],
                                      start=k == 0, stop=k == KC - 1)
                    for k in range(KC):
                        last = pe.matmul(bank(4 + q)[:, 0:C], xT[:, q, k, :], w_band[:, k, 2 * C:3 * C],
                                         start=k == 0, stop=k == KC - 1)
                    last.then_inc(s["band_qkv_ps"], 1)
                if (i := tile_at(t, 0, NT)) is not None:
                    pe.wait_ge(s["band_ln"], 4 * i + 4)
                    if some(i - 1):
                        pe.wait_ge(s["band_xT"], i - 1)
                    q = r % 2
                    for k in range(KC):
                        last = pe.transpose(bank(q)[:, k * P:(k + 1) * P], xin[:, q, k * P:(k + 1) * P], ident[:, :])
                    last.then_inc(s["band_xT_ps"], 1)

            ticks(pe, NT, 3, tick)

        def band_scalar(act):
            act.wait_ge(s["const"], 1)

            def tick(t, r):
                if (i := tile_at(t, 3, NT)) is not None:
                    norm_root(act, 2 + (r - 3) % 2, s["band_out"], 5 * i, s["band_root"])
                if (i := tile_at(t, 0, NT)) is not None:
                    norm_root(act, r % 2, s["band_ln"], 4 * i, s["band_ln_root"])
                    act.wait_ge(s["band_xT_ps"], i + 1)
                    if some(i - 1):
                        act.wait_ge(s["band_qkv_ps"], i - 1)
                    act.activation(xT[:, r % 2, :, :], bank(r % 2)[:, 0:C].rearrange("p (k t) -> p k t", k=KC),
                                   ACT.Copy).then_inc(s["band_xT"], 1)

            ticks(act, NT, 3, tick)

        def band_vector(dve):
            dve.memset(band_qk[:, 3, :, :], 0.0).then_inc(s["band_zero"], 1)
            dve.memset(band_v[:, 3, :], 0.0).then_inc(s["band_zero"], 1)
            dve.wait_ge(s["ld_x0"], 16)

            def tick(t, r):
                if isinstance(t, int) and t == GRP - 1:
                    dve.wait_ge(s["ld_x"], 16)
                o = bank(7)[:, 0:C]
                q3 = (r - 3) % 2
                if (i := tile_at(t, 3, NT)) is not None:
                    dve.wait_ge(s["band_av"], i + 1)
                    dve.bn_stats(stat6[:, 2 + q3, :], o).then_inc(s["band_out"], 1)
                if (i := tile_at(t, 0, NT)) is not None:
                    dve.bn_stats(stat6[:, r % 2, :], x_sb[:, i, :]).then_inc(s["band_ln"], 1)
                    dve.wait_ge(s["band_ln"], 4 * i + 1)
                if (i := tile_at(t, 3, NT)) is not None:
                    dve.wait_ge(s["band_out"], 5 * i + 1)
                if (i := tile_at(t, 2, NT)) is not None:
                    dve.wait_ge(s["band_s"], i + 1)
                    if some(i - 1):
                        dve.wait_ge(s["band_av"], i - 1)
                    dve.tensor_tensor(band_st[:, (r - 2) % 2, :], bank(6)[:, 0:2 * P], band_mask[:, :],
                                      ALU.mult).then_inc(s["band_st"], 1)
                if tile_at(t, 3, NT) is not None:
                    norm_aggr(dve, 2 + q3, s["band_out"])
                if tile_at(t, 0, NT) is not None:
                    norm_aggr(dve, r % 2, s["band_ln"])
                if (i := tile_at(t, 3, NT)) is not None:
                    dve.wait_ge(s["band_out"], 5 * i + 2)
                    ring, c = 2 + q3, 5 * i
                    dve.scalar_tensor_tensor(band_tmp[:, q3, :], o, mean_var[:, ring, 0:1], band_rows[:, 1, :],
                                             ALU.subtract, ALU.mult).then_inc(s["band_out"], 1)
                    dve.wait_ge(s["band_root"], i + 1)
                    dve.reciprocal(rstd[:, ring:ring + 1], rstd[:, ring:ring + 1]).then_inc(s["band_out"], 1)
                    dve.wait_ge(s["band_out"], c + 4)
                    dve.wait_ge(s["band_xb"], i + 1)
                    dve.scalar_tensor_tensor(x_sb[:, i, :], band_tmp[:, q3, :], rstd[:, ring:ring + 1], x_sb[:, i, :],
                                             ALU.mult, ALU.add).then_inc(s["band_out"], 1)
                if (i := tile_at(t, 0, NT)) is not None:
                    if some(i - 1):
                        dve.wait_ge(s["band_xT_ps"], i - 1)
                    norm_apply(dve, i, r % 2, x_sb[:, i, :], xin[:, r % 2, :], s["band_ln"], 4 * i, s["band_ln_root"])
                if (i := tile_at(t, 1, NT)) is not None:
                    q = (r - 1) % 4
                    dve.wait_ge(s["band_qkv_ps"], i + 1)
                    dve.tensor_tensor(band_qk[:, q, :, :], bank(2 + q % 2).rearrange("p (f t) -> p f t", f=4),
                                      bqk_col[:, :].unsqueeze(2).broadcast_to([P, 4, P]), ALU.add).then_inc(s["band_qkv"], 1)
                    dve.tensor_tensor(band_v[:, q, :], bank(4 + q % 2)[:, 0:C], band_rows[:, 0, :],
                                      ALU.add).then_inc(s["band_qkv"], 1)

            ticks(dve, NT, 3, tick)

        def band_gpsimd(pool):
            pool.wait_ge(s["ld_band"], 16 * 5)

            def tick(t, r):
                if (i := tile_at(t, 1, NT)) is not None:
                    pool.wait_ge(s["band_ln"], 4 * i + 4)
                    pool.tensor_tensor(x_sb[:, i, :], x_sb[:, i, :], band_rows[:, 2, :], ALU.add).then_inc(s["band_xb"], 1)

            ticks(pool, NT, 1, tick)

        def weights_tensor(pe):
            pe.wait_ge(s["ld_xw"], 16 * 4)
            pe.wait_ge(s["band_xT"], NT)
            pe.wait_ge(s["band_qkv"], 2 * NT)
            for w in range(4):
                for k in range(KC):
                    for o in range(KC):
                        last = pe.transpose(bank(w)[:, k * C + o * P:k * C + (o + 1) * P],
                                            w_xraw[:, w, o, k * P:(k + 1) * P], ident[:, :])
                last.then_inc(s["xw_ps"], 1)

        def weights_scalar(act):
            for w, dest in enumerate((w_xq[:, :, :], w_xkv[:, :, 0:C], w_xkv[:, :, C:2 * C], w_xo[:, :, :])):
                act.wait_ge(s["xw_ps"], w + 1)
                act.activation(dest, bank(w).rearrange("p (k n) -> p k n", k=KC), ACT.Copy).then_inc(s["xw"], 1)

        HEAD = 6

        class Stage:
            def __init__(self, name, tiles, weights, width, bias, has_q, has_kv, front=None, loaded=None):
                self.name, self.tiles, self.weights, self.width = name, tiles, weights, width
                self.bias, self.has_q, self.has_kv, self.front, self.loaded = bias, has_q, has_kv, front, loaded
                self.f = 1 if front else 0
                self.s = {n: ctx.enter_context(nc.semaphore(f"{name}_{n}")) for n in (
                    "in0", "in1", "ln", "root", "xT_ps", "xT", "proj", "sum", "hi", "split", "copy", "kT", "kop",
                    "at", "aT_ps", "aT", "o_ps", "kept", "res", "res_bias")}

            def rows(self, t):
                return CTX_LAST if self.loaded and isinstance(t, int) and t == NCT - 1 else P

        qk32 = carve(p_arena, 1024, 2, 2 * C)
        k_tok = carve(p_arena, 2048, 2, H * SLOT // 2)
        k_tok = k_tok.rearrange("p a b -> p (a b)").bitcast(fp16).rearrange("p (a h s) -> p a h s", h=H, s=SLOT)
        at_in = carve(p_arena, 3072, 2, C)
        aT = carve(p_arena, 3584, 2, KC, P)

        def stage_tensor(pe, st):
            z, f, n = st.s, st.f, st.tiles

            def tick(t, r):
                if st.has_kv and (i := tile_at(t, f + 3, n)) is not None:
                    q, m = (r - f - 3) % 2, st.rows(i)
                    pe.wait_ge(z["split"], i + 1)
                    pe.wait_ge(z["copy"], i + 1)
                    if some(i - 1):
                        pe.wait_ge(z["kop"], i - 1)
                    for pair in range(H // 2):
                        last = pe.transpose(bank(6 + q).bitcast(fp16)[:, pair * P:pair * P + m],
                                            k_tok[0:m, q, 2 * pair:2 * pair + 2, :].rearrange("p h s -> p (h s)"),
                                            ident16[0:m, 0:m])
                    last.then_inc(z["kT"], 1)
                if (i := tile_at(t, f + 2, n)) is not None:
                    q, m = (r - f - 2) % 2, st.rows(i)
                    pe.wait_ge(z["xT"], i + 1)
                    if some(i - 1):
                        pe.wait_ge(z["sum"], i - 1)
                    if some(i):
                        pe.wait_ge(z["split"], i)
                    for at in range(0, st.width, 512):
                        w = min(512, st.width - at)
                        dest = bank(3 + q) if at == 0 else bank(5)
                        for k in range(KC):
                            last = pe.matmul(dest[0:m, 0:w], xT[:, q, k, 0:m], st.weights[:, k, at:at + w],
                                             start=k == 0, stop=k == KC - 1)
                    last.then_inc(z["proj"], 1)
                if (i := tile_at(t, f + 1, n)) is not None:
                    q, m = (r - f - 1) % 2, st.rows(i)
                    if st.loaded:
                        pe.wait_ge(z[f"in{q}"], 16 * half(i, r - f - 1) + 16)
                    else:
                        pe.wait_ge(z["ln"], 4 * i + 4)
                    if some(i):
                        pe.wait_ge(z["xT"], i)
                    for k in range(KC):
                        last = pe.transpose(bank(2)[:, k * P:k * P + m], xin[0:m, q, k * P:(k + 1) * P], ident[0:m, 0:m])
                    last.then_inc(z["xT_ps"], 1)
                if st.front and (i := tile_at(t, 1, n)) is not None:
                    pe.wait_ge(z["aT"], i + 1)
                    if some(i):
                        pe.wait_ge(z["res"], i)
                    for k in range(KC):
                        last = pe.matmul(bank(1)[:, 0:C], aT[:, (r - 1) % 2, k, :], st.front[:, k, :],
                                         start=k == 0, stop=k == KC - 1)
                    last.then_inc(z["o_ps"], 1)
                if st.front and (i := tile_at(t, 0, n)) is not None:
                    pe.wait_ge(z["at"], i + 1)
                    if some(i):
                        pe.wait_ge(z["aT"], i)
                    for k in range(KC):
                        last = pe.transpose(bank(0)[:, k * P:(k + 1) * P], at_in[:, r % 2, k * P:(k + 1) * P], ident[:, :])
                    last.then_inc(z["aT_ps"], 1)

            ticks(pe, n, f + 3, tick, HEAD, 2)

        def stage_scalar(act, st):
            z, f, n = st.s, st.f, st.tiles

            def tick(t, r):
                if st.has_kv and (i := tile_at(t, f + 3, n)) is not None:
                    m = st.rows(i)
                    act.wait_ge(z["kT"], i + 1)
                    act.activation(k_op[:, :, bass.ds(i * P, m)],
                                   bank(6 + (r - f - 3) % 2).bitcast(fp16).rearrange("p (h t) -> p h t", t=P)[:, :, 0:m],
                                   ACT.Copy).then_inc(z["kop"], 1)
                if (i := tile_at(t, f + 1, n)) is not None:
                    q, m = (r - f - 1) % 2, st.rows(i)
                    act.wait_ge(z["xT_ps"], i + 1)
                    if some(i - 1):
                        act.wait_ge(z["proj"], i - 1)
                    act.activation(xT[:, q, :, 0:m], bank(2)[:, 0:C].rearrange("p (k t) -> p k t", k=KC)[:, :, 0:m],
                                   ACT.Copy).then_inc(z["xT"], 1)
                if (i := tile_at(t, f + 2, n)) is not None:
                    q, m = (r - f - 2) % 2, st.rows(i)
                    act.wait_ge(z["hi"], i + 1)
                    if st.has_q:
                        last = act.activation(q_tok[0:m, i, :, D:2 * D], q_tok[0:m, i, :, 0:D], ACT.Copy)
                    if st.has_kv:
                        last = act.activation(k_tok[0:m, q, :, 2 * D:3 * D], k_tok[0:m, q, :, 0:D], ACT.Copy)
                    last.then_inc(z["copy"], 1)
                if st.front and (i := tile_at(t, f + 1, n)) is not None:
                    act.activation(src_sb[:, i, :], xin[:, (r - f - 1) % 2, :], ACT.Copy).then_inc(z["kept"], 1)
                if not st.loaded and (i := tile_at(t, f, n)) is not None:
                    norm_root(act, (r - f) % 2, z["ln"], 4 * i, z["root"])
                if st.front and (i := tile_at(t, 0, n)) is not None:
                    act.wait_ge(z["aT_ps"], i + 1)
                    if some(i - 1):
                        act.wait_ge(z["o_ps"], i - 1)
                    act.activation(aT[:, r % 2, :, :], bank(0)[:, 0:C].rearrange("p (k t) -> p k t", k=KC),
                                   ACT.Copy).then_inc(z["aT"], 1)

            ticks(act, n, f + 3, tick, HEAD, 2)

        def stage_vector(dve, st):
            z, f, n = st.s, st.f, st.tiles
            ck = C if st.has_q else 0
            first = C * (st.has_q + st.has_kv)

            def tick(t, r):
                if st.front and (i := tile_at(t, f, n)) is not None:
                    dve.wait_ge(z["o_ps"], i + 1)
                    dve.wait_ge(z["res_bias"], i + 1)
                    dve.tensor_tensor(x_sb[:, i, :], bank(1)[:, 0:C], x_sb[:, i, :], ALU.add).then_inc(z["res"], 1)
                    dve.wait_ge(z["res"], i + 1)
                if (i := tile_at(t, f + 2, n)) is not None:
                    q, m = (r - f - 2) % 2, st.rows(i)
                    dve.wait_ge(z["proj"], i + 1)
                    dve.tensor_tensor(qk32[0:m, q, 0:first], bank(3 + q)[0:m, 0:first], row(st.bias, first // C)[0:m, :],
                                      ALU.add).then_inc(z["sum"], 1)
                if not st.loaded and (b := tile_at(t, f, n)) is not None:
                    dve.bn_stats(stat6[:, (r - f) % 2, :], x_sb[:, b, :]).then_inc(z["ln"], 1)
                    dve.wait_ge(z["ln"], 4 * b + 1)
                if i is not None:
                    if st.has_kv:
                        v_ps = bank(5)[0:m, 0:C] if first == 2 * C else bank(3 + q)[0:m, C:2 * C]
                        dve.tensor_tensor(v_aug[0:m, i, :, 0:D], v_ps.rearrange("p (h d) -> p h d", h=H),
                                          row(st.bias, 3)[0:m, first:first + C].rearrange("p (h d) -> p h d", h=H)
                                          if st.has_q else row(st.bias, 2)[0:m, C:2 * C].rearrange("p (h d) -> p h d", h=H),
                                          ALU.add)
                    dve.wait_ge(z["sum"], i + 1)
                    parts = []
                    if st.has_q:
                        parts.append((q_tok[0:m, i, :, :], 2 * D, qk32[0:m, q, 0:C].rearrange("p (h d) -> p h d", h=H)))
                    if st.has_kv:
                        if some(i - 1):
                            dve.wait_ge(z["kT"], i - 1)
                        parts.append((k_tok[0:m, q, :, :], D, qk32[0:m, q, ck:ck + C].rearrange("p (h d) -> p h d", h=H)))
                    for op, _, full in parts:
                        last = dve.tensor_copy(op[:, :, 0:D], full)
                    last.then_inc(z["hi"], 1)
                    dve.wait_ge(z["hi"], i + 1)
                    for op, lo, full in parts:
                        last = dve.tensor_tensor(op[:, :, lo:lo + D], full, op[:, :, 0:D], ALU.subtract)
                    last.then_inc(z["split"], 1)
                if not st.loaded and (i := tile_at(t, f, n)) is not None:
                    norm_aggr(dve, (r - f) % 2, z["ln"])
                    if some(i - 1):
                        dve.wait_ge(z["xT_ps"], i - 1)
                        if st.front:
                            dve.wait_ge(z["kept"], i - 1)
                    norm_apply(dve, i, (r - f) % 2, x_sb[:, i, :], xin[:, (r - f) % 2, :], z["ln"], 4 * i, z["root"])

            ticks(dve, n, f + 3, tick, HEAD, 2)

        def stage_gpsimd(pool, st):
            z, f, n = st.s, st.f, st.tiles

            def tick(t, r):
                if st.front and (i := tile_at(t, 0, n)) is not None:
                    if some(i - 1):
                        pool.wait_ge(z["aT_ps"], i - 1)
                    pool.tensor_tensor(x_sb[:, i, :], x_sb[:, i, :], row("xattn_bo"), ALU.add).then_inc(z["res_bias"], 1)
                    pool.tensor_copy(at_in[:, r % 2, :], attn_tok[:, i, :]).then_inc(z["at"], 1)

            ticks(pool, n, f + 3, tick, HEAD, 2)

        def half(i, r):
            return i // 2 if isinstance(i, int) else (i - r % 2) // 2

        def stage_sync(sp, st):
            z, n = st.s, st.tiles

            def tick(t, r):
                m = st.rows(t)
                if some(t - 1):
                    sp.wait_ge(z["xT_ps"], t - 1)
                sp.dma_start(xin[0:m, r % 2, :], st.loaded[bass.ds(t * P, m), :]).then_inc(z[f"in{r % 2}"], 16)

            ticks(sp, n, 0, tick, HEAD, 2)

        ctx_kv = Stage("ctx", NCT, w_xkv, 2 * C, "xattn_bk", has_q=False, has_kv=True, loaded=io["ctx_1024"][0])
        cross_q = Stage("xq", NT, w_xq, C, "xattn_bq", has_q=True, has_kv=False)
        self_qkv = Stage("self", NT, w_fqkv, 3 * C, "ffn_bq", has_q=True, has_kv=True, front=w_xo)

        JOBS = NG * H // 2
        UNITS = 16
        SCALE = float(D) ** -0.5

        q_max = (sb("q_max", [P, 2, QG], fp16)[:, :, :],
                 w_xq[:, :, :].rearrange("p k n -> p (k n)").bitcast(fp16).rearrange("p (a q) -> p a q", a=2))
        q_exp = sb("q_exp", [P, 2, 2, QG], fp16)
        neg_max = sb("neg_max", [P, 2, GRP, 2, 4])
        o_sb = sb("o_sb", [P, QG])
        rden = sb("rden", [P, GRP * 4])
        prob = carve(p_arena, 0, 4, 1024)
        max_bank, o_bank, misc = (bank(4), bank(5)), bank(6), bank(7)
        q_op = q_tok.rearrange("p t h s -> p t (h s)")

        class Attention:
            def __init__(self, name, keys):
                self.tiles = [(i, min(P, keys - i * P)) for i in range(-(-keys // P))]
                self.n = len(self.tiles)
                width = -(-keys // 4)
                self.chunks = [(a, min(width, keys - a)) for a in range(0, keys, width)]
                self.s = {n: ctx.enter_context(nc.semaphore(f"{name}_{n}")) for n in (
                    "q_ps", "q_op", "max_ps", "max", "job", "score", "exp", "pv", "o_sb", "oT", "recip", "out")}
                self.until = [2 * UNITS * (i + 1) // self.n for i in range(self.n)]
                self.turn = next(i for i, u in enumerate(self.until) if u >= UNITS)

            def builds_at(self, h):
                return {1: ("qb", 2 * h + 2), 4: ("qa", 2 * h + 4),
                        self.turn + 1: ("qb", 2 * h + 3), self.turn + 3: ("qa", 2 * h + 5)}

            def maxima_at(self, h, kt, quarter=None):
                first, last = (4 * kt, 4 * kt + 4) if quarter is None else (4 * kt + quarter, 4 * kt + quarter + 1)
                total = 2 * 2 * UNITS
                return [(2 * h + 3 + i // (2 * UNITS), i // 2 % UNITS, i % 2)
                        for i in range(total * first // (4 * self.n), total * last // (4 * self.n))]

            def prob_at(self, h, kt, p):
                return (2 * self.n * h + 2 * kt + p) % 4

        def build_count(kind, n):
            if isinstance(n, int) and (kind, n) in (("qa", 0), ("qb", JOBS - 1)):
                return 1 if n == 0 else 2 * JOBS
            return 2 * n if kind == "qa" else 2 * n + 3

        def exists(n):
            return not isinstance(n, int) or n < JOBS

        def groups(eng, group):
            with eng.Fori(0, NG - 1) as g:
                group(g)
            group(NG - 1)

        FIRST_BUILDS = [("qa", 0), ("qa", 1), ("qb", 0), ("qa", 2), ("qb", 1), ("qa", 3)]

        def attention_tensor(pe, at):
            z = at.s

            def build(kind, g, r):
                n, pair, tile0 = 8 * g + r, r % 8, 4 * g + 4 * (r // 8)
                if kind == "qb":
                    pe.wait_ge(z["job"], n + 1)
                for q in range(GRP):
                    last = pe.matmul(misc[:, q * P:(q + 1) * P], q_op[:, tile0 + q, pair * P:(pair + 1) * P], ident16[:, :],
                                     start=True, stop=True)
                last.then_inc(z["q_ps"], 1)

            def maxima(g, r, u, j):
                n, pair, (k0, width) = 8 * g + r, r % 8, at.chunks[u % 4]
                if u == 0 and j == 0:
                    pe.wait_ge(z["q_op"], build_count("qa", n))
                before = 2 * (UNITS * n + u) + j - 1
                if some(before):
                    pe.wait_ge(z["max"], before)
                pe.matmul(max_bank[j][:, 0:width], q_max[j][:, r % 2, (u // 4) * P:(u // 4 + 1) * P],
                          k_op[:, pair, k0:k0 + width], start=True, stop=True).then_inc(z["max_ps"], 1)

            def sums(g, h, kt, part):
                m, it, whole = at.tiles[kt][1], 4 * g + h, kt in (0, at.n - 1)
                if whole and part == 0:
                    return
                if part == 0 or whole:
                    pe.wait_ge(z["exp"], 2 * at.n * it + 2 * kt + 2)
                if kt == 0 and h:
                    pe.wait_ge(z["o_sb"], it)
                q0, q1 = (0, QG) if whole else (part * QG // 2, (part + 1) * QG // 2)
                for hh in range(4):
                    last = pe.matmul(o_bank[32 * hh:32 * hh + 32, q0:q1], v_aug[0:m, kt, 4 * h + hh, :],
                                     prob[0:m, at.prob_at(h, kt, hh // 2), (hh % 2) * QG + q0:(hh % 2) * QG + q1],
                                     start=kt == 0, stop=kt == at.n - 1, tile_position=(0, 32 * hh))
                if part == 1:
                    last.then_inc(z["pv"], 1)

            def turn_sums(g, h):
                pe.wait_ge(z["o_sb"], 4 * g + h + 1)
                for q in range(GRP):
                    last = pe.transpose(misc[:, q * P:(q + 1) * P], o_sb[:, q * P:(q + 1) * P], ident[:, :])
                last.then_inc(z["oT"], 1)

            for i, (kind, r) in enumerate(FIRST_BUILDS):
                if i:
                    pe.wait_ge(z["q_op"], i)
                build(kind, 0, r)
                if i in (1, 3, 5):
                    for u in range(0 if i == 1 else 2, UNITS):
                        for j in range(2):
                            maxima(0, i // 2, u, j)
                    for u in range(0, 2 if i < 5 else 0):
                        for j in range(2):
                            maxima(0, i // 2 + 1, u, j)
            pe.wait_ge(z["q_op"], len(FIRST_BUILDS))

            def group(g):
                free = (z["out"], 4 * g + 1)
                for h in range(4):
                    it = 4 * g + h
                    for kt, m in at.tiles:
                        for quarter in range(4):
                            p = quarter // 2
                            if quarter % 2 == 0:
                                if kt == 0:
                                    pe.wait_ge(z["q_op"], build_count("qb", 8 * g + 2 * h + p))
                                if kt or h:
                                    pe.wait_ge(z["exp"], 2 * at.n * it + 2 * kt + p - 1)
                                for j in range(2):
                                    last = pe.matmul(s_pair[p][0:m, j * QG:(j + 1) * QG],
                                                     k_op[SLOT * j:SLOT * (j + 1), 2 * h + p, kt * P:kt * P + m],
                                                     q_exp[SLOT * j:SLOT * (j + 1), h % 2, p, :],
                                                     start=True, stop=True, tile_position=(SLOT * j, 0))
                                last.then_inc(z["score"], 1)
                            elif kt:
                                sums(g, h, kt - 1, p)
                            elif h:
                                sums(g, h - 1, at.n - 1, p)
                            for r, u, j in at.maxima_at(h, kt, quarter):
                                if exists(8 * g + r):
                                    maxima(g, r, u, j)
                        if kt in at.builds_at(h):
                            kind, r = at.builds_at(h)[kt]
                            if exists(8 * g + r):
                                pe.wait_ge(*free)
                                build(kind, g, r)
                                free = (z["q_op"], build_count(kind, 8 * g + r))
                        if kt == 2 and h:
                            pe.wait_ge(*free)
                            turn_sums(g, h - 1)
                            free = (z["out"], it + 1)
                for part in range(2):
                    sums(g, 3, at.n - 1, part)
                pe.wait_ge(*free)
                turn_sums(g, 3)

            groups(pe, group)

        def attention_scalar(act, at):
            z = at.s

            def read_build(kind, g, r):
                act.wait_ge(z["q_ps"], build_count(kind, 8 * g + r))
                if kind == "qa":
                    for j in range(2):
                        rows = slice(SLOT * j, SLOT * (j + 1))
                        last = act.activation(q_max[j][rows, r % 2, :], misc[rows, :], ACT.Copy)
                else:
                    last = act.activation(q_exp[:, (r // 2) % 2, r % 2, :], misc, ACT.Copy)
                last.then_inc(z["q_op"], 1)

            def read_sums(g, h):
                act.wait_ge(z["pv"], at.n * (4 * g + h + 1))
                act.activation(o_sb[:, :], o_bank, ACT.Copy).then_inc(z["o_sb"], 1)

            for kind, r in FIRST_BUILDS:
                read_build(kind, 0, r)

            def group(g):
                for h in range(4):
                    it = 4 * g + h
                    for kt, m in at.tiles:
                        for p in range(2):
                            act.wait_ge(z["score"], 2 * at.n * it + 2 * kt + p + 1)
                            if p == 0 and (kt >= 2 or h):
                                act.wait_ge(z["pv"], at.n * it + kt - 1)
                            act.activation(prob[0:m, at.prob_at(h, kt, p), :], s_pair[p][0:m, :], ACT.Exp,
                                           scale=SCALE).then_inc(z["exp"], 1)
                        if kt in at.builds_at(h):
                            kind, r = at.builds_at(h)[kt]
                            if exists(8 * g + r):
                                read_build(kind, g, r)
                        if kt == 0 and h:
                            read_sums(g, h - 1)
                read_sums(g, 3)

            groups(act, group)

        def attention_vector(dve, at):
            z = at.s
            dve.memset(rden[:, :], 1.0).then_inc(z["out"], 1)

            def maxima(g, r, u, j):
                n, (_, width) = 8 * g + r, at.chunks[u % 4]
                dve.wait_ge(z["max_ps"], 2 * (UNITS * n + u) + j + 1)
                dve.tensor_reduce(neg_max[:, r % 2, u // 4, j, u % 4:u % 4 + 1], max_bank[j][:, 0:width], AX.X, ALU.max,
                                  negate=True).then_inc(z["max"], 1)
                if u == UNITS - 1 and j == 1:
                    dve.wait_ge(z["max"], 2 * UNITS * (n + 1))
                    dve.tensor_reduce(q_tok[:, bass.ds(4 * g + 4 * (r // 8), GRP), 2 * (r % 8):2 * (r % 8) + 2, MROW],
                                      neg_max[:, r % 2, :, :, :], AX.X, ALU.min).then_inc(z["job"], 1)

            def result(g, h):
                it = 4 * g + h
                sums = misc.rearrange("p (q h d) -> p q h d", q=GRP, h=4)
                dve.wait_ge(z["oT"], it + 1)
                dve.reciprocal(rden[:, :].rearrange("p (q h) -> p q h", h=4), sums[:, :, :, D]).then_inc(z["recip"], 1)
                dve.wait_ge(z["recip"], it + 1)
                dve.tensor_tensor(attn_tok[:, bass.ds(4 * g, GRP), h * 4 * D:(h + 1) * 4 * D].rearrange("p q (h d) -> p q h d", h=4),
                                  sums[:, :, :, 0:D],
                                  rden[:, :].rearrange("p (q h) -> p q h", h=4).unsqueeze(3).broadcast_to([P, GRP, 4, D]),
                                  ALU.mult).then_inc(z["out"], 1)

            for r in range(3):
                for u in range(UNITS):
                    for j in range(2):
                        maxima(0, r, u, j)

            def group(g):
                for h in range(4):
                    for kt, _ in at.tiles:
                        for r, u, j in at.maxima_at(h, kt):
                            if exists(8 * g + r):
                                maxima(g, r, u, j)
                        if kt == 2 and h:
                            result(g, h - 1)
                result(g, 3)

            groups(dve, group)

        cross = Attention("cross", S_CTX)
        selfa = Attention("selfa", T)

        post = sems(*("post_" + n for n in ("at", "bias", "aT_ps", "aT", "o_ps", "ln", "root", "norm", "xT_ps", "x3T", "kept", "apply")))
        x3T = carve(q_arena, 0, KC, T)
        post_sum = band_tmp

        def post_gpsimd(pool):
            pool.wait_ge(selfa.s["out"], 4 * NG + 1)

            def tick(t, r):
                if (i := tile_at(t, 0, NT)) is not None:
                    if some(i - 1):
                        pool.wait_ge(post["post_aT_ps"], i - 1)
                    pool.tensor_tensor(src_sb[:, i, :], src_sb[:, i, :], row("ffn_bo"), ALU.add).then_inc(post["post_bias"], 1)
                    pool.tensor_copy(at_in[:, r % 2, :], attn_tok[:, i, :]).then_inc(post["post_at"], 1)

            ticks(pool, NT, 3, tick, HEAD, 2)
            pool.wait_ge(self_qkv.s["ln"], 4 * NT)
            pool.tensor_tensor(x_sb[:, :, :], x_sb[:, :, :], row("ffn_ln2_b").unsqueeze(1).broadcast_to([P, NT, C]),
                               ALU.add).then_inc(moe["moe_xb"], 1)

        def post_tensor(pe):
            z = post

            def tick(t, r):
                if (i := tile_at(t, 3, NT)) is not None:
                    pe.wait_ge(z["post_norm"], i + 1)
                    if some(i):
                        pe.wait_ge(z["post_x3T"], i)
                    for k in range(KC):
                        last = pe.transpose(bank(2)[:, k * P:(k + 1) * P], xin[:, (r - 3) % 2, k * P:(k + 1) * P], ident[:, :])
                    last.then_inc(z["post_xT_ps"], 1)
                if (i := tile_at(t, 1, NT)) is not None:
                    pe.wait_ge(z["post_aT"], i + 1)
                    if some(i):
                        pe.wait_ge(z["post_ln"], 3 * i - 2)
                    for k in range(KC):
                        last = pe.matmul(bank(1)[:, 0:C], aT[:, (r - 1) % 2, k, :], w_fo[:, k, :], start=k == 0, stop=k == KC - 1)
                    last.then_inc(z["post_o_ps"], 1)
                if (i := tile_at(t, 0, NT)) is not None:
                    pe.wait_ge(z["post_at"], i + 1)
                    if some(i):
                        pe.wait_ge(z["post_aT"], i)
                    for k in range(KC):
                        last = pe.transpose(bank(0)[:, k * P:(k + 1) * P], at_in[:, r % 2, k * P:(k + 1) * P], ident[:, :])
                    last.then_inc(z["post_aT_ps"], 1)

            ticks(pe, NT, 3, tick, HEAD, 2)

        def post_scalar(act):
            z = post

            def tick(t, r):
                if (i := tile_at(t, 3, NT)) is not None:
                    act.wait_ge(z["post_xT_ps"], i + 1)
                    act.activation(x3T[:, :, bass.ds(i * P, P)], bank(2)[:, 0:C].rearrange("p (k t) -> p k t", k=KC),
                                   ACT.Copy).then_inc(z["post_x3T"], 1)
                    act.activation(src_sb[:, i, :], xin[:, (r - 3) % 2, :], ACT.Copy).then_inc(z["post_kept"], 1)
                if (i := tile_at(t, 0, NT)) is not None:
                    act.wait_ge(z["post_aT_ps"], i + 1)
                    if some(i - 1):
                        act.wait_ge(z["post_o_ps"], i - 1)
                    act.activation(aT[:, r % 2, :, :], bank(0)[:, 0:C].rearrange("p (k t) -> p k t", k=KC),
                                   ACT.Copy).then_inc(z["post_aT"], 1)
                if (i := tile_at(t, 1, NT)) is not None:
                    q = (r - 1) % 2
                    act.wait_ge(z["post_ln"], 3 * i + 3)
                    act.activation(rstd[:, q:q + 1], mean_var[:, q, 1:2], ACT.Sqrt, bias=eps_col[:, :]).then_inc(z["post_root"], 1)

            ticks(act, NT, 3, tick, HEAD, 2)

        def post_vector(dve):
            z = post

            def tick(t, r):
                if (i := tile_at(t, 1, NT)) is not None:
                    q = (r - 1) % 2
                    dve.wait_ge(z["post_o_ps"], i + 1)
                    dve.wait_ge(z["post_bias"], i + 1)
                    dve.tensor_tensor(post_sum[:, q, :], bank(1)[:, 0:C], src_sb[:, i, :], ALU.add).then_inc(z["post_ln"], 1)
                    dve.wait_ge(z["post_ln"], 3 * i + 1)
                    dve.bn_stats(stat6[:, q, :], post_sum[:, q, :]).then_inc(z["post_ln"], 1)
                    dve.wait_ge(z["post_ln"], 3 * i + 2)
                b = tile_at(t, 2, NT)
                p = (r - 2) % 2
                if b is not None:
                    dve.wait_ge(z["post_root"], b + 1)
                    dve.reciprocal(rstd[:, p:p + 1], rstd[:, p:p + 1]).then_inc(z["post_apply"], 1)
                if i is not None:
                    dve.bn_aggr(mean_var[:, q, :], stat6[:, q, :]).then_inc(z["post_ln"], 1)
                if b is not None:
                    dve.scalar_tensor_tensor(post_sum[:, p, :], post_sum[:, p, :], mean_var[:, p, 0:1], row("ffn_ln1_g"),
                                             ALU.subtract, ALU.mult).then_inc(z["post_apply"], 1)
                    dve.wait_ge(z["post_apply"], 2 * b + 2)
                    if some(b - 1):
                        dve.wait_ge(z["post_xT_ps"], b - 1)
                        dve.wait_ge(z["post_kept"], b - 1)
                    dve.scalar_tensor_tensor(xin[:, p, :], post_sum[:, p, :], rstd[:, p:p + 1], row("ffn_ln1_b"),
                                             ALU.mult, ALU.add).then_inc(z["post_norm"], 1)

            ticks(dve, NT, 3, tick, HEAD, 2)

        moe = sems(*("moe_" + n for n in ("zero_set", "zeroed", "weights", "consts", "const_f", "key_ps", "route", "rank_ps", "count_ps",
                                          "sorted", "in0", "in1", "xT_ps", "xT", "w1", "w2", "b1", "h_ps", "relu", "y_ps", "y",
                                          "stored0", "stored1", "tokens0", "tokens1", "tokens2", "tokens3", "ln", "root", "apply", "xb", "out", "out_stored")))
        NS = NT + E - 1
        x_sorted = nc.dram_tensor("x_sorted", [NS * P, C], fp32).ap()
        y_sorted = nc.dram_tensor("y_sorted", [NS * P, C], fp32).ap()
        w1_sb = k_op[:, :, :].rearrange("p a b -> p (a b)").bitcast(fp32)
        w2_sb = v_aug[:, :, :, :].rearrange("p t h d -> p (t h d)")
        WIDE = KC * F
        w1_use = carve(q_arena, 0, KC, F)
        w2_use = carve(q_arena, WIDE, FC, C)
        hidden = carve(q_arena, 2 * WIDE, 2, FC, P)
        xs_in = carve(q_arena, 2 * WIDE + 2 * F, 2, C)
        xsT = carve(q_arena, 2 * WIDE + 2 * F + 2 * C, 2, KC, P)
        y_out = carve(q_arena, 2 * WIDE + 2 * F + 4 * C, 2, C)
        b2_rows = w_fqkv[:, :, :].rearrange("p k n -> p (k n)")[:, 0:E * C]
        b2_use = w_fqkv[:, :, :].rearrange("p k n -> p (k n)")[:, E * C:(E + 1) * C]
        y_tok = carve(p_arena, 0, NT, C)
        moe_sum = w_xkv[:, :, :].rearrange("p k n -> p (k n)").rearrange("p (q c) -> p q c", c=C)
        out_sb = attn_tok
        before_token, ones = band_mask[:, 0:P], band_mask[:, P:2 * P]
        cut = [1024]

        def small(*shape):
            n = 1
            for k in shape:
                n *= k
            cut[0] += n
            return carve(p_arena, cut[0] - n, *shape)

        key, floor_f, above = small(NT), small(NT), small(NT)
        key_int = small(NT).bitcast(i32)
        ids, ids_f = small(NS + 1).bitcast(i32), small(NS + 1)
        chosen, place = small(E, NT), small(E, NT)
        counts, full, first = small(E), small(E, NT), small(E)
        tiles_of, place_f = small(E), small(NT)
        after, slot_f = small(NS, E), small(NS)
        slot_expert = small(NS).bitcast(i32)
        key_ps, place_ps, count_ps = bank(4)[:, 0:NT], bank(5)[:, 0:E * NT], bank(6)[:, 0:E * NT]

        def moe_sync(sp):
            z = moe
            sp.wait_ge(selfa.s["out"], 4 * NG + 1)
            sp.dma_start(w1_sb.rearrange("p (e k f) -> p e k f", e=E, k=KC),
                         io["L0_ffn_W1"].rearrange("e (k p) f -> p e k f", p=P)).then_inc(z["moe_weights"], 16)
            sp.dma_start(w2_sb.rearrange("p (e c n) -> p e c n", e=E, c=FC),
                         io["L0_ffn_W2"].rearrange("e (c p) n -> p e c n", p=P)).then_inc(z["moe_weights"], 16)
            sp.dma_start(b2_rows, io["L0_ffn_b2"].rearrange("e n -> (e n)").partition_broadcast(P)).then_inc(z["moe_weights"], 16)
            sp.wait_ge(z["moe_sorted"], 16 * NT)

            def tick(t, r):
                if (i := tile_at(t, 0, NS)) is not None:
                    if some(i - 1):
                        sp.wait_ge(z["moe_xT_ps"], i - 1)
                    sp.dma_start(xs_in[:, r % 2, :], x_sorted[bass.ds(i * P, P), :]).then_inc(z[f"moe_in{r % 2}"], 16)
                if (i := tile_at(t, 3, NS)) is not None:
                    sp.wait_ge(z["moe_y"], i + 1)
                    sp.dma_start(y_sorted[bass.ds(i * P, P), :], y_out[:, (r - 3) % 2, :]).then_inc(z[f"moe_stored{(r - 3) % 2}"], 16)

            ticks(sp, NS, 3, tick, HEAD, 2)
            for g in range(NG):
                sp.wait_ge(z["moe_out"], GRP * g + GRP)
                sp.dma_start(out_view[:, GRP * g:GRP * (g + 1), :], out_sb[:, GRP * g:GRP * (g + 1), :]).then_inc(z["moe_out_stored"], 16)
            sp.wait_ge(z["moe_out_stored"], 16 * NG)

        def moe_gpsimd(pool):
            z = moe
            pool.iota(ids, pattern=[[1, NS + 1]], base=0, channel_multiplier=0).then_inc(z["moe_consts"], 1)
            pool.memset(before_token, 1.0).then_inc(z["moe_consts"], 1)
            pool.memset(ones, 1.0).then_inc(z["moe_consts"], 1)
            pool.wait_ge(z["moe_consts"], 3)
            pool.affine_select(out=before_token, in_=before_token, compare_op=ALU.is_ge, fill=0.0, base=-1,
                               pattern=[[1, P]], channel_multiplier=-1).then_inc(z["moe_consts"], 1)
            pool.wait_ge(z["moe_zeroed"], 16 * 2)
            pool.wait_ge(post["post_kept"], NT)
            pool.wait_ge(z["moe_route"], ROUTED)
            for t in range(NT):
                pool.indirect_dma_start(out=x_sorted, out_offset=bass.IndirectOffsetOnAxis(ap=dest[:, t:t + 1], axis=0),
                                        in_=src_sb[:, t, :], in_offset=None).then_inc(z["moe_sorted"], 16)
            pool.wait_ge(z["moe_stored0"], 16 * (NS - NS // 2))
            pool.wait_ge(z["moe_stored1"], 16 * (NS // 2))
            for t in range(NT):
                pool.indirect_dma_start(out=y_tok[:, t, :], out_offset=None, in_=y_sorted,
                                        in_offset=bass.IndirectOffsetOnAxis(ap=dest[:, t:t + 1], axis=0)).then_inc(z[f"moe_tokens{t // GRP}"], 16)

        def moe_tensor(pe):
            z = moe
            pe.wait_ge(s["ld_small"], 16 * 3)
            pe.wait_ge(post["post_x3T"], NT)
            for t in range(NT):
                for k in range(KC):
                    last = pe.matmul(key_ps[:, t:t + 1], x3T[:, k, t * P:(t + 1) * P], router_col[:, k:k + 1],
                                     start=k == 0, stop=k == KC - 1)
            last.then_inc(z["moe_key_ps"], 1)
            pe.wait_ge(z["moe_consts"], 4)
            pe.wait_ge(z["moe_route"], CHOSEN)
            pe.matmul(count_ps, ones, chosen.rearrange("p e t -> p (e t)"), start=True, stop=True).then_inc(z["moe_count_ps"], 1)
            places = place_ps.rearrange("p (e t) -> p e t", t=NT)
            pe.matmul(places, before_token, chosen, start=True, stop=False)
            for d in range(1, NT):
                last = pe.matmul(places[:, :, d:NT], ones, chosen[:, :, 0:NT - d], start=False, stop=d == NT - 1)
            last.then_inc(z["moe_rank_ps"], 1)
            pe.wait_ge(z["moe_route"], ROUTED)

            def tick(t, r):
                if (i := tile_at(t, 2, NS)) is not None:
                    q = (r - 2) % 2
                    pe.wait_ge(z["moe_xT"], i + 1)
                    pe.wait_ge(z["moe_w1"], i + 1)
                    if some(i - 1):
                        pe.wait_ge(z["moe_relu"], FC * (i - 1))
                    for c in range(FC):
                        for k in range(KC):
                            last = pe.matmul(bank(2 * q + c // 4)[:, (c % 4) * P:(c % 4 + 1) * P], w1_use[:, k, c * P:(c + 1) * P],
                                             xsT[:, q, k, :], start=k == 0, stop=k == KC - 1)
                        last.then_inc(z["moe_h_ps"], 1)
                if (i := tile_at(t, 1, NS)) is not None:
                    q = (r - 1) % 2
                    pe.wait_ge(z[f"moe_in{q}"], 16 * half(i, r - 1) + 16)
                    if some(i):
                        pe.wait_ge(z["moe_xT"], i)
                    for k in range(KC):
                        last = pe.transpose(bank(4)[:, k * P:(k + 1) * P], xs_in[:, q, k * P:(k + 1) * P], ident[:, :])
                    last.then_inc(z["moe_xT_ps"], 1)
                if (i := tile_at(t, 3, NS)) is not None:
                    q = (r - 3) % 2
                    pe.wait_ge(z["moe_relu"], FC * (i + 1))
                    pe.wait_ge(z["moe_w2"], i + 1)
                    if some(i - 1):
                        pe.wait_ge(z["moe_y"], i - 1)
                    for c in range(FC):
                        last = pe.matmul(bank(5 + q)[:, 0:C], hidden[:, q, c, :], w2_use[:, c, :], start=c == 0, stop=c == FC - 1)
                    last.then_inc(z["moe_y_ps"], 1)

            ticks(pe, NS, 3, tick, HEAD, 2)

        def moe_scalar(act):
            z = moe
            act.wait_ge(z["moe_weights"], 16 * 3)
            act.wait_ge(z["moe_route"], ROUTED)

            def tick(t, r):
                if (i := tile_at(t, 2, NS)) is not None:
                    q = (r - 2) % 2
                    act.wait_ge(z["moe_b1"], i + 1)
                    for c in range(FC):
                        if c % 4 == 0:
                            act.wait_ge(z["moe_h_ps"], FC * i + c + 4)
                        act.activation(hidden[:, q, c, :], bank(2 * q + c // 4)[:, (c % 4) * P:(c % 4 + 1) * P], ACT.Relu,
                                       bias=b1_use[:, c:c + 1]).then_inc(z["moe_relu"], 1)
                if (i := tile_at(t, 1, NS)) is not None:
                    e = act.value_load(slot_expert[0:1, bass.ds(i, 1)], min_val=0, max_val=E - 1)
                    act.activation(w1_use.rearrange("p k f -> p (k f)"), w1_sb[:, bass.ds(e * WIDE, WIDE)], ACT.Copy).then_inc(z["moe_w1"], 1)
                    if some(i):
                        act.wait_ge(z["moe_relu"], FC * i)
                    act.activation(b1_use[:, :], b1_col[:, :, :].rearrange("p e c -> p (e c)")[:, bass.ds(e * FC, FC)],
                                   ACT.Copy).then_inc(z["moe_b1"], 1)

            ticks(act, NS, 3, tick, HEAD, 2)
            for t in range(NT):
                act.wait_ge(z["moe_ln"], 3 * t + 3)
                act.activation(rstd[:, t % 4:t % 4 + 1], mean_var[:, t % 4, 1:2], ACT.Sqrt, bias=eps_col[:, :]).then_inc(z["moe_root"], 1)

        ROUTED, CHOSEN = 22, 9

        def moe_vector(dve):
            z = moe
            dve.wait_ge(z["moe_consts"], 1)
            dve.tensor_copy(ids_f, ids).then_inc(z["moe_const_f"], 1)
            dve.memset(first[:, 0:1], 0.0).then_inc(z["moe_const_f"], 1)
            dve.wait_ge(z["moe_const_f"], 2)
            dve.wait_ge(z["moe_key_ps"], 1)
            by_expert = "p (e t) -> p e t"
            spread = lambda v, n: v.unsqueeze(2).broadcast_to([P, v.shape[1], n])
            along = lambda v, n: v.unsqueeze(1).broadcast_to([P, n, v.shape[1]])
            dve.tensor_scalar(key, key_ps, router_col[:, KC:KC + 1], None, ALU.add).then_inc(z["moe_route"], 1)
            dve.wait_ge(z["moe_route"], 1)
            dve.tensor_copy(key_int, key).then_inc(z["moe_route"], 1)
            dve.wait_ge(z["moe_route"], 2)
            dve.tensor_copy(floor_f, key_int).then_inc(z["moe_route"], 1)
            dve.wait_ge(z["moe_route"], 3)
            dve.tensor_tensor(above, floor_f, key, ALU.is_gt).then_inc(z["moe_route"], 1)
            dve.wait_ge(z["moe_route"], 4)
            dve.tensor_tensor(floor_f, floor_f, above, ALU.subtract).then_inc(z["moe_route"], 1)
            dve.wait_ge(z["moe_route"], 5)
            dve.tensor_copy(key_int, floor_f).then_inc(z["moe_route"], 1)
            dve.wait_ge(z["moe_route"], 6)
            dve.tensor_scalar(key_int, key_int, E - 1, None, ALU.bitwise_and).then_inc(z["moe_route"], 1)
            dve.wait_ge(z["moe_route"], 7)
            dve.tensor_copy(key, key_int).then_inc(z["moe_route"], 1)
            dve.wait_ge(z["moe_route"], 8)
            dve.tensor_tensor(chosen, along(key, E), spread(ids_f[:, 0:E], NT), ALU.is_equal).then_inc(z["moe_route"], 1)
            dve.wait_ge(z["moe_count_ps"], 1)
            dve.tensor_reduce(counts, count_ps.rearrange(by_expert, t=NT), AX.X, ALU.add).then_inc(z["moe_route"], 1)
            dve.wait_ge(z["moe_route"], 10)
            dve.scalar_tensor_tensor(full, along(ids_f[:, 0:NT], E), float(P), spread(counts, NT), ALU.mult, ALU.is_lt).then_inc(z["moe_route"], 1)
            dve.wait_ge(z["moe_route"], 11)
            dve.tensor_reduce(tiles_of, full, AX.X, ALU.add).then_inc(z["moe_route"], 1)
            for e in range(1, E):
                dve.wait_ge(z["moe_route"], 11 + e)
                dve.tensor_tensor(first[:, e:e + 1], first[:, e - 1:e], tiles_of[:, e - 1:e], ALU.add).then_inc(z["moe_route"], 1)
            dve.wait_ge(z["moe_route"], 11 + E)
            dve.wait_ge(z["moe_rank_ps"], 1)
            dve.scalar_tensor_tensor(place, spread(first, NT), float(P), place_ps.rearrange(by_expert, t=NT),
                                     ALU.mult, ALU.add).then_inc(z["moe_route"], 1)
            dve.wait_ge(z["moe_route"], 12 + E)
            dve.tensor_tensor(place, place, chosen, ALU.mult).then_inc(z["moe_route"], 1)
            dve.wait_ge(z["moe_route"], 13 + E)
            dve.tensor_reduce(place_f, place.rearrange("p e t -> p t e"), AX.X, ALU.add).then_inc(z["moe_route"], 1)
            dve.wait_ge(z["moe_route"], 14 + E)
            dve.tensor_copy(dest[:, :], place_f).then_inc(z["moe_route"], 1)
            dve.tensor_tensor(after, spread(ids_f[:, 0:NS], E), along(first, NS), ALU.is_ge).then_inc(z["moe_route"], 1)
            dve.wait_ge(z["moe_route"], 16 + E)
            dve.tensor_reduce(slot_f, after[:, :, 1:E], AX.X, ALU.add).then_inc(z["moe_route"], 1)
            dve.wait_ge(z["moe_route"], 17 + E)
            dve.tensor_copy(slot_expert, slot_f).then_inc(z["moe_route"], 1)
            dve.wait_ge(z["moe_weights"], 16 * 3)
            dve.wait_ge(z["moe_route"], ROUTED)

            def tick(t, r):
                if (i := tile_at(t, 1, NS)) is not None:
                    dve.wait_ge(z["moe_xT_ps"], i + 1)
                    dve.tensor_copy(xsT[:, (r - 1) % 2, :, :], bank(4)[:, 0:C].rearrange("p (k t) -> p k t", k=KC)).then_inc(z["moe_xT"], 1)
                if (i := tile_at(t, 3, NS)) is not None:
                    q = (r - 3) % 2
                    dve.wait_ge(z["moe_y_ps"], i + 1)
                    if some(i - 1):
                        dve.wait_ge(z[f"moe_stored{q}"], 16 * half(i, r - 3))
                    dve.tensor_tensor(y_out[:, q, :], bank(5 + q)[:, 0:C], b2_use, ALU.add).then_inc(z["moe_y"], 1)
                if (i := tile_at(t, 2, NS)) is not None:
                    e = dve.value_load(slot_expert[0:1, bass.ds(i, 1)], min_val=0, max_val=E - 1)
                    dve.tensor_copy(w2_use.rearrange("p c n -> p (c n)"), w2_sb[:, bass.ds(e * WIDE, WIDE)])
                    if some(i):
                        dve.wait_ge(z["moe_y"], i)
                    dve.tensor_copy(b2_use, b2_rows[:, bass.ds(e * C, C)]).then_inc(z["moe_w2"], 1)

            ticks(dve, NS, 3, tick, HEAD, 2)

            def final(i):
                q = i % 4
                dve.wait_ge(z["moe_root"], i + 1)
                dve.reciprocal(rstd[:, q:q + 1], rstd[:, q:q + 1]).then_inc(z["moe_apply"], 1)
                dve.scalar_tensor_tensor(moe_sum[:, q, :], moe_sum[:, q, :], mean_var[:, q, 0:1], row("ffn_ln2_g"),
                                         ALU.subtract, ALU.mult).then_inc(z["moe_apply"], 1)
                dve.wait_ge(z["moe_apply"], 2 * i + 2)
                dve.scalar_tensor_tensor(out_sb[:, i, :], moe_sum[:, q, :], rstd[:, q:q + 1], x_sb[:, i, :],
                                         ALU.mult, ALU.add).then_inc(z["moe_out"], 1)

            dve.wait_ge(z["moe_xb"], 1)
            for t in range(NT):
                q = t % 4
                dve.wait_ge(z[f"moe_tokens{t // GRP}"], 16 * GRP)
                dve.tensor_tensor(moe_sum[:, q, :], y_tok[:, t, :], src_sb[:, t, :], ALU.add).then_inc(z["moe_ln"], 1)
                dve.wait_ge(z["moe_ln"], 3 * t + 1)
                dve.bn_stats(stat6[:, q, :], moe_sum[:, q, :]).then_inc(z["moe_ln"], 1)
                dve.wait_ge(z["moe_ln"], 3 * t + 2)
                dve.bn_aggr(mean_var[:, q, :], stat6[:, q, :]).then_inc(z["moe_ln"], 1)
                if t >= 1:
                    final(t - 1)
            final(NT - 1)

        @block.sync
        def _(sp):
            sp.dma_start(x_sb[:, 0:GRP, :], x_view[:, 0:GRP, :]).then_inc(s["ld_x0"], 16)
            sp.dma_start(w_band[:, :, :], io["L0_attn_W_qkv"].rearrange("(k p) n -> p k n", p=P)).then_inc(s["ld_band"], 16)
            sp.dma_start(bqk_col[:, :], io["L0_attn_b_qkv"][0:2 * C].rearrange("(f p) -> p f", p=P),
                         allow_slow_non_contiguous=True).then_inc(s["ld_band"], 16)
            sp.dma_start(band_rows[:, 0, :], io["L0_attn_b_qkv"][2 * C:3 * C].partition_broadcast(P)).then_inc(s["ld_band"], 16)
            sp.dma_start(band_rows[:, 1, :], io["L0_attn_ln_w"].partition_broadcast(P)).then_inc(s["ld_band"], 16)
            sp.dma_start(band_rows[:, 2, :], io["L0_attn_ln_b"].partition_broadcast(P)).then_inc(s["ld_band"], 16)
            sp.dma_start(x_sb[:, GRP:NT, :], x_view[:, GRP:NT, :]).then_inc(s["ld_x"], 16)
            for w, n in enumerate(("Wq", "Wk", "Wv", "Wo")):
                sp.dma_start(w_xraw[:, w, :, :], io["L0_xattn_" + n].rearrange("(o p) i -> p o i", p=P)).then_inc(s["ld_xw"], 16)
            for n in ROWS:
                sp.dma_start(row(n), io["L0_" + n].partition_broadcast(P)).then_inc(s["ld_rows"], 16)
            sp.dma_start(b1_col[:, :, :], io["L0_ffn_b1"].rearrange("e (c p) -> p e c", p=P),
                         allow_slow_non_contiguous=True).then_inc(s["ld_small"], 16)
            sp.dma_start(router_col[:, 0:KC], io["L0_ffn_router_w"].rearrange("(k p) o -> p (k o)", p=P),
                         allow_slow_non_contiguous=True).then_inc(s["ld_small"], 16)
            sp.dma_start(router_col[:, KC:KC + 1], io["L0_ffn_router_b"].partition_broadcast(P)).then_inc(s["ld_small"], 16)
            for w, n in enumerate(("Wq", "Wk", "Wv")):
                sp.dma_start(w_fqkv[:, :, w * C:(w + 1) * C], io["L0_ffn_" + n].rearrange("(k p) n -> p k n", p=P)).then_inc(s["ld_fw"], 16)
            sp.dma_start(w_fo[:, :, :], io["L0_ffn_Wo"].rearrange("(k p) n -> p k n", p=P)).then_inc(s["ld_fw"], 16)
            sp.wait_ge(moe["moe_zero_set"], 1)
            zero_rows = x_sorted.rearrange("(t p) c -> p t c", p=P)
            for a, b in ((0, NT), (NT, NS)):
                sp.dma_start(zero_rows[:, a:b, :], attn_tok[:, 0:b - a, :]).then_inc(moe["moe_zeroed"], 16)
            sp.wait_ge(s["band_xT_ps"], NT)
            stage_sync(sp, ctx_kv)
            moe_sync(sp)

        @block.gpsimd
        def _(pool):
            pool.memset(eps_col[:, :], EPS).then_inc(s["const"], 1)
            pool.memset(attn_tok[:, :, :], 0.0).then_inc(moe["moe_zero_set"], 1)
            pool.memset(ident[:, :], 0.0).then_inc(s["const_zero"], 1)
            pool.memset(ident16[:, :], 0.0).then_inc(s["const_zero"], 1)
            pool.memset(band_mask[:, :], BAND_SCALE).then_inc(s["const_zero"], 1)
            pool.wait_ge(s["const_zero"], 3)
            for m in (ident, ident16):
                pool.affine_select(out=m[:, :], in_=m[:, :], compare_op=ALU.not_equal, fill=1.0, base=0,
                                   pattern=[[-1, P]], channel_multiplier=1).then_inc(s["const"], 1)
            pool.affine_select(out=band_mask[:, :], in_=band_mask[:, :], compare_op=ALU.is_ge, fill=0.0, base=0,
                               pattern=[[1, 2 * P]], channel_multiplier=-1).then_inc(s["const_zero"], 1)
            pool.wait_ge(s["const_zero"], 4)
            pool.affine_select(out=band_mask[:, :], in_=band_mask[:, :], compare_op=ALU.is_ge, fill=0.0, base=SPAN - 1,
                               pattern=[[-1, 2 * P]], channel_multiplier=1).then_inc(s["const"], 1)
            pool.memset(v_aug[:, :, :, D:2 * D], 0.0).then_inc(s["v_const"], 1)
            pool.wait_ge(s["v_const"], 1)
            pool.memset(v_aug[:, :, :, D:D + 1], 1.0).then_inc(s["v_const"], 1)
            for q in range(2):
                pool.memset(k_tok[:, q, :, MROW:SLOT], 0.0).then_inc(s["k_const"], 1)
            pool.wait_ge(s["k_const"], 2)
            for q in range(2):
                pool.memset(k_tok[:, q, :, MROW:MROW + 1], 1.0).then_inc(s["k_const"], 1)
            band_gpsimd(pool)
            pool.wait_ge(s["xw_ps"], 4)
            pool.wait_ge(s["band_out"], 5 * NT)
            pool.memset(q_tok[:, :, :, MROW:SLOT], 0.0).then_inc(s["q_const"], 1)
            pool.wait_ge(cross_q.s["proj"], NT)
            for j in range(2):
                pool.wait_ge(s["q_const"], j + 1)
                pool.memset(q_max[j][SLOT * (1 - j):SLOT * (2 - j), :, :], 0.0).then_inc(s["q_const"], 1)
            pool.wait_ge(s["q_const"], 3)
            pool.wait_ge(cross.s["out"], 4 * NG + 1)
            pool.memset(q_tok[:, :, :, MROW:MROW + 1], 0.0).then_inc(s["q_const"], 1)
            for q in range(2):
                pool.memset(k_tok[:, q, :, MROW:SLOT], 0.0).then_inc(s["k_const"], 1)
            pool.wait_ge(s["k_const"], 6)
            for q in range(2):
                pool.memset(k_tok[:, q, :, MROW:MROW + 1], 1.0).then_inc(s["k_const"], 1)
            stage_gpsimd(pool, self_qkv)
            post_gpsimd(pool)
            moe_gpsimd(pool)

        @block.tensor
        def _(pe):
            band_tensor(pe)
            weights_tensor(pe)
            pe.wait_ge(s["band_st"], NT)
            pe.wait_ge(s["band_out"], 5 * NT)
            pe.wait_ge(s["xw"], 4)
            pe.wait_ge(s["k_const"], 4)
            stage_tensor(pe, ctx_kv)
            pe.wait_ge(ctx_kv.s["split"], NCT)
            stage_tensor(pe, cross_q)
            pe.wait_ge(cross_q.s["split"], NT)
            pe.wait_ge(cross_q.s["copy"], NT)
            pe.wait_ge(s["q_const"], 3)
            pe.wait_ge(s["v_const"], 2)
            pe.wait_ge(ctx_kv.s["kop"], NCT)
            attention_tensor(pe, cross)
            pe.wait_ge(cross.s["out"], 4 * NG + 1)
            pe.wait_ge(s["k_const"], 8)
            pe.wait_ge(s["ld_fw"], 16 * 4)
            stage_tensor(pe, self_qkv)
            pe.wait_ge(self_qkv.s["split"], NT)
            pe.wait_ge(self_qkv.s["copy"], NT)
            pe.wait_ge(self_qkv.s["kop"], NT)
            pe.wait_ge(s["q_const"], 4)
            attention_tensor(pe, selfa)
            pe.wait_ge(selfa.s["out"], 4 * NG + 1)
            post_tensor(pe)
            moe_tensor(pe)

        @block.scalar
        def _(act):
            band_scalar(act)
            weights_scalar(act)
            stage_scalar(act, ctx_kv)
            stage_scalar(act, cross_q)
            attention_scalar(act, cross)
            stage_scalar(act, self_qkv)
            attention_scalar(act, selfa)
            post_scalar(act)
            moe_scalar(act)

        @block.vector
        def _(dve):
            band_vector(dve)
            dve.wait_ge(s["ld_rows"], 16 * len(ROWS))
            stage_vector(dve, ctx_kv)
            dve.wait_ge(s["xw_ps"], 4)
            stage_vector(dve, cross_q)
            dve.wait_ge(moe["moe_zeroed"], 16 * 2)
            attention_vector(dve, cross)
            stage_vector(dve, self_qkv)
            attention_vector(dve, selfa)
            post_vector(dve)
            moe_vector(dve)


_NAMES = ["x", "ctx_1024"] + ["L0_attn_" + n for n in ("W_qkv", "b_qkv", "ln_w", "ln_b")] + \
    ["L0_xattn_" + n for n in ("Wq", "bq", "Wk", "bk", "Wv", "bv", "Wo", "bo")] + \
    ["L0_ffn_" + n for n in ("Wq", "bq", "Wk", "bk", "Wv", "bv", "Wo", "bo", "router_w", "router_b",
                             "W1", "b1", "W2", "b2", "ln1_g", "ln1_b", "ln2_g", "ln2_b")]


def kernel(**inputs):
    import numpy as _np
    import concourse.bacc as _bacc
    from concourse import mybir as _mybir
    from concourse.bass_utils import run_bass_kernel_spmd as _run

    nc = _bacc.Bacc("TRN2", target_bir_lowering=False, num_devices=1)
    arrays, io = {}, {}
    for name in _NAMES:
        a = _np.ascontiguousarray(inputs[name])
        arrays[f"in_{name}"] = a
        io[name] = nc.dram_tensor(f"in_{name}", a.shape, _mybir.dt.from_np(a.dtype), kind="ExternalInput").ap()
    x = arrays["in_x"]
    out = nc.dram_tensor("out_x", x.shape, _mybir.dt.from_np(x.dtype), kind="ExternalOutput").ap()
    decoder_layer_kernel(nc, io, out)
    r = _run(nc, [arrays], core_ids=[0])
    return r.results[0]["out_x"]
```

```python
import concourse.bass as bass
from concourse import mybir
from contextlib import ExitStack


def decoder_layer_kernel(nc, io, out):
    fp32, fp16, i32 = mybir.dt.float32, mybir.dt.float16, mybir.dt.int32
    ALU = mybir.AluOpType
    ACT = mybir.ActivationFunctionType
    AX = mybir.AxisListType

    P = 128
    T, C = io["x"].shape[1:]
    S_CTX = io["ctx_1024"].shape[1]
    NT = T // P
    KC = C // P
    GRP = 4
    NG = NT // GRP
    QG = GRP * P
    EPS = 1e-5
    SPAN = 64
    BAND_SCALE = 1.0 / float((C * SPAN) ** 0.5)
    H, D = 16, C // 16
    SLOT = 64
    MROW = 3 * D
    NCT = -(-S_CTX // P)
    CTX_LAST = S_CTX - (NCT - 1) * P

    ctx = ExitStack()
    with ctx:
        def sb(name, shape, dt=fp32):
            return ctx.enter_context(nc.sbuf_tensor(name, shape, dt))

        def sems(*names):
            return {n: ctx.enter_context(nc.semaphore(n)) for n in names}

        x_sb = sb("x_sb", [P, NT, C])
        src_sb = sb("src_sb", [P, NT, C])
        k_op = sb("k_op", [P, H // 2, T], fp16)
        v_aug = sb("v_aug", [P, NT, H, 2 * D])
        q_arena = sb("q_arena", [P, NT * H * SLOT // 2])
        attn_tok = sb("attn_tok", [P, NT, C])
        p_arena = sb("p_arena", [P, 4 * 1024])
        w_xq = sb("w_xq", [P, KC, C])
        w_xkv = sb("w_xkv", [P, KC, 2 * C])
        w_xo = sb("w_xo", [P, KC, C])
        w_fqkv = sb("w_fqkv", [P, KC, 3 * C])
        w_fo = sb("w_fo", [P, KC, C])
        ROWS = ["xattn_bq", "xattn_bk", "xattn_bv", "xattn_bo", "ffn_bq", "ffn_bk", "ffn_bv", "ffn_bo",
                "ffn_router_w", "ffn_ln1_g", "ffn_ln1_b", "ffn_ln2_g", "ffn_ln2_b"]
        rows = sb("rows", [P, len(ROWS), C])

        def row(name, n=1):
            i = ROWS.index(name)
            return rows[:, i:i + n, :].rearrange("p n c -> p (n c)")

        ident = sb("ident", [P, P])
        ident16 = sb("ident16", [P, P], fp16)
        band_mask = sb("band_mask", [P, 2 * P])
        stat6 = sb("stat6", [P, 4, 6])
        mean_var = sb("mean_var", [P, 4, 2])
        rstd = sb("rstd", [P, 4])
        eps_col = sb("eps_col", [P, 1])
        E, F = io["L0_ffn_W1"].shape[0], io["L0_ffn_W1"].shape[2]
        FC = F // P
        b1_col = sb("b1_col", [P, E, FC])
        b1_use = sb("b1_use", [P, FC])
        router_bias = sb("router_bias", [P, 1])

        def carve(arena, at, *shape):
            n = 1
            for k in shape:
                n *= k
            v = arena[:, at:at + n]
            if len(shape) == 2:
                v = v.rearrange("p (a b) -> p a b", b=shape[1])
            if len(shape) == 3:
                v = v.rearrange("p (a b c) -> p a b c", b=shape[1], c=shape[2])
            return v

        q_tok = q_arena[:, :].bitcast(fp16).rearrange("p (t h s) -> p t h s", h=H, s=SLOT)
        w_band = carve(q_arena, 0, KC, 3 * C)
        band_qk = carve(q_arena, 1536, 4, 4, P)
        band_v = carve(q_arena, 3584, 4, C)
        band_st = carve(q_arena, 4608, 2, 2 * P)
        w_xraw = carve(q_arena, 5120, 4, KC, C)
        band_rows = carve(q_arena, 7168, 3, C)
        band_tmp = sb("band_tmp", [P, 2, C])
        bqk_col = sb("bqk_col", [P, 4])
        xin = carve(p_arena, 0, 2, C)
        xT = carve(p_arena, 512, 2, KC, P)

        s_pair = [ctx.enter_context(nc.psum_tensor(f"s_pair{i}", [P, 1024], fp32)) for i in range(2)]
        singles = [ctx.enter_context(nc.psum_tensor(f"bank{i}", [P, 512], fp32)) for i in range(4, 8)]

        def bank(i):
            return s_pair[i // 2][:, (i % 2) * 512:(i % 2 + 1) * 512] if i < 4 else singles[i - 4][:, :]

        s = sems("ld_x0", "ld_x", "ld_band", "ld_xw", "ld_rows", "ld_fw", "const_zero", "const", "stored",
                 "band_zero", "band_ln", "band_xT_ps", "band_xT", "band_qkv_ps", "band_qkv", "band_s", "band_st",
                 "band_av", "band_out", "band_root", "band_ln_root", "band_xb", "xw_ps", "xw", "v_const", "k_const", "q_const",
                 "ld_small")

        x_view = io["x"][0].rearrange("(t p) c -> p t c", p=P)
        out_view = out[0].rearrange("(t p) c -> p t c", p=P)

        def ticks(eng, n, depth, tick, head=GRP, unroll=GRP):
            loops = (n - head) // unroll
            for t in range(head):
                tick(t, t % unroll)
            with eng.Fori(head // unroll, head // unroll + loops) as g:
                for r in range(unroll):
                    tick(g * unroll + r, r)
            for t in range(head + loops * unroll, n + depth):
                tick(t, t % unroll)

        def tile_at(t, stage, n):
            if isinstance(t, int) and not 0 <= t - stage < n:
                return None
            return t - stage

        def some(t, least=1):
            return not isinstance(t, int) or t >= least

        block = ctx.enter_context(nc.Block())

        def norm_aggr(dve, ring, steps):
            dve.bn_aggr(mean_var[:, ring, :], stat6[:, ring, :]).then_inc(steps, 1)

        def norm_root(act, ring, steps, count, roots):
            act.wait_ge(steps, count + 2)
            act.activation(rstd[:, ring:ring + 1], mean_var[:, ring, 1:2], ACT.Sqrt, bias=eps_col[:, :]).then_inc(roots, 1)

        def norm_apply(dve, i, ring, source, dest, steps, count, roots):
            dve.wait_ge(roots, i + 1)
            dve.reciprocal(rstd[:, ring:ring + 1], rstd[:, ring:ring + 1]).then_inc(steps, 1)
            dve.wait_ge(steps, count + 3)
            dve.tensor_scalar(dest, source, mean_var[:, ring, 0:1], rstd[:, ring:ring + 1],
                              ALU.subtract, ALU.mult).then_inc(steps, 1)

        def band_tensor(pe):
            pe.wait_ge(s["const"], 4)
            pe.wait_ge(s["ld_band"], 16 * 5)
            pe.wait_ge(s["band_zero"], 2)

            def tick(t, r):
                if (i := tile_at(t, 3, NT)) is not None:
                    pe.wait_ge(s["band_st"], i + 1)
                    if some(i):
                        pe.wait_ge(s["band_out"], 5 * i)
                    q, prev = (r - 3) % 4, (r - 4) % 4
                    pe.matmul(bank(7)[:, 0:C], band_st[:, q % 2, 0:P], band_v[:, q, :], start=True, stop=False)
                    pe.matmul(bank(7)[:, 0:C], band_st[:, q % 2, P:2 * P], band_v[:, prev, :],
                              start=False, stop=True).then_inc(s["band_av"], 1)
                if (i := tile_at(t, 2, NT)) is not None:
                    pe.wait_ge(s["band_qkv"], 2 * i + 2)
                    if some(i):
                        pe.wait_ge(s["band_st"], i)
                    q, prev = (r - 2) % 4, (r - 3) % 4
                    for part, keys in ((0, q), (1, prev)):
                        for k in range(KC):
                            last = pe.matmul(bank(6)[:, part * P:(part + 1) * P], band_qk[:, keys, KC + k, :],
                                             band_qk[:, q, k, :], start=k == 0, stop=k == KC - 1)
                    last.then_inc(s["band_s"], 1)
                if (i := tile_at(t, 1, NT)) is not None:
                    pe.wait_ge(s["band_xT"], i + 1)
                    if some(i - 1):
                        pe.wait_ge(s["band_qkv"], 2 * (i - 1))
                    q = (r - 1) % 2
                    for f in range(4):
                        for k in range(KC):
                            pe.matmul(bank(2 + q)[:, f * P:(f + 1) * P], w_band[:, k, f * P:(f + 1) * P], xT[:, q, k, :],
                                      start=k == 0, stop=k == KC - 1)
                    for k in range(KC):
                        last = pe.matmul(bank(4 + q)[:, 0:C], xT[:, q, k, :], w_band[:, k, 2 * C:3 * C],
                                         start=k == 0, stop=k == KC - 1)
                    last.then_inc(s["band_qkv_ps"], 1)
                if (i := tile_at(t, 0, NT)) is not None:
                    pe.wait_ge(s["band_ln"], 4 * i + 4)
                    if some(i - 1):
                        pe.wait_ge(s["band_xT"], i - 1)
                    q = r % 2
                    for k in range(KC):
                        last = pe.transpose(bank(q)[:, k * P:(k + 1) * P], xin[:, q, k * P:(k + 1) * P], ident[:, :])
                    last.then_inc(s["band_xT_ps"], 1)

            ticks(pe, NT, 3, tick)

        def band_scalar(act):
            act.wait_ge(s["const"], 1)

            def tick(t, r):
                if (i := tile_at(t, 3, NT)) is not None:
                    norm_root(act, 2 + (r - 3) % 2, s["band_out"], 5 * i, s["band_root"])
                if (i := tile_at(t, 0, NT)) is not None:
                    norm_root(act, r % 2, s["band_ln"], 4 * i, s["band_ln_root"])
                    act.wait_ge(s["band_xT_ps"], i + 1)
                    if some(i - 1):
                        act.wait_ge(s["band_qkv_ps"], i - 1)
                    act.activation(xT[:, r % 2, :, :], bank(r % 2)[:, 0:C].rearrange("p (k t) -> p k t", k=KC),
                                   ACT.Copy).then_inc(s["band_xT"], 1)

            ticks(act, NT, 3, tick)

        def band_vector(dve):
            dve.memset(band_qk[:, 3, :, :], 0.0).then_inc(s["band_zero"], 1)
            dve.memset(band_v[:, 3, :], 0.0).then_inc(s["band_zero"], 1)
            dve.wait_ge(s["ld_x0"], 16)

            def tick(t, r):
                if isinstance(t, int) and t == GRP - 1:
                    dve.wait_ge(s["ld_x"], 16)
                o = bank(7)[:, 0:C]
                q3 = (r - 3) % 2
                if (i := tile_at(t, 3, NT)) is not None:
                    dve.wait_ge(s["band_av"], i + 1)
                    dve.bn_stats(stat6[:, 2 + q3, :], o).then_inc(s["band_out"], 1)
                if (i := tile_at(t, 0, NT)) is not None:
                    dve.bn_stats(stat6[:, r % 2, :], x_sb[:, i, :]).then_inc(s["band_ln"], 1)
                    dve.wait_ge(s["band_ln"], 4 * i + 1)
                if (i := tile_at(t, 3, NT)) is not None:
                    dve.wait_ge(s["band_out"], 5 * i + 1)
                if (i := tile_at(t, 2, NT)) is not None:
                    dve.wait_ge(s["band_s"], i + 1)
                    if some(i - 1):
                        dve.wait_ge(s["band_av"], i - 1)
                    dve.tensor_tensor(band_st[:, (r - 2) % 2, :], bank(6)[:, 0:2 * P], band_mask[:, :],
                                      ALU.mult).then_inc(s["band_st"], 1)
                if tile_at(t, 3, NT) is not None:
                    norm_aggr(dve, 2 + q3, s["band_out"])
                if tile_at(t, 0, NT) is not None:
                    norm_aggr(dve, r % 2, s["band_ln"])
                if (i := tile_at(t, 3, NT)) is not None:
                    dve.wait_ge(s["band_out"], 5 * i + 2)
                    ring, c = 2 + q3, 5 * i
                    dve.scalar_tensor_tensor(band_tmp[:, q3, :], o, mean_var[:, ring, 0:1], band_rows[:, 1, :],
                                             ALU.subtract, ALU.mult).then_inc(s["band_out"], 1)
                    dve.wait_ge(s["band_root"], i + 1)
                    dve.reciprocal(rstd[:, ring:ring + 1], rstd[:, ring:ring + 1]).then_inc(s["band_out"], 1)
                    dve.wait_ge(s["band_out"], c + 4)
                    dve.wait_ge(s["band_xb"], i + 1)
                    dve.scalar_tensor_tensor(x_sb[:, i, :], band_tmp[:, q3, :], rstd[:, ring:ring + 1], x_sb[:, i, :],
                                             ALU.mult, ALU.add).then_inc(s["band_out"], 1)
                if (i := tile_at(t, 0, NT)) is not None:
                    if some(i - 1):
                        dve.wait_ge(s["band_xT_ps"], i - 1)
                    norm_apply(dve, i, r % 2, x_sb[:, i, :], xin[:, r % 2, :], s["band_ln"], 4 * i, s["band_ln_root"])
                if (i := tile_at(t, 1, NT)) is not None:
                    q = (r - 1) % 4
                    dve.wait_ge(s["band_qkv_ps"], i + 1)
                    dve.tensor_tensor(band_qk[:, q, :, :], bank(2 + q % 2).rearrange("p (f t) -> p f t", f=4),
                                      bqk_col[:, :].unsqueeze(2).broadcast_to([P, 4, P]), ALU.add).then_inc(s["band_qkv"], 1)
                    dve.tensor_tensor(band_v[:, q, :], bank(4 + q % 2)[:, 0:C], band_rows[:, 0, :],
                                      ALU.add).then_inc(s["band_qkv"], 1)

            ticks(dve, NT, 3, tick)

        def band_gpsimd(pool):
            pool.wait_ge(s["ld_band"], 16 * 5)

            def tick(t, r):
                if (i := tile_at(t, 1, NT)) is not None:
                    pool.wait_ge(s["band_ln"], 4 * i + 4)
                    pool.tensor_tensor(x_sb[:, i, :], x_sb[:, i, :], band_rows[:, 2, :], ALU.add).then_inc(s["band_xb"], 1)

            ticks(pool, NT, 1, tick)

        def weights_tensor(pe):
            pe.wait_ge(s["ld_xw"], 16 * 4)
            pe.wait_ge(s["band_xT"], NT)
            pe.wait_ge(s["band_qkv"], 2 * NT)
            for w in range(4):
                for k in range(KC):
                    for o in range(KC):
                        last = pe.transpose(bank(w)[:, k * C + o * P:k * C + (o + 1) * P],
                                            w_xraw[:, w, o, k * P:(k + 1) * P], ident[:, :])
                last.then_inc(s["xw_ps"], 1)

        def weights_scalar(act):
            for w, dest in enumerate((w_xq[:, :, :], w_xkv[:, :, 0:C], w_xkv[:, :, C:2 * C], w_xo[:, :, :])):
                act.wait_ge(s["xw_ps"], w + 1)
                act.activation(dest, bank(w).rearrange("p (k n) -> p k n", k=KC), ACT.Copy).then_inc(s["xw"], 1)

        HEAD = 6

        qk32 = carve(p_arena, 1024, 2, 2 * C)
        k_tok = carve(p_arena, 2048, 2, H * SLOT // 2)
        k_tok = k_tok.rearrange("p a b -> p (a b)").bitcast(fp16).rearrange("p (a h s) -> p a h s", h=H, s=SLOT)
        at_in = carve(p_arena, 3072, 2, C)
        aT = carve(p_arena, 3584, 2, KC, P)

        class Stage:
            def __init__(self, name, tiles, weights, width, bias, has_q, has_kv, front=None, loaded=None, beside=False):
                self.name, self.tiles, self.weights, self.width = name, tiles, weights, width
                self.bias, self.has_q, self.has_kv, self.front, self.loaded = bias, has_q, has_kv, front, loaded
                self.f = 1 if front else 0
                self.s = {n: ctx.enter_context(nc.semaphore(f"{name}_{n}")) for n in (
                    "in0", "in1", "ln", "root", "xT_ps", "xT", "proj", "sum", "hi", "split", "copy", "kT", "kop",
                    "at", "aT_ps", "aT", "o_ps", "kept", "res", "res_bias")}
                self.xin, self.xT = (at_in, aT) if beside else (xin, xT)
                self.qk = qk32[:, :, C:2 * C] if beside else qk32
                self.xT_bank, self.proj_banks = (0, (1, 5)) if beside else (2, (3, 4))

            def rows(self, t):
                return CTX_LAST if self.loaded and isinstance(t, int) and t == NCT - 1 else P

        def stage_tensor(pe, st):
            z, f, n = st.s, st.f, st.tiles

            def tick(t, r):
                if (i := tile_at(t, f + 2, n)) is not None:
                    q, m = (r - f - 2) % 2, st.rows(i)
                    pe.wait_ge(z["xT"], i + 1)
                    if some(i - 1):
                        pe.wait_ge(z["split"], i - 1)
                    for at in range(0, st.width, 512):
                        w = min(512, st.width - at)
                        dest = bank(st.proj_banks[q]) if at == 0 else bank(5 + 2 * q)
                        for k in range(KC):
                            last = pe.matmul(dest[0:m, 0:w], st.xT[:, q, k, 0:m], st.weights[:, k, at:at + w],
                                             start=k == 0, stop=k == KC - 1)
                    last.then_inc(z["proj"], 1)
                if (i := tile_at(t, f + 1, n)) is not None:
                    q, m = (r - f - 1) % 2, st.rows(i)
                    if st.loaded:
                        pe.wait_ge(z[f"in{q}"], 16 * half(i, r - f - 1) + 16)
                    else:
                        pe.wait_ge(z["ln"], 4 * i + 4)
                    if some(i):
                        pe.wait_ge(z["xT"], i)
                    for k in range(KC):
                        last = pe.transpose(bank(st.xT_bank)[:, k * P:k * P + m], st.xin[0:m, q, k * P:(k + 1) * P], ident[0:m, 0:m])
                    last.then_inc(z["xT_ps"], 1)
                if st.front and (i := tile_at(t, 1, n)) is not None:
                    pe.wait_ge(z["aT"], i + 1)
                    if some(i):
                        pe.wait_ge(z["res"], i)
                    for k in range(KC):
                        last = pe.matmul(bank(1)[:, 0:C], aT[:, (r - 1) % 2, k, :], st.front[:, k, :],
                                         start=k == 0, stop=k == KC - 1)
                    last.then_inc(z["o_ps"], 1)
                if st.front and (i := tile_at(t, 0, n)) is not None:
                    pe.wait_ge(z["at"], i + 1)
                    if some(i):
                        pe.wait_ge(z["aT"], i)
                    for k in range(KC):
                        last = pe.transpose(bank(0)[:, k * P:(k + 1) * P], at_in[:, r % 2, k * P:(k + 1) * P], ident[:, :])
                    last.then_inc(z["aT_ps"], 1)
                if st.has_kv and (i := tile_at(t, f + 3, n)) is not None:
                    q, m = (r - f - 3) % 2, st.rows(i)
                    pe.wait_ge(z["split"], i + 1)
                    pe.wait_ge(z["copy"], i + 1)
                    if some(i):
                        pe.wait_ge(z["kop"], i)
                    for pair in range(H // 2):
                        last = pe.transpose(bank(6).bitcast(fp16)[:, pair * P:pair * P + m],
                                            k_tok[0:m, q, 2 * pair:2 * pair + 2, :].rearrange("p h s -> p (h s)"),
                                            ident16[0:m, 0:m])
                    last.then_inc(z["kT"], 1)

            return tick

        def stage_scalar(act, st):
            z, f, n = st.s, st.f, st.tiles

            def tick(t, r):
                if (i := tile_at(t, f + 1, n)) is not None:
                    q, m = (r - f - 1) % 2, st.rows(i)
                    act.wait_ge(z["xT_ps"], i + 1)
                    if some(i - 1):
                        act.wait_ge(z["proj"], i - 1)
                    act.activation(st.xT[:, q, :, 0:m], bank(st.xT_bank)[:, 0:C].rearrange("p (k t) -> p k t", k=KC)[:, :, 0:m],
                                   ACT.Copy).then_inc(z["xT"], 1)
                if st.front and (i := tile_at(t, 0, n)) is not None:
                    act.wait_ge(z["aT_ps"], i + 1)
                    if some(i - 1):
                        act.wait_ge(z["o_ps"], i - 1)
                    act.activation(aT[:, r % 2, :, :], bank(0)[:, 0:C].rearrange("p (k t) -> p k t", k=KC),
                                   ACT.Copy).then_inc(z["aT"], 1)
                if (i := tile_at(t, f + 2, n)) is not None:
                    q, m = (r - f - 2) % 2, st.rows(i)
                    act.wait_ge(z["hi"], i + 1)
                    if st.has_q:
                        last = act.activation(q_tok[0:m, i, :, D:2 * D], q_tok[0:m, i, :, 0:D], ACT.Copy)
                    if st.has_kv:
                        last = act.activation(k_tok[0:m, q, :, 2 * D:3 * D], k_tok[0:m, q, :, 0:D], ACT.Copy)
                    last.then_inc(z["copy"], 1)
                if not st.loaded and (i := tile_at(t, f, n)) is not None:
                    norm_root(act, (r - f) % 2, z["ln"], 4 * i, z["root"])
                if st.has_kv and (i := tile_at(t, f + 3, n)) is not None:
                    m = st.rows(i)
                    act.wait_ge(z["kT"], i + 1)
                    act.activation(k_op[:, :, bass.ds(i * P, m)],
                                   bank(6).bitcast(fp16).rearrange("p (h t) -> p h t", t=P)[:, :, 0:m],
                                   ACT.Copy).then_inc(z["kop"], 1)

            return tick

        def stage_vector(dve, st):
            z, f, n = st.s, st.f, st.tiles
            ck = C if st.has_q else 0
            first = C * (st.has_q + st.has_kv)

            def tick(t, r):
                i, b = tile_at(t, f + 2, n), None if st.loaded else tile_at(t, f, n)
                if i is not None:
                    q, m = (r - f - 2) % 2, st.rows(i)
                    dve.wait_ge(z["proj"], i + 1)
                    dve.tensor_tensor(st.qk[0:m, q, 0:first], bank(st.proj_banks[q])[0:m, 0:first], row(st.bias, first // C)[0:m, :],
                                      ALU.add).then_inc(z["sum"], 1)
                if st.front and b is not None:
                    dve.wait_ge(z["o_ps"], b + 1)
                    dve.wait_ge(z["res_bias"], b + 1)
                    dve.tensor_tensor(x_sb[:, b, :], bank(1)[:, 0:C], x_sb[:, b, :], ALU.add).then_inc(z["res"], 1)
                    dve.wait_ge(z["res"], b + 1)
                if i is not None and st.has_kv:
                    v_ps = bank(5 + 2 * q)[0:m, 0:C] if first == 2 * C else bank(st.proj_banks[q])[0:m, C:2 * C]
                    dve.tensor_tensor(v_aug[0:m, i, :, 0:D], v_ps.rearrange("p (h d) -> p h d", h=H),
                                      row(st.bias, 3)[0:m, first:first + C].rearrange("p (h d) -> p h d", h=H)
                                      if st.has_q else row(st.bias, 2)[0:m, C:2 * C].rearrange("p (h d) -> p h d", h=H),
                                      ALU.add)
                if b is not None:
                    dve.bn_stats(stat6[:, (r - f) % 2, :], x_sb[:, b, :]).then_inc(z["ln"], 1)
                    dve.wait_ge(z["ln"], 4 * b + 1)
                if i is not None:
                    dve.wait_ge(z["sum"], i + 1)
                    parts = []
                    if st.has_q:
                        parts.append((q_tok[0:m, i, :, :], 2 * D, st.qk[0:m, q, 0:C].rearrange("p (h d) -> p h d", h=H)))
                    if st.has_kv:
                        if some(i - 1):
                            dve.wait_ge(z["kT"], i - 1)
                        parts.append((k_tok[0:m, q, :, :], D, st.qk[0:m, q, ck:ck + C].rearrange("p (h d) -> p h d", h=H)))
                    for op, _, full in parts:
                        last = dve.tensor_copy(op[:, :, 0:D], full)
                    last.then_inc(z["hi"], 1)
                    dve.wait_ge(z["hi"], i + 1)
                    for op, lo, full in parts:
                        last = dve.tensor_tensor(op[:, :, lo:lo + D], full, op[:, :, 0:D], ALU.subtract)
                    last.then_inc(z["split"], 1)
                if not st.loaded and (i := tile_at(t, f, n)) is not None:
                    norm_aggr(dve, (r - f) % 2, z["ln"])
                    if some(i - 1):
                        dve.wait_ge(z["xT_ps"], i - 1)
                        if st.front:
                            dve.wait_ge(z["kept"], i - 1)
                    norm_apply(dve, i, (r - f) % 2, x_sb[:, i, :], st.xin[:, (r - f) % 2, :], z["ln"], 4 * i, z["root"])

            return tick

        def stage_gpsimd(pool, st):
            z, f, n = st.s, st.f, st.tiles

            def tick(t, r):
                if st.front and (i := tile_at(t, 0, n)) is not None:
                    if some(i - 1):
                        pool.wait_ge(z["aT_ps"], i - 1)
                    pool.tensor_tensor(x_sb[:, i, :], x_sb[:, i, :], row("xattn_bo"), ALU.add).then_inc(z["res_bias"], 1)
                    pool.tensor_copy(at_in[:, r % 2, :], attn_tok[:, i, :]).then_inc(z["at"], 1)
                if st.front and (i := tile_at(t, f + 1, n)) is not None:
                    pool.wait_ge(z["ln"], 4 * i + 4)
                    pool.tensor_tensor(src_sb[:, i, :], st.xin[:, (r - f - 1) % 2, :], row("ffn_bo"), ALU.add).then_inc(z["kept"], 1)

            ticks(pool, n, f + 3, tick, HEAD, 2)

        def half(i, r):
            return i // 2 if isinstance(i, int) else (i - r % 2) // 2

        def stage_sync(sp, st):
            z, n = st.s, st.tiles

            def tick(t, r):
                m = st.rows(t)
                if some(t - 1):
                    sp.wait_ge(z["xT_ps"], t - 1)
                sp.dma_start(xin[0:m, r % 2, :], st.loaded[bass.ds(t * P, m), :]).then_inc(z[f"in{r % 2}"], 16)

            ticks(sp, n, 0, tick, HEAD, 2)

        ctx_kv = Stage("ctx", NCT, w_xkv, 2 * C, "xattn_bk", has_q=False, has_kv=True, loaded=io["ctx_1024"][0])
        cross_q = Stage("xq", NT, w_xq, C, "xattn_bq", has_q=True, has_kv=False, beside=True)
        self_qkv = Stage("self", NT, w_fqkv, 3 * C, "ffn_bq", has_q=True, has_kv=True, front=w_xo)

        def run_stage(eng, tick_of, st):
            ticks(eng, st.tiles, st.f + 3, tick_of(eng, st), HEAD, 2)

        def run_beside(eng, tick_of, a, b):
            tick_a, tick_b = tick_of(eng, a), tick_of(eng, b)

            def tick(t, r):
                tick_a(t, r)
                tick_b(t, r)

            ticks(eng, a.tiles, b.tiles - a.tiles + 3, tick, HEAD, 2)

        JOBS = NG * H // 2
        AHEAD = 8
        UNITS = 16
        SCALE = float(D) ** -0.5

        q_max = (sb("q_max", [P, 2, QG], fp16)[:, :, :],
                 w_xq[:, :, :].rearrange("p k n -> p (k n)").bitcast(fp16).rearrange("p (a q) -> p a q", a=2))
        q_exp = sb("q_exp", [P, 2, 2, QG], fp16)
        neg_max = sb("neg_max", [P, 2, GRP, 2, 4])
        o_sb = sb("o_sb", [P, QG])
        rden = sb("rden", [P, GRP * 4])
        prob = carve(p_arena, 0, 8, QG)
        score_bank, max_bank, o_bank, misc = [bank(i) for i in range(3)], [bank(i) for i in range(3, 6)], bank(6), bank(7)
        q_op = q_tok.rearrange("p t h s -> p t (h s)")

        class Attention:
            def __init__(self, name, keys):
                self.tiles = [(i, min(P, keys - i * P)) for i in range(-(-keys // P))]
                self.n = len(self.tiles)
                width = -(-keys // 4)
                self.chunks = [(a, min(width, keys - a)) for a in range(0, keys, width)]
                self.s = {n: ctx.enter_context(nc.semaphore(f"{name}_{n}")) for n in (
                    "q_ps", "q_op", "max_ps", "max", "job", "score", "exp", "pv", "o_sb", "oT", "recip", "out")}
                done = [2 * 2 * UNITS * (i + 1) // self.n for i in range(self.n)]
                self.first_ends = next(i for i, d in enumerate(done) if d >= 2 * UNITS - AHEAD)
                self.second_ends = next(i for i, d in enumerate(done) if d >= 2 * 2 * UNITS - AHEAD)

            def builds_at(self, h):
                return {1: ("qa", 2 * h + 3), self.first_ends + 1: ("qb", 2 * h + 2),
                        self.first_ends + 3: ("qa", 2 * h + 4), self.second_ends + 1: ("qb", 2 * h + 3)}

            def maxima_at(self, h, kt, quarter=None):
                first, last = (4 * kt, 4 * kt + 4) if quarter is None else (4 * kt + quarter, 4 * kt + quarter + 1)
                total = 2 * 2 * UNITS
                return [(2 * h + 2 + i // (2 * UNITS), i // 2 % UNITS, i % 2)
                        for i in range(AHEAD + total * first // (4 * self.n), AHEAD + total * last // (4 * self.n))]

            def unit_at(self, h, kt, head):
                return 4 * (self.n * h + kt) + head

        def max_bank_of(r, u, j):
            return max_bank[(2 * UNITS * r + 2 * u + j) % 3]

        def build_count(kind, n):
            if isinstance(n, int) and (kind, n) in (("qa", 0), ("qb", JOBS - 1)):
                return 1 if n == 0 else 2 * JOBS
            return 2 * n if kind == "qa" else 2 * n + 3

        def exists(n):
            return not isinstance(n, int) or n < JOBS

        def steps(eng, step):
            step(0, 0)
            with eng.Fori(0, NG - 1) as g:
                for h in range(1, 4):
                    step(g, h)
                step(g + 1, 0)
            for h in range(1, 4):
                last = step(NG - 1, h)
            return last

        def before(g, h):
            return (g, h - 1) if h else None if isinstance(g, int) and g == 0 else (g - 1, 3)

        FIRST_BUILDS = [("qa", 0), ("qa", 1), ("qb", 0), ("qa", 2), ("qb", 1)]

        def attention_tensor(pe, at):
            z = at.s

            def build(kind, g, r):
                n, pair, tile0 = 8 * g + r, r % 8, 4 * g + 4 * (r // 8)
                if kind == "qb":
                    pe.wait_ge(z["job"], n + 1)
                for q in range(GRP):
                    last = pe.matmul(misc[:, q * P:(q + 1) * P], q_op[:, tile0 + q, pair * P:(pair + 1) * P], ident16[:, :],
                                     start=True, stop=True)
                last.then_inc(z["q_ps"], 1)

            def maxima(g, r, u, j):
                n, pair, (k0, width) = 8 * g + r, r % 8, at.chunks[u % 4]
                if u == 0 and j == 0:
                    pe.wait_ge(z["q_op"], build_count("qa", n))
                before = 2 * (UNITS * n + u) + j - 2
                if (r, u, j) == (2, AHEAD // 2, 0):
                    before = before + 2
                if some(before):
                    pe.wait_ge(z["max"], before)
                pe.matmul(max_bank_of(r, u, j)[:, 0:width], q_max[j][:, r % 2, (u // 4) * P:(u // 4 + 1) * P],
                          k_op[:, pair, k0:k0 + width], start=True, stop=True).then_inc(z["max_ps"], 1)

            def scores(g, h, kt, head):
                m, k = at.tiles[kt][1], at.unit_at(h, kt, head)
                pair, j = head // 2, head % 2
                if kt == 0 and j == 0:
                    pe.wait_ge(z["q_op"], build_count("qb", 8 * g + 2 * h + pair))
                if k >= 3:
                    pe.wait_ge(z["exp"], 4 * at.n * 4 * g + k - 2)
                elif k == 0 and before(g, h):
                    pe.wait_ge(z["exp"], 4 * at.n * 4 * g)
                pe.matmul(score_bank[k % 3][0:m, :], k_op[SLOT * j:SLOT * (j + 1), 2 * h + pair, kt * P:kt * P + m],
                          q_exp[SLOT * j:SLOT * (j + 1), h % 2, pair, :],
                          start=True, stop=True, tile_position=(SLOT * j, 0)).then_inc(z["score"], 1)

            def sums(g, h, kt):
                m, it = at.tiles[kt][1], 4 * g + h
                pe.wait_ge(z["exp"], 4 * (at.n * it + kt + 1))
                if kt == 0 and before(g, h):
                    pe.wait_ge(z["o_sb"], it)
                for head in range(4):
                    last = pe.matmul(o_bank[32 * head:32 * head + 32, :], v_aug[0:m, kt, 4 * h + head, :],
                                     prob[0:m, at.unit_at(h, kt, head) % 8, :],
                                     start=kt == 0, stop=kt == at.n - 1, tile_position=(0, 32 * head))
                last.then_inc(z["pv"], 1)

            def turn_sums(g, h):
                pe.wait_ge(z["o_sb"], 4 * g + h + 1)
                for q in range(GRP):
                    last = pe.transpose(misc[:, q * P:(q + 1) * P], o_sb[:, q * P:(q + 1) * P], ident[:, :])
                last.then_inc(z["oT"], 1)

            for i, (kind, r) in enumerate(FIRST_BUILDS):
                if i:
                    pe.wait_ge(z["q_op"], i)
                build(kind, 0, r)
                if i in (1, 3):
                    for u in range(0 if i == 1 else 2, UNITS):
                        for j in range(2):
                            maxima(0, i // 2, u, j)
                    for u in range(2 if i == 1 else AHEAD // 2):
                        for j in range(2):
                            maxima(0, i // 2 + 1, u, j)
            pe.wait_ge(z["q_op"], len(FIRST_BUILDS))

            def step(g, h):
                it, last_step = 4 * g + h, before(g, h)
                free = (z["q_op"], build_count("qb", 8 * g + 2 * h + 1))
                for kt, m in at.tiles:
                    todo = [[m for m in at.maxima_at(h, kt, head) if exists(8 * g + m[0])] for head in range(4)]
                    for head in range(5):
                        if head == (2 if any(todo) else 4):
                            if kt:
                                sums(g, h, kt - 1)
                            elif last_step:
                                sums(*last_step, at.n - 1)
                        if head < 4:
                            scores(g, h, kt, head)
                            for r, u, j in todo[head]:
                                maxima(g, r, u, j)
                    if kt in at.builds_at(h):
                        kind, r = at.builds_at(h)[kt]
                        if exists(8 * g + r):
                            pe.wait_ge(*free)
                            build(kind, g, r)
                            free = (z["q_op"], build_count(kind, 8 * g + r))
                    if kt == 2 and last_step:
                        pe.wait_ge(*free)
                        turn_sums(*last_step)
                        free = (z["out"], it + 1)
                return free

            free = steps(pe, step)
            sums(NG - 1, 3, at.n - 1)
            pe.wait_ge(*free)
            turn_sums(NG - 1, 3)

        def attention_scalar(act, at):
            z = at.s

            def read_build(kind, g, r):
                act.wait_ge(z["q_ps"], build_count(kind, 8 * g + r))
                if kind == "qa":
                    for j in range(2):
                        rows = slice(SLOT * j, SLOT * (j + 1))
                        last = act.activation(q_max[j][rows, r % 2, :], misc[rows, :], ACT.Copy)
                else:
                    last = act.activation(q_exp[:, (r // 2) % 2, r % 2, :], misc, ACT.Copy)
                last.then_inc(z["q_op"], 1)

            def read_sums(g, h):
                act.wait_ge(z["pv"], at.n * (4 * g + h + 1))
                act.activation(o_sb[:, :], o_bank, ACT.Copy).then_inc(z["o_sb"], 1)

            for kind, r in FIRST_BUILDS:
                read_build(kind, 0, r)

            def step(g, h):
                it, last_step = 4 * g + h, before(g, h)
                for kt, m in at.tiles:
                    for head in range(4):
                        k = at.unit_at(h, kt, head)
                        act.wait_ge(z["score"], 4 * at.n * 4 * g + k + 1)
                        if head == 0 and (kt >= 2 or last_step):
                            act.wait_ge(z["pv"], at.n * it + kt - 1)
                        act.activation(prob[0:m, k % 8, :], score_bank[k % 3][0:m, :], ACT.Exp, scale=SCALE).then_inc(z["exp"], 1)
                    if kt in at.builds_at(h):
                        kind, r = at.builds_at(h)[kt]
                        if exists(8 * g + r):
                            read_build(kind, g, r)
                    if kt == 0 and last_step:
                        read_sums(*last_step)

            steps(act, step)
            read_sums(NG - 1, 3)

        def attention_vector(dve, at):
            z = at.s
            dve.memset(rden[:, :], 1.0).then_inc(z["out"], 1)

            def maxima(g, r, u, j):
                n, (_, width) = 8 * g + r, at.chunks[u % 4]
                dve.wait_ge(z["max_ps"], 2 * (UNITS * n + u) + j + 1)
                dve.tensor_reduce(neg_max[:, r % 2, u // 4, j, u % 4:u % 4 + 1], max_bank_of(r, u, j)[:, 0:width], AX.X, ALU.max,
                                  negate=True).then_inc(z["max"], 1)
                if u == UNITS - 1 and j == 1:
                    dve.wait_ge(z["max"], 2 * UNITS * (n + 1))
                    dve.tensor_reduce(q_tok[:, bass.ds(4 * g + 4 * (r // 8), GRP), 2 * (r % 8):2 * (r % 8) + 2, MROW],
                                      neg_max[:, r % 2, :, :, :], AX.X, ALU.min).then_inc(z["job"], 1)

            def result(g, h):
                it = 4 * g + h
                sums = misc.rearrange("p (q h d) -> p q h d", q=GRP, h=4)
                dve.wait_ge(z["oT"], it + 1)
                dve.reciprocal(rden[:, :].rearrange("p (q h) -> p q h", h=4), sums[:, :, :, D]).then_inc(z["recip"], 1)
                dve.wait_ge(z["recip"], it + 1)
                dve.tensor_tensor(attn_tok[:, bass.ds(4 * g, GRP), h * 4 * D:(h + 1) * 4 * D].rearrange("p q (h d) -> p q h d", h=4),
                                  sums[:, :, :, 0:D],
                                  rden[:, :].rearrange("p (q h) -> p q h", h=4).unsqueeze(3).broadcast_to([P, GRP, 4, D]),
                                  ALU.mult).then_inc(z["out"], 1)

            for r in range(3):
                for u in range(UNITS if r < 2 else AHEAD // 2):
                    for j in range(2):
                        maxima(0, r, u, j)

            def step(g, h):
                last_step = before(g, h)
                for kt, _ in at.tiles:
                    for r, u, j in at.maxima_at(h, kt):
                        if exists(8 * g + r):
                            maxima(g, r, u, j)
                    if kt == 2 and last_step:
                        result(*last_step)

            steps(dve, step)
            result(NG - 1, 3)

        cross = Attention("cross", S_CTX)
        selfa = Attention("selfa", T)

        post = sems(*("post_" + n for n in ("at", "aT_ps", "aT", "o_ps", "ln", "root", "norm", "apply", "product", "key")))
        post_sum = band_tmp
        product = xin
        key = carve(p_arena, 1024, NT)

        def post_gpsimd(pool):
            pool.wait_ge(selfa.s["out"], 4 * NG + 1)

            def tick(t, r):
                if (i := tile_at(t, 0, NT)) is not None:
                    if some(i - 1):
                        pool.wait_ge(post["post_aT_ps"], i - 1)
                    pool.tensor_copy(at_in[:, r % 2, :], attn_tok[:, i, :]).then_inc(post["post_at"], 1)
                if (i := tile_at(t, 3, NT)) is not None:
                    pool.wait_ge(post["post_norm"], i + 1)
                    if some(i - 1):
                        pool.wait_ge(post["post_key"], i - 1)
                    pool.tensor_tensor(product[:, (r - 3) % 2, :], src_sb[:, i, :], row("ffn_router_w"), ALU.mult).then_inc(post["post_product"], 1)

            ticks(pool, NT, 3, tick, HEAD, 2)

        def post_tensor(pe):
            z = post

            def tick(t, r):
                if (i := tile_at(t, 1, NT)) is not None:
                    pe.wait_ge(z["post_aT"], i + 1)
                    if some(i - 1):
                        pe.wait_ge(z["post_ln"], 3 * (i - 1) - 2)
                    for k in range(KC):
                        last = pe.matmul(bank(1 + (r - 1) % 2)[:, 0:C], aT[:, (r - 1) % 2, k, :], w_fo[:, k, :], start=k == 0, stop=k == KC - 1)
                    last.then_inc(z["post_o_ps"], 1)
                if (i := tile_at(t, 0, NT)) is not None:
                    pe.wait_ge(z["post_at"], i + 1)
                    if some(i):
                        pe.wait_ge(z["post_aT"], i)
                    for k in range(KC):
                        last = pe.transpose(bank(0)[:, k * P:(k + 1) * P], at_in[:, r % 2, k * P:(k + 1) * P], ident[:, :])
                    last.then_inc(z["post_aT_ps"], 1)

            ticks(pe, NT, 2, tick, HEAD, 2)

        def post_scalar(act):
            z = post

            def tick(t, r):
                if (i := tile_at(t, 0, NT)) is not None:
                    act.wait_ge(z["post_aT_ps"], i + 1)
                    if some(i - 1):
                        act.wait_ge(z["post_o_ps"], i - 1)
                    act.activation(aT[:, r % 2, :, :], bank(0)[:, 0:C].rearrange("p (k t) -> p k t", k=KC),
                                   ACT.Copy).then_inc(z["post_aT"], 1)
                if (i := tile_at(t, 4, NT)) is not None:
                    act.wait_ge(z["post_product"], i + 1)
                    act.activation(product[:, (r - 4) % 2, :], product[:, (r - 4) % 2, :], ACT.Copy,
                                   accum_out=key[:, bass.ds(i, 1)]).then_inc(z["post_key"], 1)
                if (i := tile_at(t, 1, NT)) is not None:
                    q = (r - 1) % 2
                    act.wait_ge(z["post_ln"], 3 * i + 3)
                    act.activation(rstd[:, q:q + 1], mean_var[:, q, 1:2], ACT.Sqrt, bias=eps_col[:, :]).then_inc(z["post_root"], 1)

            ticks(act, NT, 4, tick, HEAD, 2)

        def post_vector(dve):
            z = post

            def tick(t, r):
                i, b = tile_at(t, 1, NT), tile_at(t, 2, NT)
                q, p = (r - 1) % 2, (r - 2) % 2
                if i is not None:
                    if some(i - 1):
                        dve.wait_ge(z["post_norm"], i - 1)
                    dve.wait_ge(z["post_o_ps"], i + 1)
                    dve.tensor_tensor(post_sum[:, q, :], bank(1 + q)[:, 0:C], src_sb[:, i, :], ALU.add).then_inc(z["post_ln"], 1)
                if b is not None:
                    dve.wait_ge(z["post_root"], b + 1)
                    dve.reciprocal(rstd[:, p:p + 1], rstd[:, p:p + 1]).then_inc(z["post_apply"], 1)
                    dve.scalar_tensor_tensor(post_sum[:, p, :], post_sum[:, p, :], mean_var[:, p, 0:1], row("ffn_ln1_g"),
                                             ALU.subtract, ALU.mult).then_inc(z["post_apply"], 1)
                if i is not None:
                    dve.wait_ge(z["post_ln"], 3 * i + 1)
                    dve.bn_stats(stat6[:, q, :], post_sum[:, q, :]).then_inc(z["post_ln"], 1)
                if b is not None:
                    if i is not None:
                        dve.wait_ge(z["post_ln"], 3 * i + 2)
                    dve.wait_ge(z["post_apply"], 2 * b + 2)
                    dve.scalar_tensor_tensor(src_sb[:, b, :], post_sum[:, p, :], rstd[:, p:p + 1], row("ffn_ln1_b"),
                                             ALU.mult, ALU.add).then_inc(z["post_norm"], 1)
                elif i is not None:
                    dve.wait_ge(z["post_ln"], 3 * i + 2)
                if i is not None:
                    dve.bn_aggr(mean_var[:, q, :], stat6[:, q, :]).then_inc(z["post_ln"], 1)

            ticks(dve, NT, 2, tick, HEAD, 2)

        moe = sems(*("moe_" + n for n in ("weights", "consts", "const_f", "route", "rank_ps", "count_ps", "token_ps",
                                          "rows_stored", "in0", "in1", "res0", "res1", "xT_ps", "xT", "w1", "w2", "b1", "h_ps", "relu",
                                          "y_ps", "kept", "apply", "stored0", "stored1", "ln", "root", "xb")))
        NS = NT + E - 1
        x_rows = nc.dram_tensor("x_rows", [T, C], fp32).ap()
        res_rows = nc.dram_tensor("res_rows", [T, C], fp32).ap()
        w1_sb = k_op[:, :, :].rearrange("p a b -> p (a b)").bitcast(fp32)
        w2_sb = v_aug[:, :, :, :].rearrange("p t h d -> p (t h d)")
        WIDE = KC * F
        w1_use = carve(q_arena, 0, KC, F)
        w2_use = carve(q_arena, WIDE, FC, C)
        hidden = carve(q_arena, 2 * WIDE, 2, FC, P)
        xs_in = carve(q_arena, 2 * WIDE + 2 * F, 2, C)
        xsT = carve(q_arena, 2 * WIDE + 2 * F + 2 * C, 2, KC, P)
        y_out = carve(q_arena, 2 * WIDE + 2 * F + 4 * C, 2, C)
        b2_rows = w_fqkv[:, :, :].rearrange("p k n -> p (k n)")[:, 0:E * C]
        x_kept = carve(q_arena, 2 * WIDE + 2 * F + 6 * C, 2, C)
        res_in = carve(p_arena, 3584, 2, C)
        before_token, ones = (band_mask[:, i * P // 2:(i + 1) * P // 2].bitcast(fp16) for i in range(2))
        cut = [1024 + NT]

        def small(*shape):
            n = 1
            for k in shape:
                n *= k
            cut[0] += n
            return carve(p_arena, cut[0] - n, *shape)

        floor_f, above = small(NT), small(NT)
        key_int = small(NT).bitcast(i32)
        chosen = small(E * NT // 2).bitcast(fp16).rearrange("p (e t) -> p e t", t=NT)
        place = small(E, NT)
        counts, full, first = small(E), small(E, NT), small(E)
        tiles_of, place_f = small(E), small(NT)
        after, slot_f = small(NS, E), small(NS)
        slot_expert = small(NS).bitcast(i32)
        dest, place_in, place_tile = (small(NT).bitcast(i32) for _ in range(3))
        place_in_f, place_tile_f = small(NT), small(NT)
        in_tile, of_token = small(NT, NS), small(NT * NS // 2).bitcast(fp16).rearrange("p (t s) -> p t s", s=NS)
        in_row = carve(p_arena, 2560, NT * P // 2).bitcast(fp16).rearrange("p (t r) -> p t r", r=P)
        empty, token_f, gather_f = small(NS), small(NS), small(NS)
        gather_row, scatter_row = small(NS).bitcast(i32), small(NS).bitcast(i32)
        spare = w_xkv[:, :, :].rearrange("p k n -> p (k n)")
        ids, ids_f, token_no, token_no_f = (spare[:, a:a + n] for a, n in ((0, P), (P, P), (2 * P, NT), (2 * P + NT, NT)))
        ids, token_no = ids.bitcast(i32), token_no.bitcast(i32)
        place_ps, count_ps, token_ps = bank(5)[:, 0:E * NT], bank(6)[:, 0:E * NT], bank(7)[:, 0:NS]

        def moe_sync(sp):
            z = moe

            def by_tile(rows):
                return rows.rearrange("(t p) c -> p t c", p=P)

            sp.wait_ge(z["moe_xb"], 1)
            sp.dma_start(by_tile(res_rows), x_sb[:, :, :]).then_inc(z["moe_rows_stored"], 16)
            sp.wait_ge(selfa.s["out"], 4 * NG + 1)
            sp.dma_start(w1_sb.rearrange("p (e k f) -> p e k f", e=E, k=KC),
                         io["L0_ffn_W1"].rearrange("e (k p) f -> p e k f", p=P)).then_inc(z["moe_weights"], 16)
            sp.dma_start(w2_sb.rearrange("p (e c n) -> p e c n", e=E, c=FC),
                         io["L0_ffn_W2"].rearrange("e (c p) n -> p e c n", p=P)).then_inc(z["moe_weights"], 16)
            sp.dma_start(b2_rows, io["L0_ffn_b2"].rearrange("e n -> (e n)").partition_broadcast(P)).then_inc(z["moe_weights"], 16)
            for g in range(NG):
                sp.wait_ge(post["post_norm"], GRP * (g + 1))
                sp.dma_start(by_tile(x_rows)[:, GRP * g:GRP * (g + 1), :], src_sb[:, GRP * g:GRP * (g + 1), :]).then_inc(z["moe_rows_stored"], 16)
            sp.wait_ge(z["moe_stored0"], 16 * (NS - NS // 2))
            sp.wait_ge(z["moe_stored1"], 16 * (NS // 2))

        def moe_constants(pool):
            z = moe
            pool.iota(ids, pattern=[[1, P]], base=0, channel_multiplier=0).then_inc(z["moe_consts"], 1)
            pool.iota(token_no, pattern=[[P, NT]], base=1, channel_multiplier=1).then_inc(z["moe_consts"], 1)
            pool.memset(before_token, 1.0).then_inc(z["moe_consts"], 1)
            pool.memset(ones, 1.0).then_inc(z["moe_consts"], 1)
            pool.wait_ge(z["moe_consts"], 4)
            pool.affine_select(out=before_token, in_=before_token, compare_op=ALU.is_ge, fill=0.0, base=-1,
                               pattern=[[1, P]], channel_multiplier=-1).then_inc(z["moe_consts"], 1)
            pool.wait_ge(self_qkv.s["ln"], 4 * NT)
            pool.tensor_tensor(x_sb[:, :, :], x_sb[:, :, :], row("ffn_ln2_b").unsqueeze(1).broadcast_to([P, NT, C]),
                               ALU.add).then_inc(moe["moe_xb"], 1)

        def moe_gpsimd(pool):
            z = moe
            pool.wait_ge(z["moe_rows_stored"], 16 * (1 + NG))
            pool.wait_ge(z["moe_route"], ROUTED)
            for t in range(NS + 4):
                if t < NS:
                    if t >= 2:
                        pool.wait_ge(z["moe_xT_ps"], t - 1)
                        pool.wait_ge(z["moe_kept"], t - 1)
                    pool.indirect_dma_start(out=xs_in[:, t % 2, :], out_offset=None, in_=x_rows,
                                            in_offset=bass.IndirectOffsetOnAxis(ap=gather_row[:, t:t + 1], axis=0)
                                            ).then_inc(z[f"moe_in{t % 2}"], 16)
                if 0 <= (i := t - 3) < NS:
                    if i >= 2:
                        pool.wait_ge(z["moe_apply"], 3 * (i - 1))
                    pool.indirect_dma_start(out=res_in[:, i % 2, :], out_offset=None, in_=res_rows,
                                            in_offset=bass.IndirectOffsetOnAxis(ap=gather_row[:, i:i + 1], axis=0)
                                            ).then_inc(z[f"moe_res{i % 2}"], 16)
                if 0 <= (i := t - 4) < NS:
                    pool.wait_ge(z["moe_apply"], 3 * i + 3)
                    pool.indirect_dma_start(out=out[0], in_=y_out[:, i % 2, :], in_offset=None,
                                            out_offset=bass.IndirectOffsetOnAxis(ap=scatter_row[:, i:i + 1], axis=0),
                                            bounds_check=T - 1, oob_is_err=False).then_inc(z[f"moe_stored{i % 2}"], 16)

        def moe_tensor(pe):
            z = moe
            pe.wait_ge(z["moe_consts"], 5)
            pe.wait_ge(z["moe_route"], CHOSEN)
            pe.matmul(count_ps, ones, chosen.rearrange("p e t -> p (e t)"), start=True, stop=True).then_inc(z["moe_count_ps"], 1)
            places = place_ps.rearrange("p (e t) -> p e t", t=NT)
            pe.matmul(places, before_token, chosen, start=True, stop=False)
            for d in range(1, NT):
                last = pe.matmul(places[:, :, d:NT], ones, chosen[:, :, 0:NT - d], start=False, stop=d == NT - 1)
            last.then_inc(z["moe_rank_ps"], 1)
            pe.wait_ge(z["moe_route"], ONE_HOT)
            for t in range(NT):
                last = pe.matmul(token_ps, in_row[:, t, :], of_token[:, t, :], start=t == 0, stop=t == NT - 1)
            last.then_inc(z["moe_token_ps"], 1)
            pe.wait_ge(z["moe_route"], ROUTED)

            def tick(t, r):
                if (i := tile_at(t, 2, NS)) is not None:
                    q = (r - 2) % 2
                    pe.wait_ge(z["moe_xT"], i + 1)
                    pe.wait_ge(z["moe_w1"], i + 1)
                    if some(i - 1):
                        pe.wait_ge(z["moe_relu"], FC * (i - 1))
                    for c in range(FC):
                        for k in range(KC):
                            last = pe.matmul(bank(2 * q + c // 4)[:, (c % 4) * P:(c % 4 + 1) * P], w1_use[:, k, c * P:(c + 1) * P],
                                             xsT[:, q, k, :], start=k == 0, stop=k == KC - 1)
                        last.then_inc(z["moe_h_ps"], 1)
                if (i := tile_at(t, 1, NS)) is not None:
                    q = (r - 1) % 2
                    pe.wait_ge(z[f"moe_in{q}"], 16 * half(i, r - 1) + 16)
                    if some(i - 1):
                        pe.wait_ge(z["moe_xT"], i - 1)
                    for k in range(KC):
                        last = pe.transpose(bank(4 + 3 * q)[:, k * P:(k + 1) * P], xs_in[:, q, k * P:(k + 1) * P], ident[:, :])
                    last.then_inc(z["moe_xT_ps"], 1)
                if (i := tile_at(t, 3, NS)) is not None:
                    q = (r - 3) % 2
                    pe.wait_ge(z["moe_relu"], FC * (i + 1))
                    pe.wait_ge(z["moe_w2"], i + 1)
                    if some(i - 1):
                        pe.wait_ge(z["moe_ln"], 3 * (i - 1) - 2)
                    for c in range(FC):
                        last = pe.matmul(bank(5 + q)[:, 0:C], hidden[:, q, c, :], w2_use[:, c, :], start=c == 0, stop=c == FC - 1)
                    last.then_inc(z["moe_y_ps"], 1)

            ticks(pe, NS, 3, tick, HEAD, 2)

        def moe_scalar(act):
            z = moe
            act.wait_ge(z["moe_weights"], 16 * 3)
            act.wait_ge(s["ld_small"], 16 * 2)
            act.wait_ge(z["moe_route"], ROUTED)

            def tick(t, r):
                if (i := tile_at(t, 1, NS)) is not None:
                    e = act.value_load(slot_expert[0:1, bass.ds(i, 1)], min_val=0, max_val=E - 1)
                if (i := tile_at(t, 2, NS)) is not None:
                    q = (r - 2) % 2
                    act.wait_ge(z["moe_b1"], i + 1)
                    for c in range(FC):
                        if c % 4 == 0:
                            act.wait_ge(z["moe_h_ps"], FC * i + c + 4)
                        act.activation(hidden[:, q, c, :], bank(2 * q + c // 4)[:, (c % 4) * P:(c % 4 + 1) * P], ACT.Relu,
                                       bias=b1_use[:, c:c + 1]).then_inc(z["moe_relu"], 1)
                if (i := tile_at(t, 1, NS)) is not None:
                    act.activation(w1_use.rearrange("p k f -> p (k f)"), w1_sb[:, bass.ds(e * WIDE, WIDE)], ACT.Copy).then_inc(z["moe_w1"], 1)
                    if some(i):
                        act.wait_ge(z["moe_relu"], FC * i)
                    act.activation(b1_use[:, :], b1_col[:, :, :].rearrange("p e c -> p (e c)")[:, bass.ds(e * FC, FC)],
                                   ACT.Copy).then_inc(z["moe_b1"], 1)

                if (i := tile_at(t, 3, NS)) is not None:
                    q = (r - 3) % 2
                    act.wait_ge(z["moe_ln"], 3 * i + 3)
                    act.activation(rstd[:, q:q + 1], mean_var[:, q, 1:2], ACT.Sqrt, bias=eps_col[:, :]).then_inc(z["moe_root"], 1)

            ticks(act, NS, 3, tick, HEAD, 2)

        ROUTED, CHOSEN, ONE_HOT = 35, 9, 26

        def moe_vector(dve):
            z = moe
            dve.wait_ge(z["moe_consts"], 2)
            dve.tensor_copy(ids_f, ids).then_inc(z["moe_const_f"], 1)
            dve.tensor_copy(token_no_f, token_no).then_inc(z["moe_const_f"], 1)
            dve.memset(first[:, 0:1], 0.0).then_inc(z["moe_const_f"], 1)
            dve.wait_ge(z["moe_const_f"], 3)
            dve.wait_ge(post["post_key"], NT)
            by_expert = "p (e t) -> p e t"
            spread = lambda v, n: v.unsqueeze(2).broadcast_to([P, v.shape[1], n])
            along = lambda v, n: v.unsqueeze(1).broadcast_to([P, n, v.shape[1]])
            dve.tensor_scalar(key, key, router_bias[:, :], None, ALU.add).then_inc(z["moe_route"], 1)
            dve.wait_ge(z["moe_route"], 1)
            dve.tensor_copy(key_int, key).then_inc(z["moe_route"], 1)
            dve.wait_ge(z["moe_route"], 2)
            dve.tensor_copy(floor_f, key_int).then_inc(z["moe_route"], 1)
            dve.wait_ge(z["moe_route"], 3)
            dve.tensor_tensor(above, floor_f, key, ALU.is_gt).then_inc(z["moe_route"], 1)
            dve.wait_ge(z["moe_route"], 4)
            dve.tensor_tensor(floor_f, floor_f, above, ALU.subtract).then_inc(z["moe_route"], 1)
            dve.wait_ge(z["moe_route"], 5)
            dve.tensor_copy(key_int, floor_f).then_inc(z["moe_route"], 1)
            dve.wait_ge(z["moe_route"], 6)
            dve.tensor_scalar(key_int, key_int, E - 1, None, ALU.bitwise_and).then_inc(z["moe_route"], 1)
            dve.wait_ge(z["moe_route"], 7)
            dve.tensor_copy(key, key_int).then_inc(z["moe_route"], 1)
            dve.wait_ge(z["moe_route"], 8)
            dve.tensor_tensor(chosen, along(key, E), spread(ids_f[:, 0:E], NT), ALU.is_equal).then_inc(z["moe_route"], 1)
            dve.wait_ge(z["moe_count_ps"], 1)
            dve.tensor_reduce(counts, count_ps.rearrange(by_expert, t=NT), AX.X, ALU.add).then_inc(z["moe_route"], 1)
            dve.wait_ge(z["moe_route"], 10)
            dve.scalar_tensor_tensor(full, along(ids_f[:, 0:NT], E), float(P), spread(counts, NT), ALU.mult, ALU.is_lt).then_inc(z["moe_route"], 1)
            dve.wait_ge(z["moe_route"], 11)
            dve.tensor_reduce(tiles_of, full, AX.X, ALU.add).then_inc(z["moe_route"], 1)
            for e in range(1, E):
                dve.wait_ge(z["moe_route"], 11 + e)
                dve.tensor_tensor(first[:, e:e + 1], first[:, e - 1:e], tiles_of[:, e - 1:e], ALU.add).then_inc(z["moe_route"], 1)
            dve.wait_ge(z["moe_route"], 11 + E)
            dve.wait_ge(z["moe_rank_ps"], 1)
            dve.scalar_tensor_tensor(place, spread(first, NT), float(P), place_ps.rearrange(by_expert, t=NT),
                                     ALU.mult, ALU.add).then_inc(z["moe_route"], 1)
            dve.wait_ge(z["moe_route"], 12 + E)
            dve.tensor_tensor(place, place, chosen, ALU.mult).then_inc(z["moe_route"], 1)
            dve.wait_ge(z["moe_route"], 13 + E)
            dve.tensor_reduce(place_f, place.rearrange("p e t -> p t e"), AX.X, ALU.add).then_inc(z["moe_route"], 1)
            dve.wait_ge(z["moe_route"], 14 + E)
            dve.tensor_copy(dest, place_f).then_inc(z["moe_route"], 1)
            dve.wait_ge(z["moe_route"], 15 + E)
            dve.tensor_scalar(place_in, dest, P - 1, None, ALU.bitwise_and).then_inc(z["moe_route"], 1)
            dve.tensor_scalar(place_tile, dest, P.bit_length() - 1, None, ALU.logical_shift_right).then_inc(z["moe_route"], 1)
            dve.wait_ge(z["moe_route"], 16 + E)
            dve.tensor_copy(place_in_f, place_in).then_inc(z["moe_route"], 1)
            dve.wait_ge(z["moe_route"], 17 + E)
            dve.tensor_copy(place_tile_f, place_tile).then_inc(z["moe_route"], 1)
            dve.wait_ge(z["moe_route"], 18 + E)
            dve.tensor_tensor(in_row, along(ids_f, NT), spread(place_in_f, P), ALU.is_equal).then_inc(z["moe_route"], 1)
            dve.wait_ge(z["moe_route"], 19 + E)
            dve.tensor_tensor(in_tile, along(ids_f[:, 0:NS], NT), spread(place_tile_f, NS), ALU.is_equal).then_inc(z["moe_route"], 1)
            dve.wait_ge(z["moe_route"], 21 + E)
            dve.tensor_tensor(of_token, in_tile, spread(token_no_f, NS), ALU.mult).then_inc(z["moe_route"], 1)
            dve.tensor_tensor(after, spread(ids_f[:, 0:NS], E), along(first, NS), ALU.is_ge).then_inc(z["moe_route"], 1)
            dve.wait_ge(z["moe_route"], 23 + E)
            dve.tensor_reduce(slot_f, after[:, :, 1:E], AX.X, ALU.add).then_inc(z["moe_route"], 1)
            dve.wait_ge(z["moe_route"], 24 + E)
            dve.tensor_copy(slot_expert, slot_f).then_inc(z["moe_route"], 1)
            dve.wait_ge(z["moe_token_ps"], 1)
            dve.tensor_scalar(empty, token_ps, 0.0, float(T + 1), ALU.is_equal, ALU.mult).then_inc(z["moe_route"], 1)
            dve.wait_ge(z["moe_route"], 26 + E)
            dve.tensor_tensor(token_f, token_ps, empty, ALU.add).then_inc(z["moe_route"], 1)
            dve.wait_ge(z["moe_route"], 27 + E)
            dve.tensor_scalar(gather_f, token_f, -1.0, float(T - 1), ALU.add, ALU.min).then_inc(z["moe_route"], 1)
            dve.tensor_scalar(token_f, token_f, -1.0, None, ALU.add).then_inc(z["moe_route"], 1)
            dve.wait_ge(z["moe_route"], 28 + E)
            dve.tensor_copy(gather_row, gather_f).then_inc(z["moe_route"], 1)
            dve.wait_ge(z["moe_route"], 29 + E)
            dve.tensor_copy(scatter_row, token_f).then_inc(z["moe_route"], 1)
            dve.wait_ge(z["moe_weights"], 16 * 3)
            dve.wait_ge(z["moe_route"], ROUTED)

            def tick(t, r):
                expert_of = {}
                for stage in (1, 2):
                    if (i := tile_at(t, stage, NS)) is not None:
                        expert_of[stage] = dve.value_load(slot_expert[0:1, bass.ds(i, 1)], min_val=0, max_val=E - 1)
                if (i := tile_at(t, 1, NS)) is not None:
                    dve.wait_ge(z["moe_xT_ps"], i + 1)
                    dve.tensor_copy(xsT[:, (r - 1) % 2, :, :], bank(4 + 3 * ((r - 1) % 2))[:, 0:C].rearrange("p (k t) -> p k t", k=KC)).then_inc(z["moe_xT"], 1)
                if (i := tile_at(t, 4, NS)) is not None:
                    q = r % 2
                    dve.wait_ge(z["moe_root"], i + 1)
                    dve.reciprocal(rstd[:, q:q + 1], rstd[:, q:q + 1]).then_inc(z["moe_apply"], 1)
                    dve.scalar_tensor_tensor(y_out[:, q, :], y_out[:, q, :], mean_var[:, q, 0:1], row("ffn_ln2_g"),
                                             ALU.subtract, ALU.mult).then_inc(z["moe_apply"], 1)
                    dve.wait_ge(z["moe_apply"], 3 * i + 2)
                    dve.wait_ge(z[f"moe_res{q}"], 16 * half(i, r) + 16)
                    dve.scalar_tensor_tensor(y_out[:, q, :], y_out[:, q, :], rstd[:, q:q + 1], res_in[:, q, :],
                                             ALU.mult, ALU.add).then_inc(z["moe_apply"], 1)
                if (i := tile_at(t, 3, NS)) is not None:
                    q = (r - 3) % 2
                    dve.wait_ge(z["moe_y_ps"], i + 1)
                    dve.wait_ge(z["moe_kept"], i + 1)
                    if some(i - 1):
                        dve.wait_ge(z[f"moe_stored{q}"], 16 * half(i - 2, r - 3) + 16)
                    dve.tensor_tensor(y_out[:, q, :], bank(5 + q)[:, 0:C], x_kept[:, q, :], ALU.add).then_inc(z["moe_ln"], 1)
                    dve.wait_ge(z["moe_ln"], 3 * i + 1)
                    dve.bn_stats(stat6[:, q, :], y_out[:, q, :]).then_inc(z["moe_ln"], 1)
                    dve.wait_ge(z["moe_ln"], 3 * i + 2)
                if (b := tile_at(t, 1, NS)) is not None:
                    dve.tensor_tensor(x_kept[:, (r - 1) % 2, :], xs_in[:, (r - 1) % 2, :], b2_rows[:, bass.ds(expert_of[1] * C, C)],
                                      ALU.add).then_inc(z["moe_kept"], 1)
                if i is not None:
                    dve.bn_aggr(mean_var[:, q, :], stat6[:, q, :]).then_inc(z["moe_ln"], 1)
                if (i := tile_at(t, 2, NS)) is not None:
                    dve.tensor_copy(w2_use.rearrange("p c n -> p (c n)"), w2_sb[:, bass.ds(expert_of[2] * WIDE, WIDE)]).then_inc(z["moe_w2"], 1)

            ticks(dve, NS, 4, tick, HEAD, 2)

        @block.sync
        def _(sp):
            sp.dma_start(x_sb[:, 0:GRP, :], x_view[:, 0:GRP, :]).then_inc(s["ld_x0"], 16)
            sp.dma_start(w_band[:, :, :], io["L0_attn_W_qkv"].rearrange("(k p) n -> p k n", p=P)).then_inc(s["ld_band"], 16)
            sp.dma_start(bqk_col[:, :], io["L0_attn_b_qkv"][0:2 * C].rearrange("(f p) -> p f", p=P),
                         allow_slow_non_contiguous=True).then_inc(s["ld_band"], 16)
            sp.dma_start(band_rows[:, 0, :], io["L0_attn_b_qkv"][2 * C:3 * C].partition_broadcast(P)).then_inc(s["ld_band"], 16)
            sp.dma_start(band_rows[:, 1, :], io["L0_attn_ln_w"].partition_broadcast(P)).then_inc(s["ld_band"], 16)
            sp.dma_start(band_rows[:, 2, :], io["L0_attn_ln_b"].partition_broadcast(P)).then_inc(s["ld_band"], 16)
            sp.dma_start(x_sb[:, GRP:NT, :], x_view[:, GRP:NT, :]).then_inc(s["ld_x"], 16)
            for w, n in enumerate(("Wq", "Wk", "Wv", "Wo")):
                sp.dma_start(w_xraw[:, w, :, :], io["L0_xattn_" + n].rearrange("(o p) i -> p o i", p=P)).then_inc(s["ld_xw"], 16)
            for n in ROWS:
                v = io["L0_" + n]
                v = v.rearrange("c o -> (c o)") if len(v.shape) == 2 else v
                sp.dma_start(row(n), v.partition_broadcast(P)).then_inc(s["ld_rows"], 16)
            sp.dma_start(b1_col[:, :, :], io["L0_ffn_b1"].rearrange("e (c p) -> p e c", p=P),
                         allow_slow_non_contiguous=True).then_inc(s["ld_small"], 16)
            sp.dma_start(router_bias[:, :], io["L0_ffn_router_b"].partition_broadcast(P)).then_inc(s["ld_small"], 16)
            for w, n in enumerate(("Wq", "Wk", "Wv")):
                sp.dma_start(w_fqkv[:, :, w * C:(w + 1) * C], io["L0_ffn_" + n].rearrange("(k p) n -> p k n", p=P)).then_inc(s["ld_fw"], 16)
            sp.dma_start(w_fo[:, :, :], io["L0_ffn_Wo"].rearrange("(k p) n -> p k n", p=P)).then_inc(s["ld_fw"], 16)
            sp.wait_ge(s["band_xT_ps"], NT)
            stage_sync(sp, ctx_kv)
            moe_sync(sp)

        @block.gpsimd
        def _(pool):
            pool.memset(eps_col[:, :], EPS).then_inc(s["const"], 1)
            pool.memset(ident[:, :], 0.0).then_inc(s["const_zero"], 1)
            pool.memset(ident16[:, :], 0.0).then_inc(s["const_zero"], 1)
            pool.memset(band_mask[:, :], BAND_SCALE).then_inc(s["const_zero"], 1)
            pool.wait_ge(s["const_zero"], 3)
            for m in (ident, ident16):
                pool.affine_select(out=m[:, :], in_=m[:, :], compare_op=ALU.not_equal, fill=1.0, base=0,
                                   pattern=[[-1, P]], channel_multiplier=1).then_inc(s["const"], 1)
            pool.affine_select(out=band_mask[:, :], in_=band_mask[:, :], compare_op=ALU.is_ge, fill=0.0, base=0,
                               pattern=[[1, 2 * P]], channel_multiplier=-1).then_inc(s["const_zero"], 1)
            pool.wait_ge(s["const_zero"], 4)
            pool.affine_select(out=band_mask[:, :], in_=band_mask[:, :], compare_op=ALU.is_ge, fill=0.0, base=SPAN - 1,
                               pattern=[[-1, 2 * P]], channel_multiplier=1).then_inc(s["const"], 1)
            pool.memset(v_aug[:, :, :, D:2 * D], 0.0).then_inc(s["v_const"], 1)
            pool.wait_ge(s["v_const"], 1)
            pool.memset(v_aug[:, :, :, D:D + 1], 1.0).then_inc(s["v_const"], 1)
            for q in range(2):
                pool.memset(k_tok[:, q, :, MROW:SLOT], 0.0).then_inc(s["k_const"], 1)
            pool.wait_ge(s["k_const"], 2)
            for q in range(2):
                pool.memset(k_tok[:, q, :, MROW:MROW + 1], 1.0).then_inc(s["k_const"], 1)
            band_gpsimd(pool)
            pool.wait_ge(s["xw_ps"], 4)
            pool.wait_ge(s["band_out"], 5 * NT)
            pool.memset(q_tok[:, :, :, MROW:SLOT], 0.0).then_inc(s["q_const"], 1)
            pool.wait_ge(cross_q.s["proj"], NT)
            for j in range(2):
                pool.wait_ge(s["q_const"], j + 1)
                pool.memset(q_max[j][SLOT * (1 - j):SLOT * (2 - j), :, :], 0.0).then_inc(s["q_const"], 1)
            pool.wait_ge(s["q_const"], 3)
            pool.wait_ge(cross.s["out"], 4 * NG + 1)
            pool.memset(q_tok[:, :, :, MROW:MROW + 1], 0.0).then_inc(s["q_const"], 1)
            for q in range(2):
                pool.memset(k_tok[:, q, :, MROW:SLOT], 0.0).then_inc(s["k_const"], 1)
            pool.wait_ge(s["k_const"], 6)
            for q in range(2):
                pool.memset(k_tok[:, q, :, MROW:MROW + 1], 1.0).then_inc(s["k_const"], 1)
            stage_gpsimd(pool, self_qkv)
            moe_constants(pool)
            post_gpsimd(pool)
            moe_gpsimd(pool)

        @block.tensor
        def _(pe):
            band_tensor(pe)
            weights_tensor(pe)
            pe.wait_ge(s["band_st"], NT)
            pe.wait_ge(s["band_out"], 5 * NT)
            pe.wait_ge(s["xw"], 4)
            pe.wait_ge(s["k_const"], 4)
            run_beside(pe, stage_tensor, ctx_kv, cross_q)
            pe.wait_ge(cross_q.s["split"], NT)
            pe.wait_ge(cross_q.s["copy"], NT)
            pe.wait_ge(s["q_const"], 3)
            pe.wait_ge(s["v_const"], 2)
            pe.wait_ge(ctx_kv.s["kop"], NCT)
            attention_tensor(pe, cross)
            pe.wait_ge(cross.s["out"], 4 * NG + 1)
            pe.wait_ge(s["k_const"], 8)
            pe.wait_ge(s["ld_fw"], 16 * 4)
            run_stage(pe, stage_tensor, self_qkv)
            pe.wait_ge(self_qkv.s["split"], NT)
            pe.wait_ge(self_qkv.s["copy"], NT)
            pe.wait_ge(self_qkv.s["kop"], NT)
            pe.wait_ge(s["q_const"], 4)
            attention_tensor(pe, selfa)
            pe.wait_ge(selfa.s["out"], 4 * NG + 1)
            post_tensor(pe)
            moe_tensor(pe)

        @block.scalar
        def _(act):
            band_scalar(act)
            weights_scalar(act)
            run_beside(act, stage_scalar, ctx_kv, cross_q)
            attention_scalar(act, cross)
            run_stage(act, stage_scalar, self_qkv)
            act.wait_ge(self_qkv.s["kept"], NT)
            attention_scalar(act, selfa)
            post_scalar(act)
            moe_scalar(act)

        @block.vector
        def _(dve):
            band_vector(dve)
            dve.wait_ge(s["ld_rows"], 16 * len(ROWS))
            dve.wait_ge(s["xw_ps"], 4)
            run_beside(dve, stage_vector, ctx_kv, cross_q)
            attention_vector(dve, cross)
            run_stage(dve, stage_vector, self_qkv)
            attention_vector(dve, selfa)
            post_vector(dve)
            moe_vector(dve)


_NAMES = ["x", "ctx_1024"] + ["L0_attn_" + n for n in ("W_qkv", "b_qkv", "ln_w", "ln_b")] + \
    ["L0_xattn_" + n for n in ("Wq", "bq", "Wk", "bk", "Wv", "bv", "Wo", "bo")] + \
    ["L0_ffn_" + n for n in ("Wq", "bq", "Wk", "bk", "Wv", "bv", "Wo", "bo", "router_w", "router_b",
                             "W1", "b1", "W2", "b2", "ln1_g", "ln1_b", "ln2_g", "ln2_b")]


def kernel(**inputs):
    import numpy as _np
    import concourse.bacc as _bacc
    from concourse import mybir as _mybir
    from concourse.bass_utils import run_bass_kernel_spmd as _run

    nc = _bacc.Bacc("TRN2", target_bir_lowering=False, num_devices=1)
    arrays, io = {}, {}
    for name in _NAMES:
        a = _np.ascontiguousarray(inputs[name])
        arrays[f"in_{name}"] = a
        io[name] = nc.dram_tensor(f"in_{name}", a.shape, _mybir.dt.from_np(a.dtype), kind="ExternalInput").ap()
    x = arrays["in_x"]
    out = nc.dram_tensor("out_x", x.shape, _mybir.dt.from_np(x.dtype), kind="ExternalOutput").ap()
    decoder_layer_kernel(nc, io, out)
    r = _run(nc, [arrays], core_ids=[0])
    return r.results[0]["out_x"]
```
